# Optimizing a Trainium2 kernel written in Bass

```python
import numpy as np
import jax
import jax.numpy as jnp

def _softmax(x, axis=-1):
    return jax.nn.softmax(x, axis=axis)

def _gelu(x):
    return jax.nn.gelu(x, approximate=True)

def _silu(x):
    return jax.nn.silu(x)

def _sigmoid(x):
    return jax.nn.sigmoid(x)

def _layernorm(x, axis=-1, eps=1e-05):
    m = jnp.mean(x, axis=axis, keepdims=True)
    v = jnp.var(x, axis=axis, keepdims=True)
    return (x - m) / jnp.sqrt(v + eps)

def _scatter_add(tgt, idx, src, axis=0):
    return tgt.at[idx].add(src)

def _segment_sum(src, seg, n):
    return jax.ops.segment_sum(src, seg, n)
kernel_name = 'mk_decoder_postln_d1_seqx_r4_016575'

def setup_inputs(seed: int=0):
    np.random.seed(seed)
    _w = jnp.asarray

    def _rec_inputs():
        import jax
        import jax.numpy as jnp
        _rk = jax.random.key(seed)
        x = -0.0002928 + 1 * jax.random.normal(jax.random.fold_in(_rk, 1), (8, 256, 256), jnp.float32)
        _lenS = 256 - jax.random.randint(jax.random.fold_in(_rk, 7), (8,), 0, max(1, 256 // 4) + 1, jnp.int32)
        _lenS2 = 256 - jax.random.randint(jax.random.fold_in(_rk, 8), (8,), 0, max(1, 256 // 4) + 1, jnp.int32)
        _ctx_1024P = jax.random.normal(jax.random.fold_in(_rk, 11), (8, 16, 256), jnp.float32)
        _ctx_1024c = jax.random.dirichlet(jax.random.fold_in(_rk, 511), 0.3 * jnp.ones((16,), jnp.float32), (8, 256))
        _ctx_1024t = jnp.einsum('bsk,bkd->bsd', _ctx_1024c, _ctx_1024P)
        _ctx_1024t = _ctx_1024t * jax.lax.rsqrt(jnp.mean(jnp.square(_ctx_1024t)) + 1e-12) * 0.953939
        ctx_1024 = -1.39393e-06 + 0.999914 * (_ctx_1024t + 0.3 * jax.random.normal(jax.random.fold_in(_rk, 611), (8, 256, 256), jnp.float32))
        return (x, ctx_1024)
    x, ctx_1024 = _rec_inputs()

    def _L0_attn_setup():
        import jax, jax.numpy as jnp
        import numpy as np
        B, L, D, H = (2, 512, 256, 4)
        DV = D // H
        P = 5
        CHUNK = 32
        CONV_K = 4
        FIR_K = (3, 15, 64)

        def _dwconv(x, w):
            K = w.shape[1]
            xt = jnp.pad(jnp.transpose(x, (0, 2, 1)), ((0, 0), (0, 0), (K - 1, 0)))
            y = jax.lax.conv_general_dilated(xt, w[:, None, :], (1,), 'VALID', dimension_numbers=('NCH', 'OIH', 'NCH'), feature_group_count=w.shape[0])
            return jnp.transpose(y, (0, 2, 1))

        def _l2norm(x):
            return x * jax.lax.rsqrt(jnp.sum(x * x, -1, keepdims=True) + 1e-06)

        def _delta_rule_chunkwise(q, k, v, beta, chunk=CHUNK):
            b, h, Lp, dk = q.shape
            dv = v.shape[-1]
            n = Lp // chunk
            q = _l2norm(q)
            k = _l2norm(k)
            v = v * beta[..., None]
            kb = k * beta[..., None]
            r = lambda t: t.reshape(b, h, n, chunk, -1)
            q, k, v, kb = (r(q), r(k), r(v), r(kb))
            sw = lambda t: jnp.swapaxes(t, -1, -2)
            strict = jnp.tril(jnp.ones((chunk, chunk), bool), -1)
            attn = jnp.where(strict, -(kb @ sw(k)), 0.0)
            T = jnp.linalg.inv(jnp.eye(chunk, dtype=q.dtype) - attn)
            u = T @ v
            w = T @ kb
            incl = jnp.tril(jnp.ones((chunk, chunk), bool), 0)
            qs, ks, us, ws = (jnp.moveaxis(t, 2, 0) for t in (q, k, u, w))
            S0 = jnp.zeros((b, h, dk, dv), q.dtype)

            def step(S, inp):
                q_i, k_i, u0, w_i = inp
                local = jnp.where(incl, q_i @ sw(k_i), 0.0)
                u_i = u0 - w_i @ S
                o_i = q_i @ S + local @ u_i
                return (S + sw(k_i) @ u_i, o_i)
            S, o = jax.lax.scan(step, S0, (qs, ks, us, ws))
            return (jnp.moveaxis(o, 0, 2).reshape(b, h, Lp, dv), S)

        def _stats(t):
            m = jnp.mean(t, -1, keepdims=True)
            v = jnp.mean(t * t, -1, keepdims=True)
            a = jnp.mean(jnp.abs(t), -1, keepdims=True)
            nrm = jnp.sqrt(jnp.sum(t * t, -1, keepdims=True))
            s = jnp.concatenate([jnp.broadcast_to(x, t.shape) for x in (m, v, a, nrm)], -1)
            return s.reshape(t.shape[0], t.shape[1], -1)

        def _forward(hs, Wq, Wk, Wv, conv_q, conv_k, conv_v, Wb, fir_s, fir_m, fir_l, gW1, gb1, gW2, gb2, log_tau, eps_logit, norm_w, Wo):
            b, Ln, _ = hs.shape
            q = jax.nn.silu(_dwconv(hs @ Wq, conv_q))
            k = jax.nn.silu(_dwconv(hs @ Wk, conv_k))
            v = jax.nn.silu(_dwconv(hs @ Wv, conv_v))
            beta = jax.nn.sigmoid(hs @ Wb)
            bh = lambda t: jnp.transpose(t.reshape(b, Ln, H, -1), (0, 2, 1, 3))
            o_d, _ = _delta_rule_chunkwise(bh(q), bh(k), bh(v), jnp.transpose(beta, (0, 2, 1)))
            delta_path = jnp.transpose(o_d, (0, 2, 1, 3))
            paths = jnp.stack([_dwconv(v, fir_s).reshape(b, Ln, H, DV), _dwconv(v, fir_m).reshape(b, Ln, H, DV), _dwconv(v, fir_l).reshape(b, Ln, H, DV), delta_path, v.reshape(b, Ln, H, DV)], axis=3)
            stats_flat = jnp.concatenate([_stats(paths[..., p, :]) for p in range(P)], -1)
            gate_in = jnp.concatenate([hs, stats_flat], -1)
            logits = jax.nn.gelu(gate_in @ gW1 + gb1, approximate=False) @ gW2 + gb2
            logits = logits.reshape(b, Ln, H, P)
            tau = jax.nn.softplus(log_tau) + 0.5
            probs = jax.nn.softmax(logits / tau[:, None], -1)
            eps = jax.nn.sigmoid(eps_logit) * 0.2
            probs = probs * (1.0 - jnp.sum(eps, -1, keepdims=True)) + eps
            o = jnp.einsum('blhp,blhpd->blhd', probs, paths)
            o = o * jax.lax.rsqrt(jnp.mean(o * o, -1, keepdims=True) + 1e-05) * norm_w
            return o.reshape(b, Ln, D) @ Wo
        key = jax.random.key(seed)
        ks = jax.random.split(key, 14)
        lin = lambda kk, fan_in, shape: jax.random.normal(kk, shape, jnp.float32) / np.float32(np.sqrt(fan_in))

        def fir(kk, K):
            w = np.zeros((D, K), np.float32)
            w[:, -1] = 1.0
            return jnp.asarray(w) + 0.001 * jax.random.normal(kk, (D, K), jnp.float32)
        in_gate = D + 4 * DV * H * P
        HF = 2 * D
        gb2 = np.zeros((H * P,), np.float32)
        gb2[np.arange(H) * P + P - 1] = 1.0
        return {'hidden_states': jax.random.normal(ks[0], (B, L, D), jnp.float32), 'Wq': lin(ks[1], D, (D, D)), 'Wk': lin(ks[2], D, (D, D)), 'Wv': lin(ks[3], D, (D, D)), 'conv_q': lin(ks[4], CONV_K, (D, CONV_K)), 'conv_k': lin(ks[5], CONV_K, (D, CONV_K)), 'conv_v': lin(ks[6], CONV_K, (D, CONV_K)), 'Wb': lin(ks[7], D, (D, H)), 'fir_s': fir(ks[8], FIR_K[0]), 'fir_m': fir(ks[9], FIR_K[1]), 'fir_l': fir(ks[10], FIR_K[2]), 'gW1': lin(ks[11], in_gate, (in_gate, HF)), 'gb1': jnp.zeros((HF,), jnp.float32), 'gW2': lin(ks[12], HF, (HF, H * P)), 'gb2': jnp.asarray(gb2), 'log_tau': jnp.zeros((H,), jnp.float32), 'eps_logit': jnp.zeros((H, P), jnp.float32), 'norm_w': jnp.ones((DV,), jnp.float32), 'Wo': lin(ks[13], D, (D, D))}
    _L0_attn_all = _L0_attn_setup()
    _L0_attn_in = {k: v for k, v in _L0_attn_all.items() if k in ('Wq', 'Wk', 'Wv', 'conv_q', 'conv_k', 'conv_v', 'Wb', 'fir_s', 'fir_m', 'fir_l', 'gW1', 'gb1', 'gW2', 'gb2', 'log_tau', 'eps_logit', 'norm_w', 'Wo')}
    del _L0_attn_all

    def _L0_xattn_setup():
        import jax, jax.numpy as jnp
        import numpy as np
        EMBED_DIM = 256
        NUM_HEADS = 16
        HEAD_DIM = EMBED_DIM // NUM_HEADS
        SCALE = HEAD_DIM ** (-0.5)

        def _split_heads(x, B):
            return x.reshape(B, -1, NUM_HEADS, HEAD_DIM).transpose(0, 2, 1, 3)
        key = jax.random.key(seed)
        ks = jax.random.split(key, 11)
        B, S, D = (2, 512, EMBED_DIM)
        std = D ** (-0.5)
        return {'query': jax.random.normal(ks[0], (B, S, D), jnp.float32), 'key': jax.random.normal(ks[1], (B, S, D), jnp.float32), 'value': jax.random.normal(ks[2], (B, S, D), jnp.float32), 'q_w': jax.random.normal(ks[3], (D, D), jnp.float32) * std, 'q_b': jnp.zeros((D,), jnp.float32), 'k_w': jax.random.normal(ks[4], (D, D), jnp.float32) * std, 'k_b': jnp.zeros((D,), jnp.float32), 'v_w': jax.random.normal(ks[5], (D, D), jnp.float32) * std, 'v_b': jnp.zeros((D,), jnp.float32), 'o_w': jax.random.normal(ks[6], (D, D), jnp.float32) * std, 'o_b': jnp.zeros((D,), jnp.float32)}
    _L0_xattn_all = _L0_xattn_setup()
    _L0_xattn_in = {k: v for k, v in _L0_xattn_all.items() if k in ('q_w', 'q_b', 'k_w', 'k_b', 'v_w', 'v_b', 'o_w', 'o_b')}
    del _L0_xattn_all

    def _L0_ffn_setup():
        import jax, jax.numpy as jnp
        import numpy as np
        B, L, D = (4, 512, 256)
        E, K, S = (8, 2, 2)
        F = 352
        SCALE = 1.0
        INIT = 0.02

        def _swiglu(x, wg, wu, wd):
            return jax.nn.silu(x @ wg) * (x @ wu) @ wd
        key = jax.random.key(seed)
        ks = jax.random.split(key, 8)
        return {'hidden_states': jax.random.normal(ks[0], (B, L, D), jnp.float32), 'gate_w': jax.random.normal(ks[1], (D, E), jnp.float32) * INIT, 'exp_gate': jax.random.normal(ks[2], (E, D, F), jnp.float32) * INIT, 'exp_up': jax.random.normal(ks[3], (E, D, F), jnp.float32) * INIT, 'exp_down': jax.random.normal(ks[4], (E, F, D), jnp.float32) * INIT, 'sh_gate': jax.random.normal(ks[5], (S, D, F), jnp.float32) * INIT, 'sh_up': jax.random.normal(ks[6], (S, D, F), jnp.float32) * INIT, 'sh_down': jax.random.normal(ks[7], (S, F, D), jnp.float32) * INIT}
    _L0_ffn_all = _L0_ffn_setup()
    _L0_ffn_in = {k: v for k, v in _L0_ffn_all.items() if k in ('gate_w', 'exp_gate', 'exp_up', 'exp_down', 'sh_gate', 'sh_up', 'sh_down')}
    del _L0_ffn_all
    return {'x': x, 'ctx_1024': ctx_1024, 'L0_attn_Wq': _L0_attn_in['Wq'], 'L0_attn_Wk': _L0_attn_in['Wk'], 'L0_attn_Wv': _L0_attn_in['Wv'], 'L0_attn_conv_q': _L0_attn_in['conv_q'], 'L0_attn_conv_k': _L0_attn_in['conv_k'], 'L0_attn_conv_v': _L0_attn_in['conv_v'], 'L0_attn_Wb': _L0_attn_in['Wb'], 'L0_attn_fir_s': _L0_attn_in['fir_s'], 'L0_attn_fir_m': _L0_attn_in['fir_m'], 'L0_attn_fir_l': _L0_attn_in['fir_l'], 'L0_attn_gW1': _L0_attn_in['gW1'], 'L0_attn_gb1': _L0_attn_in['gb1'], 'L0_attn_gW2': _L0_attn_in['gW2'], 'L0_attn_gb2': _L0_attn_in['gb2'], 'L0_attn_log_tau': _L0_attn_in['log_tau'], 'L0_attn_eps_logit': _L0_attn_in['eps_logit'], 'L0_attn_norm_w': _L0_attn_in['norm_w'], 'L0_attn_Wo': _L0_attn_in['Wo'], 'L0_xattn_q_w': _L0_xattn_in['q_w'], 'L0_xattn_q_b': _L0_xattn_in['q_b'], 'L0_xattn_k_w': _L0_xattn_in['k_w'], 'L0_xattn_k_b': _L0_xattn_in['k_b'], 'L0_xattn_v_w': _L0_xattn_in['v_w'], 'L0_xattn_v_b': _L0_xattn_in['v_b'], 'L0_xattn_o_w': _L0_xattn_in['o_w'], 'L0_xattn_o_b': _L0_xattn_in['o_b'], 'L0_ffn_gate_w': _L0_ffn_in['gate_w'], 'L0_ffn_exp_gate': _L0_ffn_in['exp_gate'], 'L0_ffn_exp_up': _L0_ffn_in['exp_up'], 'L0_ffn_exp_down': _L0_ffn_in['exp_down'], 'L0_ffn_sh_gate': _L0_ffn_in['sh_gate'], 'L0_ffn_sh_up': _L0_ffn_in['sh_up'], 'L0_ffn_sh_down': _L0_ffn_in['sh_down']}

def reference(x, ctx_1024, L0_attn_Wq, L0_attn_Wk, L0_attn_Wv, L0_attn_conv_q, L0_attn_conv_k, L0_attn_conv_v, L0_attn_Wb, L0_attn_fir_s, L0_attn_fir_m, L0_attn_fir_l, L0_attn_gW1, L0_attn_gb1, L0_attn_gW2, L0_attn_gb2, L0_attn_log_tau, L0_attn_eps_logit, L0_attn_norm_w, L0_attn_Wo, L0_xattn_q_w, L0_xattn_q_b, L0_xattn_k_w, L0_xattn_k_b, L0_xattn_v_w, L0_xattn_v_b, L0_xattn_o_w, L0_xattn_o_b, L0_ffn_gate_w, L0_ffn_exp_gate, L0_ffn_exp_up, L0_ffn_exp_down, L0_ffn_sh_gate, L0_ffn_sh_up, L0_ffn_sh_down):
    import jax
    import jax.numpy as jnp

    def _L0_attn_ref(hidden_states, Wq, Wk, Wv, conv_q, conv_k, conv_v, Wb, fir_s, fir_m, fir_l, gW1, gb1, gW2, gb2, log_tau, eps_logit, norm_w, Wo):
        import jax, jax.numpy as jnp
        import numpy as np
        B, L, D, H = (2, 512, 256, 4)
        DV = D // H
        P = 5
        CHUNK = 32
        CONV_K = 4
        FIR_K = (3, 15, 64)

        def _dwconv(x, w):
            K = w.shape[1]
            xt = jnp.pad(jnp.transpose(x, (0, 2, 1)), ((0, 0), (0, 0), (K - 1, 0)))
            y = jax.lax.conv_general_dilated(xt, w[:, None, :], (1,), 'VALID', dimension_numbers=('NCH', 'OIH', 'NCH'), feature_group_count=w.shape[0])
            return jnp.transpose(y, (0, 2, 1))

        def _l2norm(x):
            return x * jax.lax.rsqrt(jnp.sum(x * x, -1, keepdims=True) + 1e-06)

        def _delta_rule_chunkwise(q, k, v, beta, chunk=CHUNK):
            b, h, Lp, dk = q.shape
            dv = v.shape[-1]
            n = Lp // chunk
            q = _l2norm(q)
            k = _l2norm(k)
            v = v * beta[..., None]
            kb = k * beta[..., None]
            r = lambda t: t.reshape(b, h, n, chunk, -1)
            q, k, v, kb = (r(q), r(k), r(v), r(kb))
            sw = lambda t: jnp.swapaxes(t, -1, -2)
            strict = jnp.tril(jnp.ones((chunk, chunk), bool), -1)
            attn = jnp.where(strict, -(kb @ sw(k)), 0.0)
            T = jnp.linalg.inv(jnp.eye(chunk, dtype=q.dtype) - attn)
            u = T @ v
            w = T @ kb
            incl = jnp.tril(jnp.ones((chunk, chunk), bool), 0)
            qs, ks, us, ws = (jnp.moveaxis(t, 2, 0) for t in (q, k, u, w))
            S0 = jnp.zeros((b, h, dk, dv), q.dtype)

            def step(S, inp):
                q_i, k_i, u0, w_i = inp
                local = jnp.where(incl, q_i @ sw(k_i), 0.0)
                u_i = u0 - w_i @ S
                o_i = q_i @ S + local @ u_i
                return (S + sw(k_i) @ u_i, o_i)
            S, o = jax.lax.scan(step, S0, (qs, ks, us, ws))
            return (jnp.moveaxis(o, 0, 2).reshape(b, h, Lp, dv), S)

        def _stats(t):
            m = jnp.mean(t, -1, keepdims=True)
            v = jnp.mean(t * t, -1, keepdims=True)
            a = jnp.mean(jnp.abs(t), -1, keepdims=True)
            nrm = jnp.sqrt(jnp.sum(t * t, -1, keepdims=True))
            s = jnp.concatenate([jnp.broadcast_to(x, t.shape) for x in (m, v, a, nrm)], -1)
            return s.reshape(t.shape[0], t.shape[1], -1)

        def _forward(hs, Wq, Wk, Wv, conv_q, conv_k, conv_v, Wb, fir_s, fir_m, fir_l, gW1, gb1, gW2, gb2, log_tau, eps_logit, norm_w, Wo):
            b, Ln, _ = hs.shape
            q = jax.nn.silu(_dwconv(hs @ Wq, conv_q))
            k = jax.nn.silu(_dwconv(hs @ Wk, conv_k))
            v = jax.nn.silu(_dwconv(hs @ Wv, conv_v))
            beta = jax.nn.sigmoid(hs @ Wb)
            bh = lambda t: jnp.transpose(t.reshape(b, Ln, H, -1), (0, 2, 1, 3))
            o_d, _ = _delta_rule_chunkwise(bh(q), bh(k), bh(v), jnp.transpose(beta, (0, 2, 1)))
            delta_path = jnp.transpose(o_d, (0, 2, 1, 3))
            paths = jnp.stack([_dwconv(v, fir_s).reshape(b, Ln, H, DV), _dwconv(v, fir_m).reshape(b, Ln, H, DV), _dwconv(v, fir_l).reshape(b, Ln, H, DV), delta_path, v.reshape(b, Ln, H, DV)], axis=3)
            stats_flat = jnp.concatenate([_stats(paths[..., p, :]) for p in range(P)], -1)
            gate_in = jnp.concatenate([hs, stats_flat], -1)
            logits = jax.nn.gelu(gate_in @ gW1 + gb1, approximate=False) @ gW2 + gb2
            logits = logits.reshape(b, Ln, H, P)
            tau = jax.nn.softplus(log_tau) + 0.5
            probs = jax.nn.softmax(logits / tau[:, None], -1)
            eps = jax.nn.sigmoid(eps_logit) * 0.2
            probs = probs * (1.0 - jnp.sum(eps, -1, keepdims=True)) + eps
            o = jnp.einsum('blhp,blhpd->blhd', probs, paths)
            o = o * jax.lax.rsqrt(jnp.mean(o * o, -1, keepdims=True) + 1e-05) * norm_w
            return o.reshape(b, Ln, D) @ Wo
        return _forward(hidden_states, Wq, Wk, Wv, conv_q, conv_k, conv_v, Wb, fir_s, fir_m, fir_l, gW1, gb1, gW2, gb2, log_tau, eps_logit, norm_w, Wo)

    def _L0_xattn_ref(query, key, value, q_w, q_b, k_w, k_b, v_w, v_b, o_w, o_b):
        import jax, jax.numpy as jnp
        import numpy as np
        EMBED_DIM = 256
        NUM_HEADS = 16
        HEAD_DIM = EMBED_DIM // NUM_HEADS
        SCALE = HEAD_DIM ** (-0.5)

        def _split_heads(x, B):
            return x.reshape(B, -1, NUM_HEADS, HEAD_DIM).transpose(0, 2, 1, 3)
        B = query.shape[0]
        q = _split_heads(query @ q_w + q_b, B)
        k = _split_heads(key @ k_w + k_b, B)
        v = _split_heads(value @ v_w + v_b, B)
        scores = jnp.einsum('bhqd,bhkd->bhqk', q, k) * SCALE
        attn = jax.nn.softmax(scores, axis=-1)
        out = jnp.einsum('bhqk,bhkd->bhqd', attn, v)
        out = out.transpose(0, 2, 1, 3).reshape(B, -1, EMBED_DIM)
        return out @ o_w + o_b

    def _L0_ffn_ref(hidden_states, gate_w, exp_gate, exp_up, exp_down, sh_gate, sh_up, sh_down):
        import jax, jax.numpy as jnp
        import numpy as np
        B, L, D = (4, 512, 256)
        E, K, S = (8, 2, 2)
        F = 352
        SCALE = 1.0
        INIT = 0.02

        def _swiglu(x, wg, wu, wd):
            return jax.nn.silu(x @ wg) * (x @ wu) @ wd
        Bx, Lx, Dx = hidden_states.shape
        x = hidden_states.reshape(-1, Dx)
        T = x.shape[0]
        shared = jnp.zeros_like(x)
        for i in range(sh_gate.shape[0]):
            shared = shared + _swiglu(x, sh_gate[i], sh_up[i], sh_down[i])
        logits = x @ gate_w
        probs = jax.nn.softmax(logits.astype(jnp.float32), axis=-1)
        w, sel = jax.lax.top_k(probs, K)
        w = w / jnp.sum(w, axis=-1, keepdims=True)
        w = w.astype(hidden_states.dtype)
        Wte = jnp.zeros((T, exp_gate.shape[0]), hidden_states.dtype)
        Wte = Wte.at[jnp.arange(T)[:, None], sel].add(w)
        routed = jnp.zeros_like(x)
        for e in range(exp_gate.shape[0]):
            routed = routed + Wte[:, e:e + 1] * _swiglu(x, exp_gate[e], exp_up[e], exp_down[e])
        out = shared + SCALE * routed
        return out.reshape(Bx, Lx, Dx)
    x = _layernorm(x + _L0_attn_ref(x, L0_attn_Wq, L0_attn_Wk, L0_attn_Wv, L0_attn_conv_q, L0_attn_conv_k, L0_attn_conv_v, L0_attn_Wb, L0_attn_fir_s, L0_attn_fir_m, L0_attn_fir_l, L0_attn_gW1, L0_attn_gb1, L0_attn_gW2, L0_attn_gb2, L0_attn_log_tau, L0_attn_eps_logit, L0_attn_norm_w, L0_attn_Wo), axis=-1)
    x = _layernorm(x + _L0_xattn_ref(x, ctx_1024, ctx_1024, L0_xattn_q_w, L0_xattn_q_b, L0_xattn_k_w, L0_xattn_k_b, L0_xattn_v_w, L0_xattn_v_b, L0_xattn_o_w, L0_xattn_o_b), axis=-1)
    x = _layernorm(x + _L0_ffn_ref(x, L0_ffn_gate_w, L0_ffn_exp_gate, L0_ffn_exp_up, L0_ffn_exp_down, L0_ffn_sh_gate, L0_ffn_sh_up, L0_ffn_sh_down), axis=-1)
    return x

_drawn_inputs = setup_inputs


def setup_inputs(seed=0):
    import zlib

    import numpy as np

    out = dict(_drawn_inputs(seed))
    spreads = {'L0_attn_gb1': (0.0, 2.0),
     'L0_attn_log_tau': (0.0, 2.0),
     'L0_attn_eps_logit': (0.0, 0.8),
     'L0_attn_norm_w': (1.0, 0.2),
     'L0_xattn_q_b': (0.0, 0.409),
     'L0_xattn_k_b': (0.0, 2.0),
     'L0_xattn_v_b': (0.0, 0.1),
     'L0_xattn_o_b': (0.0, 0.1)}
    factors = {'L0_attn_gb2': 4.977,
     'L0_ffn_gate_w': 4.675,
     'L0_ffn_exp_gate': 4.043,
     'L0_ffn_exp_up': 4.04,
     'L0_ffn_exp_down': 4.02,
     'L0_attn_gW1': 4.968,
     'L0_ffn_sh_gate': 3.165,
     'L0_ffn_sh_up': 3.124,
     'L0_ffn_sh_down': 3.124}
    for name, (base, spread) in spreads.items():
        noise = np.random.default_rng([zlib.crc32(name.encode()), seed]).standard_normal(out[name].shape)
        drawn = base * np.exp(spread * noise) if base else spread * noise
        out[name] = jnp.asarray(drawn.astype(out[name].dtype))
    for name, factor in factors.items():
        out[name] = (out[name] * factor).astype(out[name].dtype)
    return out
```

```python
from contextlib import ExitStack, contextmanager

import concourse.bass as bass
from concourse import mybir

F32 = mybir.dt.float32
U32 = mybir.dt.uint32
ALU = mybir.AluOpType
ACT = mybir.ActivationFunctionType
AX = mybir.AxisListType
ET = mybir.EngineType

P = 128
B, T, D = 8, 256, 256
KT = D // P
TT = T // P
H, DH = 4, 64
HL = P // DH
NP = TT * H
CH = 32
NCH = P // CH
TAPS = 4
FIRS = (3, 15, 64)
NF = len(FIRS)
NPATH = NF + 2
NS = 4
HF = 2 * D
BLK = 64
NBLK = T // BLK
XH, XD = 16, 16
NE, NSH, FF = 8, 2, 352
FT = [(0, 128), (128, 128), (256, 96)]
TG = 512
NTOK = B * T


class Mark:

    def __init__(self, src, index, loop, prev=False):
        self.src, self.index, self.loop, self.prev = src, index, loop, prev


class Counter:

    def __init__(self, prog, name, unit):
        self.prog, self.name, self.unit = prog, name, unit
        self.sem = prog.ctx.enter_context(prog.nc.semaphore(name))
        self.count = 0
        prog.counters.append(self)

    def tick(self, ins):
        ins.then_inc(self.sem, self.unit)
        self.count += 1
        return Mark(self, self.count, self.prog.loop)


class Slot:

    def __init__(self, prog, name):
        self.name, self.readers = name, []
        prog.slots.append(self)

    def read(self, *marks):
        self.readers = list(marks)
        return marks[-1]

    def also(self, *marks):
        self.readers += list(marks)


class Loop:
    def __init__(self, name, engines):
        self.name, self.engines, self.reg, self.base = name, engines, None, {}


class Engine:
    def __init__(self, prog, eng, name, serial):
        self.prog, self.eng, self.serial = prog, eng, serial
        self.done = Counter(prog, name, 1)
        self.seen = {}
        self.last = None

    def wait(self, marks):
        prog = self.prog
        best = {}
        for m in marks:
            if m is None:
                continue
            if isinstance(m, (list, tuple)):
                raise TypeError("flat list of marks")
            loop = m.loop
            if prog.loop is not None and loop is not prog.loop:
                if self in prog.loop.engines and not prog.loop.outside:
                    continue
            if loop is not None and prog.loop is loop:
                value = m.index - (prog.per(loop, m.src) if m.prev else 0)
                key = (m.src, loop)
            elif loop is not None:
                value, key = loop.final[m.src], (m.src, None)
            else:
                value, key = m.index, (m.src, None)
            if best.get(key, -10**9) < value:
                best[key] = value
        for (src, loop), value in best.items():
            if self.seen.get((src, loop), -10**9) >= value:
                continue
            self.seen[(src, loop)] = value
            if loop is None:
                self.eng.wait_ge(src.sem, value * src.unit)
            else:
                step = prog.per(loop, src) * src.unit
                self.eng.wait_ge(src.sem, loop.reg * step + value * src.unit)
                if self is prog.sp:
                    self.part()

    def part(self):
        if self.prog.loop is not None:
            self.eng.sem_inc(self.prog.parted, 1)

    def op(self, ins_of, *args, after=(), count=True, split=False, **kw):
        own = [self.last] if self.serial else []
        self.wait(own + list(after))
        if split or self is self.prog.pool:
            self.part()
        ins = ins_of(*args, **kw)
        if not count:
            return None
        self.last = self.done.tick(ins)
        return self.last


class Program:
    def __init__(self, nc, ctx, plan):
        self.nc, self.ctx, self.plan, self.new_plan = nc, ctx, plan, {}
        self.counters, self.slots, self.loop = [], [], None
        self.pe = Engine(self, nc.tensor, "pe_done", False)
        self.act = Engine(self, nc.scalar, "act_done", True)
        self.dve = Engine(self, nc.vector, "dve_done", True)
        self.pool = Engine(self, nc.gpsimd, "pool_done", True)
        self.sp = Engine(self, nc.sync, "sp_done", False)
        self.engines = [self.pe, self.act, self.dve, self.pool, self.sp]
        self.dma_sems = {}
        self.parted = ctx.enter_context(nc.semaphore("parted"))

    def per(self, loop, src):
        return self.plan.get(loop.name, {}).get("per", {}).get(src.name, 1)

    def slot(self, name):
        return Slot(self, name)

    def dma(self, stream, out, in_, after=(), queue=None, **kw):
        if stream not in self.dma_sems:
            self.dma_sems[stream] = Counter(self, "dma_" + stream, 16)
        q = queue or self.sp
        q.wait(list(after))
        return self.dma_sems[stream].tick(q.eng.dma_start(out, in_, **kw))

    def meet(self, engines=None):
        engines = engines or self.engines
        absent = [e.done for e in self.engines if e not in engines]
        for e in engines:
            e.wait([Mark(c, c.count, None) for c in self.counters if c.count and c not in absent])

    @contextmanager
    def repeat(self, name, n, engines=None, start=0):
        engines = engines or self.engines
        loop = Loop(name, engines)
        loop.outside = False
        plan = self.plan.get(name, {})
        per = plan.get("per", {})
        for c in per:
            if c.startswith("dma_") and c[4:] not in self.dma_sems:
                self.dma_sems[c[4:]] = Counter(self, c, 16)
        self.meet(engines)
        owner = {e.done: e for e in self.engines}
        for c in self.counters:
            if per.get(c.name):
                (owner.get(c) or engines[-1]).eng.sem_inc(c.sem, per[c.name] * c.unit)
                c.count += per[c.name]
        names = {c.name: c for c in self.counters}
        outer = {s: s.readers for s in self.slots}
        for s in self.slots:
            s.readers = [Mark(names[c], i, loop, True) for c, i in plan.get("slots", {}).get(s.name, [])
                         if c in names]
        for s in self.slots:
            for m in s.readers:
                m.index += m.src.count
        before = {c: c.count for c in self.counters}
        for e in engines:
            e.seen, e.last = {}, None
        with self.nc.Fori(0, n, engines=tuple(e.eng.engine for e in engines)) as reg:
            loop.reg, self.loop = reg, loop
            last_marks = plan.get("last", {})
            for e in engines:
                if e.serial and e.done.name in last_marks:
                    e.last = Mark(e.done, before[e.done] + last_marks[e.done.name], loop, True)
            yield reg
        self.loop = None
        new = {"per": {}, "slots": {}, "last": {}}
        loop.final = {}
        for c in self.counters:
            start_count = before.get(c, 0)
            made = c.count - start_count
            if made:
                new["per"][c.name] = made
            if c in owner and made:
                new["last"][c.name] = made
            c.count = start_count + made * n
            loop.final[c] = c.count
        for s in self.slots:
            mine = [m for m in s.readers if m.loop is loop and not m.prev]
            if mine:
                new["slots"][s.name] = [(m.src.name, m.index - before.get(m.src, 0)) for m in mine]
            elif s in outer:
                s.readers = outer[s]
        self.new_plan[name] = new
        for e in engines:
            e.seen, e.last = {}, None


def make_constants(pg, a, env):
    nc, pool, dve, act, ctx = pg.nc, pg.pool, pg.dve, pg.act, pg.ctx
    sb = env.sb
    env.ident = sb("ident", [P, P])
    env.causal = sb("causal", [P, P])
    env.exponent = sb("exponent", [P, 3, 40])
    env.headmask = sb("headmask", [P, P // XD])
    env.expert_no = sb("expert_no", [P, NE])
    pool.op(nc.gpsimd.memset, env.ident[:], 0.0)
    pool.op(nc.gpsimd.affine_select, out=env.ident[:], in_=env.ident[:], compare_op=ALU.not_equal,
            fill=1.0, base=0, pattern=[[-1, P]], channel_multiplier=1)
    pool.op(nc.gpsimd.memset, env.causal[:], 1.0)
    pool.op(nc.gpsimd.affine_select, out=env.causal[:], in_=env.causal[:], compare_op=ALU.is_ge,
            fill=0.0, base=0, pattern=[[1, P]], channel_multiplier=-1)
    for k, x in enumerate((-0.5, 0.5, 2.718281828459045)):
        pool.op(nc.gpsimd.memset, env.exponent[:, k, :], x)
    pool.op(nc.gpsimd.memset, env.headmask[:], 1.0)
    pool.op(nc.gpsimd.affine_select, out=env.headmask[:], in_=env.headmask[:], compare_op=ALU.is_ge,
            fill=0.0, base=0, pattern=[[-XD, P // XD]], channel_multiplier=1)
    pool.op(nc.gpsimd.affine_select, out=env.headmask[:], in_=env.headmask[:], compare_op=ALU.is_ge,
            fill=0.0, base=XD - 1, pattern=[[XD, P // XD]], channel_multiplier=-1)
    for e in range(NE):
        pool.op(nc.gpsimd.memset, env.expert_no[:, e:e + 1], float(e))


def load_weight(pg, env, sb, name, dram, cols, stream):
    w = sb(name, [P, D // P, cols])
    m = pg.dma(stream, w[:], dram.rearrange("(k p) n -> p k n", p=P))
    return w, m


def phase_project(pg, a, env):
    nc, pe, act, dve, pool = pg.nc, pg.pe, pg.act, pg.dve, pg.pool
    with ExitStack() as mem:
        def sb(n, shape, dt=F32):
            return mem.enter_context(nc.sbuf_tensor(n, shape, dt))
        ps = env.ps
        W = []
        for n, src in (("wq", a["Wq"]), ("wk", a["Wk"]), ("wv", a["Wv"])):
            w, m = load_weight(pg, env, sb, n, src, D, "w_project")
            W.append(w)
        wb, _ = load_weight(pg, env, sb, "wb", a["Wb"], H, "w_project")
        taps = sb("taps", [P, 3, KT, TAPS])
        for j, src in enumerate((a["conv_q"], a["conv_k"], a["conv_v"])):
            pg.dma("w_project", taps[:, j], src.rearrange("(k p) i -> p k i", p=P))

        sel = [sb(f"sel{i}", [P, 180]) for i in range(2)]
        rows = [sb(f"gw1_rows{i}", [P, 5, HF]) for i in range(2)]
        rows_free = [pg.slot(f"gw1_rows{i}") for i in range(2)]
        for i, (lo, hi) in enumerate(((1.0 / DH, 1.0 / DH), (1.0 / DH, 1.0))):
            pool.op(nc.gpsimd.memset, sel[i][:], 0.0)
            pool.op(nc.gpsimd.memset, sel[i][0:DH, 80:81], lo)
            pool.op(nc.gpsimd.memset, sel[i][DH:P, 100:101], hi)
        sel_ready = pool.last
        gview = a["gW1"][D:, :].rearrange("(g k p) n -> g p k n", k=5, p=P)
        for g in range(8):
            i = g % 2
            m = pg.dma(f"gw1_{i}", rows[i][:], gview[g], after=rows_free[i].readers)
            for k in range(5):
                kt = 5 * g + k
                path, head, half = kt // 8, (kt // 2) % 4, kt % 2
                c0 = half * 2 * 20 + path * 4 + head
                r = pe.op(nc.tensor.matmul, ps[0:80, 0, :], sel[half][:, 80 - c0:160 - c0], rows[i][:, k, :],
                          start=(kt == 0), stop=(kt == 39), after=[m, sel_ready])
            rows_free[i].read(r)
        act.op(nc.scalar.copy, env.w1s[:], ps[0:80, 0, :], after=[r])

        xin = [sb(f"xin{i}", [P, TT, D]) for i in range(2)]
        xT = [sb(f"xT{i}", [P, KT, T]) for i in range(2)]
        raw = [sb(f"raw{i}", [P, 3, KT, TAPS - 1 + T]) for i in range(2)]
        conv = [sb(f"conv{i}", [P, 3, KT, T]) for i in range(2)]
        tok = [sb(f"tok{i}", [P, TT, 3, D]) for i in range(2)]
        sq = sb("sq", [P, 2, TT, D])
        ss = sb("ss", [P, 2 * TT * H])
        rn = sb("rn", [P, 2 * TT * H])
        kT = sb("kT", [P, KT, TT, P])
        km = sb("km", [P, KT, TT, HL, P])
        diag = [sb(f"diag{i}", [P, NP, CH]) for i in range(2)]
        for i in range(2):
            dve.op(nc.vector.memset, raw[i][:], 0.0)
        dve.op(nc.vector.memset, km[:], 0.0)
        sl = {n: pg.slot(n) for n in ("bank0", "bank13", "bank4", "bank57", "sq", "ss", "rn", "kT", "km")}
        for n in ("xin", "xT", "raw", "conv", "tok", "diag"):
            for i in range(2):
                sl[n, i] = pg.slot(f"{n}{i}")

        with pg.repeat("project", B // 2) as it:
            for i in range(2):
                b = it * 2 + i
                m_x = pg.dma(f"x{i}", xin[i][:], a["x"].rearrange("b (t p) d -> p b t d", p=P)[:, bass.ds(b, 1)]
                             .rearrange("p b t d -> p (b t) d"), after=sl["xin", i].readers)
                for k in range(KT):
                    for t in range(TT):
                        m = pe.op(nc.tensor.transpose, ps[:, 0, (k * TT + t) * P:(k * TT + t + 1) * P],
                                  xin[i][:, t, k * P:(k + 1) * P], env.ident[:],
                                  after=[m_x] + sl["bank0"].readers)
                sl["xin", i].read(m)
                m_xT = act.op(nc.scalar.copy, xT[i][:].rearrange("p k t -> p (k t)"), ps[:, 0, :],
                              after=[m] + sl["xT", i].readers)
                sl["bank0"].read(m_xT)
                for j in range(3):
                    for c in range(KT):
                        for k in range(KT):
                            m = pe.op(nc.tensor.matmul, ps[:, 1 + j, c * T:(c + 1) * T], W[j][:, k, c * P:(c + 1) * P],
                                      xT[i][:, k, :], start=(k == 0), stop=(k == KT - 1),
                                      after=[m_xT] + sl["bank13"].readers)
                m_proj = m
                for t in range(TT):
                    for k in range(KT):
                        m = pe.op(nc.tensor.matmul, ps[:, 4, t * H:(t + 1) * H], xT[i][:, k, t * P:(t + 1) * P],
                                  wb[:, k, :], start=(k == 0), stop=(k == KT - 1), after=[m_xT] + sl["bank4"].readers)
                m_beta = m
                sl["xT", i].read(m)
                m_raw = act.op(nc.scalar.copy, raw[i][:, :, :, TAPS - 1:].rearrange("p j c t -> p (j c) t"),
                               ps[:, 1:4, :].rearrange("p j (c t) -> p (j c) t", c=KT),
                               after=[m_proj] + sl["raw", i].readers)
                sl["bank13"].read(m_raw)
                bt = env.beta[:, bass.ds(b, 1), :].rearrange("p b n -> p (b n)")
                m = act.op(nc.scalar.activation, bt, ps[:, 4, 0:NP], ACT.Tanh, scale=0.5, after=[m_beta])
                sl["bank4"].read(m)
                m_beta = dve.op(nc.vector.tensor_scalar, bt, bt, 0.5, 0.5, ALU.mult, ALU.add, after=[m])
                for j in range(3):
                    for c in range(KT):
                        m = act.op(nc.scalar.activation, conv[i][:, j, c, :], raw[i][:, j, c, 0:T], ACT.Copy,
                                   scale=taps[:, j, c, 0:1], after=[m_raw] + sl["conv", i].readers)
                        for s in range(1, TAPS):
                            m = dve.op(nc.vector.scalar_tensor_tensor, out=conv[i][:, j, c, :],
                                       in0=raw[i][:, j, c, s:s + T], scalar=taps[:, j, c, s:s + 1],
                                       in1=conv[i][:, j, c, :], op0=ALU.mult, op1=ALU.add, after=[m])
                sl["raw", i].read(m)
                flat = conv[i][:].rearrange("p j c t -> p (j c t)")
                m_silu = act.op(nc.scalar.activation, flat, flat, ACT.Silu, after=[m])
                for j in range(3):
                    for t in range(TT):
                        for c in range(KT):
                            m = pe.op(nc.tensor.transpose, ps[:, 1 + j, (t * KT + c) * P:(t * KT + c + 1) * P],
                                      conv[i][:, j, c, t * P:(t + 1) * P], env.ident[:],
                                      after=[m_silu] + sl["bank13"].readers)
                m_t = m
                sl["conv", i].read(m)
                m_v = act.op(nc.scalar.copy, tok[i][:, :, 2, :], ps[:, 3, :].rearrange("p (t d) -> p t d", t=TT),
                             after=[m_t] + sl["tok", i].readers)
                m_sq = act.op(nc.scalar.activation, sq[:].rearrange("p j t d -> p (j t d)"),
                              ps[:, 1:3, :].rearrange("p j n -> p (j n)"), ACT.Square, after=sl["sq"].readers)
                m_ss = dve.op(nc.vector.tensor_reduce, ss[:], sq[:].rearrange("p j t (h d) -> p (j t h) d", h=H),
                              AX.X, ALU.add, after=[m_sq] + sl["ss"].readers)
                sl["sq"].read(m_ss)
                m = pool.op(nc.gpsimd.tensor_scalar, rn[:], ss[:], 1.0, 1e-6, ALU.mult, ALU.add,
                            after=[m_ss] + sl["rn"].readers)
                sl["ss"].read(m)
                m_rn = pool.op(nc.gpsimd.tensor_tensor, rn[:], rn[:], env.exponent[:, 0, 0:2 * NP], ALU.pow)
                for j in range(2):
                    m = dve.op(nc.vector.tensor_tensor, tok[i][:, :, j, :].rearrange("p t (h d) -> p t h d", h=H),
                               ps[:, 1 + j, :].rearrange("p (t h d) -> p t h d", t=TT, h=H),
                               rn[:, j * NP:(j + 1) * NP].rearrange("p (t h) -> p t h", t=TT).unsqueeze(3)
                               .broadcast_to([P, TT, H, DH]), ALU.mult, after=[m_rn, m_t])
                m_tok = m
                sl["rn"].read(m)
                sl["bank13"].read(m_v, m_sq, m_tok)
                m_st = pg.dma(f"tok{i}", env.tok_dram[bass.ds(b, 1)].rearrange("b p n -> p (b n)"),
                              tok[i][:].rearrange("p t j d -> p (t j d)"), after=[m_v, m_tok])
                for c in range(KT):
                    for t in range(TT):
                        m = pe.op(nc.tensor.transpose, ps[:, 4, (c * TT + t) * P:(c * TT + t + 1) * P],
                                  tok[i][:, t, 1, c * P:(c + 1) * P], env.ident[:],
                                  after=[m_tok] + sl["bank4"].readers)
                sl["tok", i].read(m_st, m)
                m_kT = act.op(nc.scalar.copy, kT[:].rearrange("p c t n -> p (c t n)"), ps[:, 4, :],
                              after=[m] + sl["kT"].readers)
                for h in range(HL):
                    q = slice(h * DH, (h + 1) * DH)
                    m_km = act.op(nc.scalar.copy, km[q, :, :, h, :].rearrange("p c t n -> p (c t) n"),
                                  ps[q, 4, :].rearrange("p (c n) -> p c n", n=P), after=[m] + sl["km"].readers)
                sl["bank4"].read(m_km)
                for c in range(KT):
                    for t in range(TT):
                        n = t * H + c * HL
                        m = pe.op(nc.tensor.matmul, ps[:, 5 + n // 4, (n % 4) * P:(n % 4 + HL) * P], kT[:, c, t, :],
                                  km[:, c, t, :, :], start=True, stop=True,
                                  after=[m_kT, m_km] + sl["bank57"].readers)
                sl["kT"].read(m)
                sl["km"].read(m)
                last = m
                for c in range(NCH):
                    q = slice(c * CH, (c + 1) * CH)
                    src = ps[q, 5:7, :].rearrange("p u (n j) -> p (u n) j", j=P)[:, :, q]
                    m = dve.op(nc.vector.tensor_tensor, diag[i][q, :, :], src,
                               env.beta[q, bass.ds(b, 1), :].rearrange("p b n -> p (b n)").unsqueeze(2)
                               .broadcast_to([CH, NP, CH]), ALU.mult, after=[last, m_beta] + sl["diag", i].readers)
                sl["bank57"].read(m)
                m = pg.dma(f"diag{i}", env.a_dram[:, bass.ds(b, 1), :].rearrange("p b n -> p (b n)"),
                           diag[i][:].rearrange("p n j -> p (n j)"), after=[m])
                sl["diag", i].read(m)
        pg.meet()


def phase_invert_and_fir(pg, a, env):
    nc, pe, act, dve, pool = pg.nc, pg.pe, pg.act, pg.dve, pg.pool
    G = B * NP * NCH // P
    with ExitStack() as mem:
        def sb(n, shape, dt=F32):
            return mem.enter_context(nc.sbuf_tensor(n, shape, dt))
        ps = env.ps
        am = sb("am", [P, G, CH, CH])
        inv = sb("inv", [P, G, CH, CH])
        tmp = sb("tmp", [P, G, CH, CH])
        for c in range(NCH):
            for g in range(G):
                m_am = pg.dma("am", am[c * CH:(c + 1) * CH, g],
                              env.a_dram[c * CH:(c + 1) * CH].rearrange("i b (n j) -> (b n) i j", j=CH)
                              [g * 32:(g + 1) * 32])
        win = sb("win", [P, B * NBLK, P])
        wpad = sb("wpad", [P, KT, NF, 2 * P])
        m_w = pool.op(nc.gpsimd.memset, wpad[:].rearrange("p k f n -> p (k f n)"), 0.0)
        m_win0 = pool.op(nc.gpsimd.memset, win[0:BLK].rearrange("p n c -> p (n c)"), 0.0)
        for f, taps in enumerate(FIRS):
            m_wp = pg.dma("wpad", wpad[:, :, f, P - taps:P], a[f"fir{f}"].rearrange("(k p) i -> p k i", p=P), after=[m_w])

        dve.op(nc.vector.memset, inv[:].rearrange("p g a b -> p (g a b)"), 0.0)
        dve.op(nc.vector.memset, inv[:].rearrange("p g a b -> p g (a b)")[:, :, 0:CH * CH:CH + 1], 1.0)
        for i in range(1, CH):
            dve.op(nc.vector.tensor_tensor, tmp[:, :, 0:i, 0:i], inv[:, :, 0:i, 0:i],
                   am[:, :, i, 0:i].unsqueeze(2).broadcast_to([P, G, i, i]), ALU.mult, after=[m_am])
            dve.op(nc.vector.tensor_reduce, inv[:, :, 0:i, i], tmp[:, :, 0:i, 0:i], AX.X, ALU.add, negate=True)
        m_inv = dve.last
        for g in range(G):
            m_tr = dve.op(nc.vector.tensor_copy, am[:, g], inv[:, g].rearrange("p j i -> p i j"))
        for k, (src, m) in enumerate(((inv, m_inv), (am, m_tr))):
            for c in range(NCH):
                for g in range(G):
                    pg.dma("inv", env.t_dram[k, c * CH:(c + 1) * CH].rearrange("i n j -> n i j")[g * 32:(g + 1) * 32],
                           src[c * CH:(c + 1) * CH, g], after=[m], queue=pool)

        hank = sb("hank", [P, P, NF, BLK])
        stage = sb("stage", [P, NF, BLK, CH])
        shifted = sb("shifted", [P, NF, P + 8])
        s_h, s_sh, s_win, s_st = (pg.slot(n) for n in ("hank", "shifted", "win", "stage"))
        banks = [pg.slot(f"fir_bank{n}") for n in range(8)]
        tokv = env.tok_dram.rearrange("b p (t j d) -> j t p b d", t=TT, j=3)[2]
        for c in range(KT):
            for blk in range(NBLK):
                for half in range(2):
                    start = (blk - 1) * BLK + half * BLK
                    if start < 0:
                        continue
                    t, off = start // P, start % P
                    m_win = pg.dma("win", win[half * BLK:(half + 1) * BLK].rearrange("p (b n) c -> p n b c", n=NBLK)[:, blk],
                                   tokv[t, off:off + BLK, :, c * P:(c + 1) * P], after=[m_win0] + s_win.readers)
            with pg.repeat(f"hankel{c}", BLK // 8, engines=[pe, act, pool]) as it:
                m_s = pool.op(nc.gpsimd.tensor_copy, shifted[:], wpad[:, c, :, bass.ds(it * 8, P + 8)],
                              after=s_sh.readers)
                for f in range(NF):
                    for half in range(2):
                        n = f * 2 + half
                        for j in range(4):
                            m = pe.op(nc.tensor.transpose, ps[:, n, j * P:(j + 1) * P],
                                      shifted[:, f, half * 4 + j:half * 4 + j + P], env.ident[:],
                                      after=[m_s] + banks[n].readers)
                        dst = hank[:, :, f, bass.ds(it * (-8) + (BLK - 1 - half * 4 - 3), 4)]
                        m = act.op(nc.scalar.copy, dst.rearrange("p c j -> p j c"),
                                   ps[:, n, :].rearrange("p (j c) -> p j c", c=P)[:, ::-1, :], after=[m])
                        banks[n].read(m)
                s_sh.read(pe.last)
            pg.meet([pe])
            for pair in range(CH // 2):
                bank = pair % 8
                for u in range(2):
                    for q in range(NCH):
                        ch = q * CH + pair * 2 + u
                        m = pe.op(nc.tensor.matmul, ps[q * CH:(q + 1) * CH, bank, u * NF * BLK:(u + 1) * NF * BLK],
                                  win[:, :, ch], hank[:, ch, :, :].rearrange("p f t -> p (f t)"),
                                  start=True, stop=True, after=[m_win] + banks[bank].readers)
                m = act.op(nc.scalar.copy, stage[:].rearrange("p f t c -> p c (f t)")[:, pair * 2:pair * 2 + 2],
                           ps[:, bank, 0:2 * NF * BLK].rearrange("p (c n) -> p c n", c=2), after=[m] + s_st.readers)
                banks[bank].read(m)
            s_win.read(pe.last)
            ms = []
            for q in range(NCH):
                for f in range(NF):
                    ms.append(pg.dma("stage", env.fir_dram[f].rearrange("(n t) d -> n t d", t=BLK)
                                     [:, :, c * P + q * CH:c * P + (q + 1) * CH], stage[q * CH:(q + 1) * CH, f],
                                     after=[m]))
            s_st.read(*ms[-1:])
        pg.meet()


def phase_delta_and_gate(pg, a, env):
    nc, pe, act, dve, pool = pg.nc, pg.pe, pg.act, pg.dve, pg.pool
    with ExitStack() as mem:
        def sb(n, shape, dt=F32):
            return mem.enter_context(nc.sbuf_tensor(n, shape, dt))
        ps = env.ps
        V, S, G = nc.vector, nc.scalar, nc.gpsimd
        w1x, _ = load_weight(pg, env, sb, "w1x", a["gW1"][0:D, :], HF, "w_gate")
        gw2 = sb("gw2", [P, HF // P, H * NPATH])
        pg.dma("w_gate", gw2[:], a["gW2"].rearrange("(k p) n -> p k n", p=P))
        gb1 = sb("gb1", [P, HF // P])
        pg.dma("w_gate", gb1[:], a["gb1"].rearrange("(k p) -> p k", p=P), allow_slow_non_contiguous=True)
        wo, m_w = load_weight(pg, env, sb, "wo", a["Wo"], D, "w_gate")
        nw = sb("nw", [P, 1])
        for h in range(HL):
            pg.dma("w_gate", nw[h * DH:(h + 1) * DH, :], a["norm_w"].rearrange("(d o) -> d o", o=1))
        gb2 = sb("gb2", [P, H * NPATH])
        pg.dma("w_gate", gb2[:], a["gb2"].partition_broadcast(P))
        lt = sb("lt", [P, H])
        pg.dma("w_gate", lt[:], a["log_tau"].partition_broadcast(P))
        eps = sb("eps", [P, H, NPATH])
        m_w = pg.dma("w_gate", eps[:].rearrange("p h n -> p (h n)"), a["eps_logit"].rearrange("h n -> (h n)").partition_broadcast(P))
        dve.op(V.tensor_scalar, wo[:].rearrange("p k n -> p (k n)"), wo[:].rearrange("p k n -> p (k n)"),
               nw[:, 0:1], None, ALU.mult, after=[m_w])
        t1, t2 = sb("t1", [P, H]), sb("t2", [P, H])
        m = act.op(S.activation, t1[:], lt[:], ACT.Abs, after=[m_w])
        m = act.op(S.activation, t1[:], t1[:], ACT.Exp, scale=-1.0)
        m = act.op(S.activation, t1[:], t1[:], ACT.Ln, bias=1.0)
        dve.op(V.tensor_scalar, t2[:], lt[:], 0.0, 0.5, ALU.max, ALU.add)
        dve.op(V.tensor_tensor, t2[:], t2[:], t1[:], ALU.add, after=[m])
        itau = sb("itau", [P, H])
        dve.op(V.reciprocal, itau[:], t2[:])
        m = act.op(S.activation, eps[:].rearrange("p h n -> p (h n)"), eps[:].rearrange("p h n -> p (h n)"), ACT.Exp, scale=-1.0)
        dve.op(V.tensor_scalar, eps[:], eps[:], 1.0, None, ALU.add, after=[m])
        dve.op(V.reciprocal, eps[:], eps[:])
        dve.op(V.tensor_scalar, eps[:], eps[:], 0.2, None, ALU.mult)
        keep = sb("keep", [P, H])
        dve.op(V.tensor_reduce, keep[:], eps[:], AX.X, ALU.add)
        dve.op(V.tensor_scalar, keep[:], keep[:], -1.0, 1.0, ALU.mult, ALU.add)

        tok = [sb(f"dtok{i}", [P, TT, 3, D]) for i in range(2)]
        xin = [sb(f"dx{i}", [P, TT, D]) for i in range(2)]
        paths = [sb(f"paths{i}", [P, NPATH, TT, D]) for i in range(2)]
        g0 = [sb(f"g0_{i}", [P, NP, P]) for i in range(2)]
        x0 = [sb(f"x0_{i}", [P, NP, P]) for i in range(2)]
        xT = sb("dxT", [P, KT, T])
        kT = sb("dkT", [P, KT, TT, P])
        km, qm = sb("dkm", [P, KT, TT, HL, P]), sb("dqm", [P, KT, TT, HL, P])
        qT = sb("dqT", [P, KT, P])
        kb = sb("kb", [P, TT, D])
        vb = sb("vb", [P, TT, D])
        m1, m2 = sb("m1", [P, NP, P]), sb("m2", [P, NP, P])
        lT = sb("lT", [P, NP, P])
        z = sb("z", [P, NP, P])
        x1 = sb("x1", [P, NP, P])
        gw = sb("gw", [P, NP, P])
        sbd = sb("sbd", [P, KT, P])
        uT = sb("uT", [P, TT, KT, P])
        u = sb("u", [P, TT, KT, P])
        wTn = sb("wTn", [P, KT, P])
        oT = sb("oT", [P, TT, KT, P])
        st = sb("st", [P, TT, NS, NPATH, H])
        big = sb("big", [P, NPATH, TT, D])
        stT = sb("stT", [80, T])
        hid = sb("hid", [P, HF // P, T])
        lgT = sb("lgT", [H * NPATH, T])
        lg = sb("lg", [P, TT, H, NPATH])
        sm = sb("sm", [P, 2, TT * H])
        o = sb("o", [P, TT, D])
        osq = sb("osq", [P, TT, D])
        onT = sb("onT", [P, KT, T])
        y = [sb(f"y{i}", [P, TT, D]) for i in range(2)]
        bn, mv = sb("bn", [P, TT, 6]), sb("mv", [P, TT, 2])
        for t in (m1, m2, sbd, *g0, *x0):
            pool.op(G.memset, t[:].rearrange("p a b -> p (a b)"), 0.0)
        for t in (km, qm):
            pool.op(G.memset, t[:], 0.0)
        sl = {}

        def slot(n):
            if n not in sl:
                sl[n] = pg.slot("d_" + n)
            return sl[n]

        for n in range(8):
            slot(f"b{n}")
        for n in ("xT", "kT", "km", "qm", "qT", "kb", "vb", "m1", "m2", "lT", "z", "x1", "gw", "sbd", "uT", "u", "wTn", "oT",
                  "st", "big", "stT", "hid", "lgT", "lg", "sm", "o", "osq", "onT", "bn"):
            slot(n)
        for n in ("tok", "xin", "paths", "g0", "x0", "y"):
            for i in range(2):
                slot(f"{n}{i}")

        def R(*names):
            return [m for n in names for m in slot(n).readers]

        def flat(t):
            return t.rearrange("p a b -> p (a b)")

        with pg.repeat("delta", B // 2) as it:
            for i in range(2):
                b = it * 2 + i
                s1 = bass.ds(b, 1)
                m_tok = pg.dma(f"dtok{i}", tok[i][:].rearrange("p t j d -> p (t j d)"),
                               env.tok_dram[s1].rearrange("b p n -> p (b n)"), after=R(f"tok{i}"))
                m_x = pg.dma(f"dx{i}", xin[i][:], a["x"].rearrange("b (t p) d -> p b t d", p=P)[:, s1]
                             .rearrange("p b t d -> p (b t) d"), after=R(f"xin{i}"))
                for c in range(NCH):
                    q = slice(c * CH, (c + 1) * CH)
                    m_g0 = pg.dma(f"g0{i}", g0[i][q, :, q], env.t_dram[0, q, bass.ds(b * NP, NP), :], after=R(f"g0{i}"))
                    m_x0 = pg.dma(f"x0{i}", x0[i][q, :, q], env.t_dram[1, q, bass.ds(b * NP, NP), :], after=R(f"x0{i}"))
                for f in range(NF):
                    m_fir = pg.dma(f"fir{i}", paths[i][:, f], env.fir_dram[f].rearrange("(b t p) d -> p b t d", p=P, t=TT)
                                   [:, s1].rearrange("p b t d -> p (b t) d"), after=R(f"paths{i}"))
                bt = env.beta[:, s1, :].rearrange("p b (t h) -> p (b t) h", t=TT).unsqueeze(3).broadcast_to([P, TT, H, DH])

                def heads(t):
                    return t.rearrange("p t (h d) -> p t h d", h=H)

                m_kb = dve.op(V.tensor_tensor, heads(kb[:]), heads(tok[i][:, :, 1, :]), bt, ALU.mult,
                              after=[m_tok] + R("kb"))
                m_vb = dve.op(V.tensor_tensor, heads(vb[:]), heads(tok[i][:, :, 2, :]), bt, ALU.mult, after=R("vb"))
                m_v5 = pool.op(G.tensor_copy, paths[i][:, NPATH - 1], tok[i][:, :, 2, :], after=[m_tok] + R(f"paths{i}"))
                for n, (bank, src) in enumerate(((0, xin[i]), (1, None), (2, kb), (3, None))):
                    for c in range(KT):
                        for t in range(TT):
                            in_ = src[:, t, c * P:(c + 1) * P] if src is not None else \
                                tok[i][:, t, 1 if bank == 1 else 0, c * P:(c + 1) * P]
                            m = pe.op(nc.tensor.transpose, ps[:, bank, (c * TT + t) * P:(c * TT + t + 1) * P], in_,
                                      env.ident[:], count=(c, t) == (1, 1),
                                      after=[m_x if bank == 0 else m_kb if bank == 2 else m_tok] + R(f"b{bank}"))
                    if bank == 0:
                        m_xT = act.op(S.copy, flat(xT[:]), ps[:, 0, :], after=[m] + R("xT"))
                        slot("b0").read(m_xT)
                    elif bank == 2:
                        m_kT = act.op(S.copy, kT[:].rearrange("p c t n -> p (c t n)"), ps[:, 2, :], after=[m] + R("kT"))
                        slot("b2").read(m_kT)
                    else:
                        dst, nm = (km, "km") if bank == 1 else (qm, "qm")
                        for h in range(HL):
                            q = slice(h * DH, (h + 1) * DH)
                            m_m = dve.op(V.tensor_copy, dst[q, :, :, h, :].rearrange("p c t n -> p (c t) n"),
                                         ps[q, bank, :].rearrange("p (c n) -> p c n", n=P), after=[m] + R(nm))
                        if bank == 1:
                            m_km = m_m
                            slot("b1").read(m_m)
                        else:
                            m_qm = m_m
                            m_qT = act.op(S.copy, qT[:], ps[:, 3, :].rearrange("p (c t n) -> p c t n", c=KT, t=TT)[:, :, 1, :],
                                          after=[m, m_m] + R("qT"))
                            slot("b3").read(m_m, m_qT)
                for k2, (rhs, m_r, lhs, m_l, bank) in enumerate(((km, m_km, kT, m_kT, 4), (qm, m_qm, None, None, 6))):
                    for c in range(KT):
                        for t in range(TT):
                            n = t * H + c * HL
                            if lhs is not None:
                                m = pe.op(nc.tensor.matmul, ps[:, bank + n // 4, (n % 4) * P:(n % 4 + HL) * P],
                                          kT[:, c, t, :], km[:, c, t, :, :], start=True, stop=True,
                                          after=[m_r, m_l] + R("b4", "b5"), count=(c, t) == (1, 1))
                            else:
                                for h in range(HL):
                                    m = pe.op(nc.tensor.matmul, ps[:, bank + n // 4, (n % 4 + h) * P:(n % 4 + h + 1) * P],
                                              km[:, c, t, h, :], qm[:, c, t, h, :], start=True, stop=True,
                                              after=[m_r, m_km] + R("b6", "b7"), count=(c, t, h) == (1, 1, 1))
                    if k2 == 0:
                        m_A = m
                    else:
                        m_L = m
                slot("kT").read(m_A)
                slot("km").read(m_L)
                slot("qm").read(m_L)
                pa = ps[:, 4:6, :].rearrange("p u (n j) -> p (u n) j", j=P)
                for lo in (0, 2 * CH):
                    m_m1 = act.op(S.activation, m1[lo + CH:lo + 2 * CH, :, lo:lo + CH], pa[lo + CH:lo + 2 * CH, :, lo:lo + CH],
                                  ACT.Copy, scale=-1.0, after=[m_A] + R("m1"))
                m_m2 = act.op(S.activation, m2[2 * CH:P, :, 0:2 * CH], pa[2 * CH:P, :, 0:2 * CH], ACT.Copy, scale=-1.0,
                              after=R("m2"))
                slot("b4").read(m_m2)
                slot("b5").read(m_m2)
                m_lT = dve.op(V.tensor_tensor, lT[:], ps[:, 6:8, :].rearrange("p u (n j) -> p (u n) j", j=P),
                              env.causal[:].unsqueeze(1).broadcast_to([P, NP, P]), ALU.mult, after=[m_L] + R("lT"))
                slot("b6").read(m_lT)
                slot("b7").read(m_lT)

                def each(lhs, rhs, bank, after):
                    for n in range(NP):
                        m = pe.op(nc.tensor.matmul, ps[:, bank + n // 4, (n % 4) * P:(n % 4 + 1) * P], lhs[:, n, :],
                                  rhs[:, n, :], start=True, stop=True, after=after, count=n % 4 == 3)
                        if n == 3:
                            first = m
                    return first, m

                def evac(fn, bank, marks):
                    out = None
                    for u2 in range(2):
                        out = fn(ps[:, bank + u2, :], slice(4 * u2, 4 * u2 + 4), marks[u2])
                        slot(f"b{bank + u2}").read(out)
                    return out

                mm = each(m1, g0[i], 0, [m_m1, m_g0] + R("b0", "b1"))
                m_z = evac(lambda p_, n_, m_: act.op(S.copy, flat(z[:, n_]), p_, after=[m_] + R("z")), 0, mm)
                slot("m1").read(mm[1])
                mm = each(x0[i], z, 2, [m_z, m_x0] + R("b2", "b3"))
                slot(f"x0{i}").read(mm[1])
                slot("z").read(mm[1])
                m_g = evac(lambda p_, n_, m_: dve.op(V.tensor_tensor, flat(gw[:, n_]), flat(g0[i][:, n_]), p_, ALU.add,
                                                     after=[m_] + R("gw")), 2, mm)
                slot(f"g0{i}").read(m_g)
                for n in range(NP):
                    m = pe.op(nc.tensor.transpose, ps[:, 4 + n // 4, (n % 4) * P:(n % 4 + 1) * P], gw[:, n, :], env.ident[:],
                              after=[m_g] + R("b4", "b5"), count=n % 4 == 3)
                    if n == 3:
                        first = m
                m_x1 = evac(lambda p_, n_, m_: act.op(S.copy, flat(x1[:, n_]), p_, after=[m_] + R("x1")), 4, (first, m))
                mm = each(m2, gw, 6, [m_g, m_m2] + R("b6", "b7"))
                slot("m2").read(mm[1])
                m_z = evac(lambda p_, n_, m_: act.op(S.copy, flat(z[:, n_]), p_, after=[m_] + R("z")), 6, mm)
                mm = each(x1, z, 0, [m_z, m_x1] + R("b0", "b1"))
                slot("z").read(mm[1])
                slot("x1").read(mm[1])
                m_g = evac(lambda p_, n_, m_: dve.op(V.tensor_tensor, flat(gw[:, n_]), flat(gw[:, n_]), p_, ALU.add,
                                                     after=[m_]), 0, mm)
                hs = [slice(0, DH), slice(DH, P)]

                def beta_v(t, c, h):
                    n = t * H + c * HL + h
                    return pe.op(nc.tensor.matmul, ps[hs[h], 2, (t * KT + c) * P:(t * KT + c + 1) * P],
                                 vb[:, t, (c * HL + h) * DH:(c * HL + h + 1) * DH], gw[:, n, :], start=True,
                                 stop=(t == 0), after=[m_g, m_vb] + R("b2"), skip_group_check=True, count=h == 1)

                for c in range(KT):
                    for h in range(HL):
                        m_u0 = beta_v(0, c, h)
                for c in range(KT):
                    for h in range(HL):
                        m = pe.op(nc.tensor.matmul, ps[hs[h], 3, c * P:(c + 1) * P],
                                  kb[:, 1, (c * HL + h) * DH:(c * HL + h + 1) * DH], gw[:, H + c * HL + h, :], start=True,
                                  stop=True, after=R("b3"), count=(c, h) == (1, 1))
                slot("kb").read(m)
                m_wT = act.op(S.activation, flat(wTn[:]), ps[:, 3, 0:KT * P], ACT.Copy, scale=-1.0, after=[m] + R("wTn"))
                slot("b3").read(m_wT)
                m_uT = dve.op(V.tensor_copy, flat(uT[:, 0]), ps[:, 2, 0:KT * P], after=[m_u0] + R("uT"))
                for c in range(KT):
                    m = pe.op(nc.tensor.transpose, ps[:, 4, c * P:(c + 1) * P], uT[:, 0, c, :], env.ident[:],
                              after=[m_uT] + R("b4"))
                m_u = dve.op(V.tensor_copy, flat(u[:, 0]), ps[:, 4, 0:KT * P], after=[m] + R("u"))
                slot("b4").read(m_u)
                for c in range(KT):
                    m = pe.op(nc.tensor.matmul, ps[:, 5, c * P:(c + 1) * P], tok[i][:, 0, 1, c * P:(c + 1) * P], u[:, 0, c, :],
                              start=True, stop=True, after=[m_u] + R("b5"))
                slot(f"tok{i}").read(m, m_v5)
                for h in range(HL):
                    m_s = dve.op(V.tensor_copy, sbd[hs[h], :, hs[h]],
                                 ps[hs[h], 5, 0:KT * P].rearrange("p (c n) -> p c n", c=KT)[:, :, hs[h]], after=[m] + R("sbd"))
                slot("b5").read(m_s)
                for c in range(KT):
                    for h in range(HL):
                        beta_v(1, c, h)
                    m = pe.op(nc.tensor.matmul, ps[:, 2, (KT + c) * P:(KT + c + 1) * P], sbd[:, c, :], wTn[:, c, :],
                              start=False, stop=True, after=[m_s, m_wT], skip_group_check=True)
                slot("wTn").read(m)
                slot("vb").read(m)
                slot("gw").read(m)
                m_uT = dve.op(V.tensor_copy, flat(uT[:, 1]), ps[:, 2, KT * P:2 * KT * P], after=[m])
                slot("b2").read(m_uT)
                for c in range(KT):
                    m = pe.op(nc.tensor.transpose, ps[:, 4, c * P:(c + 1) * P], uT[:, 1, c, :], env.ident[:],
                              after=[m_uT] + R("b4"))
                slot("uT").read(m)
                m_u = dve.op(V.tensor_copy, flat(u[:, 1]), ps[:, 4, 0:KT * P], after=[m])
                slot("b4").read(m_u)
                for t in range(TT):
                    for c in range(KT):
                        if t:
                            pe.op(nc.tensor.matmul, ps[:, 6, (t * KT + c) * P:(t * KT + c + 1) * P], sbd[:, c, :], qT[:, c, :],
                                  start=True, stop=False, after=[m_u, m_qT, m_lT] + R("b6"), count=False, skip_group_check=True)
                        for h in range(HL):
                            n = t * H + c * HL + h
                            m = pe.op(nc.tensor.matmul, ps[hs[h], 6, (t * KT + c) * P:(t * KT + c + 1) * P],
                                      u[:, t, c, hs[h]], lT[:, n, :], start=(t == 0), stop=True, after=[m_u, m_lT] + R("b6"),
                                      skip_group_check=True, count=(t, c, h) == (1, 1, 1))
                for nm in ("u", "lT", "qT", "sbd"):
                    slot(nm).read(m)
                m_oT = act.op(S.copy, oT[:].rearrange("p t c n -> p (t c n)"), ps[:, 6, :], after=[m] + R("oT"))
                slot("b6").read(m_oT)
                for t in range(TT):
                    for c in range(KT):
                        m = pe.op(nc.tensor.transpose, ps[:, 7, (t * KT + c) * P:(t * KT + c + 1) * P], oT[:, t, c, :],
                                  env.ident[:], after=[m_oT] + R("b7"), count=(t, c) == (1, 1))
                slot("oT").read(m)
                m_dl = act.op(S.copy, paths[i][:, NF].rearrange("p t d -> p (t d)"), ps[:, 7, :], after=[m] + R(f"paths{i}"))
                slot("b7").read(m_dl)

                pf = paths[i][:].rearrange("p n t (h d) -> p (n t h) d", h=H)

                def stat(s):
                    return st[:, :, s].rearrange("p t n h -> p n t h")

                m_sq = act.op(S.activation, big[:].rearrange("p n t d -> p (n t d)"), paths[i][:].rearrange("p n t d -> p (n t d)"),
                              ACT.Square, after=[m_fir, m_v5, m_dl] + R("big"))
                dve.op(V.tensor_reduce, stat(0), pf, AX.X, ALU.add, after=[m_fir, m_v5, m_dl] + R("st"))
                dve.op(V.tensor_reduce, stat(2), pf, AX.X, ALU.add, apply_absolute_value=True)
                m_st = dve.op(V.tensor_reduce, stat(1), big[:].rearrange("p n t (h d) -> p (n t h) d", h=H), AX.X, ALU.add,
                              after=[m_sq])
                slot("big").read(m_st)
                m_st = pool.op(G.tensor_tensor, st[:, :, 3].rearrange("p t n h -> p t (n h)"), st[:, :, 1].rearrange("p t n h -> p t (n h)"),
                               env.exponent[:, 1, :].rearrange("p (t n) -> p t n", t=TT), ALU.pow, after=[m_st])
                for t in range(TT):
                    m = pe.op(nc.tensor.transpose, ps[0:80, 0, t * P:(t + 1) * P], st[:, t].rearrange("p s n h -> p (s n h)"), env.ident[:],
                              after=[m_st] + R("b0"), count=t == 1)
                slot("st").read(m)
                m_stT = act.op(S.copy, stT[:], ps[0:80, 0, 0:T], after=[m] + R("stT"))
                slot("b0").read(m_stT)
                for c in range(HF // P):
                    for k in range(KT + 1):
                        l_ = w1x[:, k, c * P:(c + 1) * P] if k < KT else env.w1s[:, c * P:(c + 1) * P]
                        r_ = xT[:, k, :] if k < KT else stT[:]
                        m = pe.op(nc.tensor.matmul, ps[:, 1 + c // 2, (c % 2) * T:(c % 2 + 1) * T], l_, r_, start=(k == 0),
                                  stop=(k == KT), after=[m_xT] + ([m_stT] if k == KT else []) + R("b1", "b2"), count=k == KT)
                    if c % 2:
                        for e in (c - 1, c):
                            m_h = act.op(S.activation, hid[:, e, :], ps[:, 1 + e // 2, (e % 2) * T:(e % 2 + 1) * T], ACT.Gelu,
                                         bias=gb1[:, e:e + 1], after=[m] + R("hid"))
                        slot(f"b{1 + c // 2}").read(m_h)
                slot("xT").read(m)
                slot("stT").read(m)
                for c in range(HF // P):
                    m = pe.op(nc.tensor.matmul, ps[0:H * NPATH, 3, 0:T], gw2[:, c, :], hid[:, c, :], start=(c == 0),
                              stop=(c == HF // P - 1), after=[m_h] + R("b3"), count=c == 3)
                slot("hid").read(m)
                m = act.op(S.copy, lgT[:], ps[0:H * NPATH, 3, 0:T], after=[m] + R("lgT"))
                slot("b3").read(m)
                for t in range(TT):
                    m2_ = pe.op(nc.tensor.transpose, ps[:, 4, t * H * NPATH:(t + 1) * H * NPATH], lgT[:, t * P:(t + 1) * P],
                                env.ident[0:H * NPATH, 0:H * NPATH], split=True, after=[m] + R("b4"), count=t == 1)
                slot("lgT").read(m2_)
                lf = lg[:].rearrange("p t h n -> p t (h n)")
                m = dve.op(V.tensor_tensor, lf, ps[:, 4, 0:TT * H * NPATH].rearrange("p (t n) -> p t n", t=TT),
                           gb2[:].unsqueeze(1).broadcast_to([P, TT, H * NPATH]), ALU.add, after=[m2_] + R("lg"))
                slot("b4").read(m)
                lh = lg[:].rearrange("p t h n -> p (t h) n")

                def per_head(t):
                    return t.unsqueeze(1).unsqueeze(3).broadcast_to([P, TT, H, NPATH])

                dve.op(V.tensor_tensor, lg[:], lg[:], per_head(itau[:]), ALU.mult)
                dve.op(V.tensor_reduce, sm[:, 0, :], lh, AX.X, ALU.max, after=R("sm"))
                m = dve.op(V.tensor_tensor, lh, lh, sm[:, 0, :].unsqueeze(2).broadcast_to([P, NP, NPATH]), ALU.subtract)
                lw = lg[:].rearrange("p t h n -> p (t h n)")
                m = pool.op(G.tensor_tensor, lw, env.exponent[:, 2, :], lw, ALU.pow, after=[m])
                dve.op(V.tensor_reduce, sm[:, 1, :], lh, AX.X, ALU.add, after=[m])
                dve.op(V.reciprocal, sm[:, 1, :], sm[:, 1, :])
                dve.op(V.tensor_tensor, lh, lh, sm[:, 1, :].unsqueeze(2).broadcast_to([P, NP, NPATH]), ALU.mult)
                dve.op(V.tensor_tensor, lg[:], lg[:], per_head(keep[:]), ALU.mult)
                m_pr = dve.op(V.tensor_tensor, lg[:], lg[:], eps[:].unsqueeze(1).broadcast_to([P, TT, H, NPATH]), ALU.add)
                def weighed(E, eng, n, extra=()):
                    return E.op(eng.tensor_tensor, big[:, n].rearrange("p t (h d) -> p (t h) d", h=H),
                                paths[i][:, n].rearrange("p t (h d) -> p (t h) d", h=H),
                                lh[:, :, n:n + 1].broadcast_to([P, NP, DH]), ALU.mult, after=[m_pr, *extra])

                def path(n):
                    return big[:, n].rearrange("p t d -> p (t d)")

                weighed(pool, G, 3)
                weighed(pool, G, 4)
                m_p = pool.op(G.tensor_tensor, path(3), path(3), path(4), ALU.add)
                for n in range(NF):
                    m = weighed(dve, V, n)
                slot("lg").read(m, m_p)
                slot(f"paths{i}").read(m, m_p)
                dve.op(V.tensor_tensor, path(0), path(0), path(1), ALU.add)
                dve.op(V.tensor_tensor, path(0), path(0), path(2), ALU.add)
                m_o = dve.op(V.tensor_tensor, o[:].rearrange("p t d -> p (t d)"), path(0), path(3), ALU.add,
                             after=[m_p] + R("o"))
                slot("big").read(m_o)
                m = act.op(S.activation, flat(osq[:]), flat(o[:]), ACT.Square, after=[m_o] + R("osq"))
                m = dve.op(V.tensor_reduce, sm[:, 0, :], osq[:].rearrange("p t (h d) -> p (t h) d", h=H), AX.X, ALU.add, after=[m])
                slot("osq").read(m)
                m = pool.op(G.tensor_scalar, sm[:, 0, :], sm[:, 0, :], 1.0 / DH, 1e-5, ALU.mult, ALU.add, after=[m])
                m = pool.op(G.tensor_tensor, sm[:, 0, :], sm[:, 0, :], env.exponent[:, 0, 0:NP], ALU.pow)
                of = o[:].rearrange("p t (h d) -> p (t h) d", h=H)
                m_on = dve.op(V.tensor_tensor, of, of, sm[:, 0, :].unsqueeze(2).broadcast_to([P, NP, DH]), ALU.mult, after=[m])
                slot("sm").read(m_on)
                for c in range(KT):
                    for t in range(TT):
                        m = pe.op(nc.tensor.transpose, ps[:, 5, (c * TT + t) * P:(c * TT + t + 1) * P], o[:, t, c * P:(c + 1) * P],
                                  env.ident[:], after=[m_on] + R("b5"), count=(c, t) == (1, 1))
                slot("o").read(m)
                m_onT = act.op(S.copy, flat(onT[:]), ps[:, 5, :], after=[m] + R("onT"))
                slot("b5").read(m_onT)
                for t in range(TT):
                    for k in range(KT):
                        m = pe.op(nc.tensor.matmul, ps[:, 7, t * D:(t + 1) * D], onT[:, k, t * P:(t + 1) * P], wo[:, k, :],
                                  start=(k == 0), stop=(k == 1), after=[m_onT] + R("b7"), count=(t, k) == (1, 1))
                slot("onT").read(m)
                m = dve.op(V.tensor_tensor, flat(y[i][:]), ps[:, 7, :], flat(xin[i][:]), ALU.add, after=[m, m_x] + R(f"y{i}"))
                slot("b7").read(m)
                slot(f"xin{i}").read(m)
                m = norm_rows(pg, env, y[i], bn, mv, [m] + R("bn"))
                slot("bn").read(m)
                m = pg.dma(f"x1_{i}", env.x1_dram.rearrange("b (t p) d -> p b t d", p=P)[:, s1].rearrange("p b t d -> p (b t) d"),
                           y[i][:], after=[m])
                slot(f"y{i}").read(m)
        pg.meet()


def norm_rows(pg, env, y, bn, mv, after):
    nc, dve, pool = pg.nc, pg.dve, pg.pool
    for t in range(TT):
        dve.op(nc.vector.bn_stats, bn[:, t, :], y[:, t, :], after=after)
        dve.op(nc.vector.bn_aggr, mv[:, t, :], bn[:, t, :], split=True)
    m = pool.op(nc.gpsimd.tensor_scalar, mv[:, :, 1], mv[:, :, 1], 1.0, 1e-5, ALU.mult, ALU.add, after=[dve.last])
    m = pool.op(nc.gpsimd.tensor_tensor, mv[:, :, 1], mv[:, :, 1], env.exponent[:, 0, 0:TT], ALU.pow)
    for t in range(TT):
        m = dve.op(nc.vector.tensor_scalar, y[:, t, :], y[:, t, :], mv[:, t, 0:1], mv[:, t, 1:2], ALU.subtract, ALU.mult, after=[m])
    return m


def phase_cross(pg, a, env):
    nc, pe, act, dve, pool = pg.nc, pg.pe, pg.act, pg.dve, pg.pool
    V, S, G = nc.vector, nc.scalar, nc.gpsimd
    HT = P // XD
    with ExitStack() as mem:
        def sb(n, shape, dt=F32):
            return mem.enter_context(nc.sbuf_tensor(n, shape, dt))
        ps = env.ps
        Wx = {n: load_weight(pg, env, sb, "x" + n, a[n], D, "w_cross")[0] for n in ("q_w", "k_w", "v_w", "o_w")}
        gate_w, _ = load_weight(pg, env, sb, "gate_w", a["gate_w"], NE, "w_cross")
        bq, bk = sb("bq", [P, KT]), sb("bk", [P, KT])
        pg.dma("w_cross", bq[:], a["q_b"].rearrange("(k p) -> p k", p=P), allow_slow_non_contiguous=True)
        pg.dma("w_cross", bk[:], a["k_b"].rearrange("(k p) -> p k", p=P), allow_slow_non_contiguous=True)
        bv, bo = sb("bv", [P, D]), sb("bo", [P, D])
        pg.dma("w_cross", bv[:], a["v_b"].partition_broadcast(P))
        pg.dma("w_cross", bo[:], a["o_b"].partition_broadcast(P))
        xin = [sb(f"cx{i}", [P, TT, D]) for i in range(2)]
        cin = [sb(f"cc{i}", [P, TT, D]) for i in range(2)]
        xT, cT = sb("cxT", [P, KT, T]), sb("ccT", [P, KT, T])
        qT, kT = sb("cqT", [P, KT, T]), sb("ckT", [P, KT, T])
        km = [sb(f"ckm{i}", [P, XH, T]) for i in range(2)]
        vv = [sb(f"vv{i}", [P, TT, XH, CH]) for i in range(2)]
        pr = [sb(f"pr{i}", [P, TT, 2, T]) for i in range(3)]
        pT = [sb(f"pT{i}", [P, 2, TT, T]) for i in range(2)]
        mx = sb("mx", [P, XH, TT])
        oT = sb("coT", [P, XH // 4, T])
        rs = sb("rs", [P, TT, XH])
        o = sb("co", [P, TT, D])
        onT = sb("conT", [P, KT, T])
        y = [sb(f"cy{i}", [P, TT, D]) for i in range(2)]
        bn, mv = sb("cbn", [P, TT, 6]), sb("cmv", [P, TT, 2])
        lgT = sb("clgT", [NE, T])
        lg = sb("clg", [P, TT, NE])
        top = sb("top", [P, TT, 8])
        ti = sb("ti", [P, TT, 8], U32)
        tif = sb("tif", [P, TT, 8])
        wsel = sb("wsel", [P, TT, 2])
        tmp = sb("ctmp", [P, TT, NE])
        for i in range(2):
            pool.op(G.memset, vv[i][:], 1.0)
        sl = {}

        def slot(n):
            if n not in sl:
                sl[n] = pg.slot("c_" + n)
            return sl[n]

        for n in range(8):
            slot(f"b{n}")
        for n in ("xT", "cT", "qT", "kT", "mx", "oT", "rs", "o", "onT", "bn", "lgT", "lg", "top", "tmp"):
            slot(n)
        for n in ("xin", "cin", "km", "vv", "pr", "pT", "y"):
            for i in range(3):
                slot(f"{n}{i}")

        def R(*names):
            return [m for n in names for m in slot(n).readers]

        def flat(t):
            return t.rearrange("p a b -> p (a b)")

        with pg.repeat("cross", B // 2) as it:
            for i in range(2):
                b = it * 2 + i
                s1 = bass.ds(b, 1)
                m_x = pg.dma(f"cx{i}", xin[i][:], env.x1_dram.rearrange("b (t p) d -> p b t d", p=P)[:, s1]
                             .rearrange("p b t d -> p (b t) d"), after=R(f"xin{i}"))
                m_c = pg.dma(f"cc{i}", cin[i][:], a["ctx"].rearrange("b (t p) d -> p b t d", p=P)[:, s1]
                             .rearrange("p b t d -> p (b t) d"), after=R(f"cin{i}"))
                for bank, src, dst, nm, m_in in ((0, cin[i], cT, "cT", m_c), (1, xin[i], xT, "xT", m_x)):
                    for c in range(KT):
                        for t in range(TT):
                            m = pe.op(nc.tensor.transpose, ps[:, bank, (c * TT + t) * P:(c * TT + t + 1) * P],
                                      src[:, t, c * P:(c + 1) * P], env.ident[:], after=[m_in] + R(f"b{bank}"),
                                      count=(c, t) == (1, 1))
                    if bank == 0:
                        slot(f"cin{i}").read(m)
                    m_e = act.op(S.copy, flat(dst[:]), ps[:, bank, :], after=[m] + R(nm))
                    slot(f"b{bank}").read(m_e)
                    if bank == 0:
                        m_cT = m_e
                    else:
                        m_xT = m_e
                for bank, w, src, dst, nm, bias, m_in in ((2, "k_w", cT, kT, "kT", bk, m_cT), (3, "q_w", xT, qT, "qT", bq, m_xT)):
                    for c in range(KT):
                        for k in range(KT):
                            m = pe.op(nc.tensor.matmul, ps[:, bank, c * T:(c + 1) * T], Wx[w][:, k, c * P:(c + 1) * P],
                                      src[:, k, :], start=(k == 0), stop=(k == 1), after=[m_in] + R(f"b{bank}"), count=k == 1)
                    for c in range(KT):
                        m_e = dve.op(V.tensor_scalar, dst[:, c, :], ps[:, bank, c * T:(c + 1) * T], bias[:, c:c + 1], None,
                                     ALU.add, after=[m] + R(nm))
                    slot(f"b{bank}").read(m_e)
                    if bank == 2:
                        m_kT = m_e
                    else:
                        m_qT = m_e
                slot("xT").read(m)
                for t in range(TT):
                    for k in range(KT):
                        m = pe.op(nc.tensor.matmul, ps[:, 0, t * D:(t + 1) * D], cT[:, k, t * P:(t + 1) * P],
                                  Wx["v_w"][:, k, :], start=(k == 0), stop=(k == 1), after=[m_cT] + R("b0"), count=(t, k) == (1, 1))
                slot("cT").read(m)
                for t in range(TT):
                    m_v = dve.op(V.tensor_tensor, vv[i][:, t, :, 0:XD], ps[:, 0, t * D:(t + 1) * D].rearrange("p (h d) -> p h d", h=XH),
                                 bv[:].rearrange("p (h d) -> p h d", h=XH), ALU.add, after=[m] + R(f"vv{i}"))
                slot("b0").read(m_v)
                m_km = []
                for h in range(XH):
                    m = pool.op(G.tensor_scalar, km[i][:, h, :], kT[:, h // HT, :], env.headmask[:, h % HT:h % HT + 1], 1.0,
                                ALU.mult, ALU.mult, after=[m_kT] + R(f"km{i}"))
                    m_km.append(m)
                slot("kT").read(m)
                NPAIR = XH // 2
                scored, expd, turned = {}, {}, {}

                def scores(g):
                    for t in range(TT):
                        bank = 2 + 2 * (g % 2) + t
                        m = pe.op(nc.tensor.matmul, ps[:, bank, :], qT[:, (2 * g) // HT, t * P:(t + 1) * P],
                                  flat(km[i][:, 2 * g:2 * g + 2, :]), start=True, stop=True,
                                  after=[m_qT, m_km[2 * g + 1]] + R(f"b{bank}"))
                    scored[g] = m

                def softmax(g):
                    bank = 2 + 2 * (g % 2)
                    m_mx = dve.op(V.tensor_reduce, mx[:, 2 * g:2 * g + 2, :].rearrange("p h t -> p t h"),
                                  ps[:, bank:bank + 2, :].rearrange("p t (h k) -> p t h k", h=2), AX.X, ALU.max,
                                  after=[scored[g]] + R("mx"))
                    m_mx = dve.op(V.tensor_scalar, mx[:, 2 * g:2 * g + 2, :], mx[:, 2 * g:2 * g + 2, :], -float(XD) ** -0.5,
                                  None, ALU.mult)
                    for t in range(TT):
                        for h in range(2):
                            m = act.op(S.activation, pr[g % 3][:, t, h, :], ps[:, bank + t, h * T:(h + 1) * T], ACT.Exp,
                                       bias=mx[:, 2 * g + h, t:t + 1], scale=float(XD) ** -0.5,
                                       after=[m_mx] + R(f"pr{g % 3}"))
                        slot(f"b{bank + t}").read(m)
                    expd[g] = m

                def turn(g):
                    for h in range(2):
                        for kt_ in range(TT):
                            for t in range(TT):
                                m = pe.op(nc.tensor.transpose, ps[:, h, (kt_ * TT + t) * P:(kt_ * TT + t + 1) * P],
                                          pr[g % 3][:, t, h, kt_ * P:(kt_ + 1) * P], env.ident[:],
                                          after=[expd[g]] + R(f"b{h}"), count=(kt_, t) == (1, 1))
                        E, fn = (act, S.copy) if h == 0 and g % 2 else (dve, V.tensor_copy)
                        m_e = E.op(fn, pT[g % 2][:, h].rearrange("p k t -> p (k t)"), ps[:, h, :], after=[m] + R(f"pT{g % 2}"))
                        slot(f"b{h}").read(m_e)
                        turned[g, h] = m_e
                    slot(f"pr{g % 3}").read(m)

                def values(g):
                    for h in range(2):
                        head = 2 * g + h
                        q = (head % 4) * CH
                        for k in range(TT):
                            m = pe.op(nc.tensor.matmul, ps[q:q + CH, 6 + head // 8, (head // 4 % 2) * T:(head // 4 % 2 + 1) * T],
                                      vv[i][:, k, head, :], pT[g % 2][:, h, k, :], start=(k == 0), stop=(k == 1),
                                      after=[turned[g, 0], turned[g, 1], m_v] + R("b6", "b7"), skip_group_check=True)
                    slot(f"pT{g % 2}").read(m)
                    return m

                for g in range(NPAIR + 2):
                    if g < NPAIR:
                        scores(g)
                        softmax(g)
                    if 1 <= g <= NPAIR:
                        turn(g - 1)
                    if g >= 2:
                        m = values(g - 2)
                slot("mx").read(expd[NPAIR - 1])
                slot(f"km{i}").read(scored[NPAIR - 1])
                slot("qT").read(scored[NPAIR - 1])
                slot(f"vv{i}").read(m)
                m_oT = act.op(S.copy, oT[:].rearrange("p g t -> p (g t)"), ps[:, 6:8, :].rearrange("p u n -> p (u n)"),
                              after=[m] + R("oT"))
                slot("b6").read(m_oT)
                slot("b7").read(m_oT)
                for t in range(TT):
                    for g in range(XH // 4):
                        m = pe.op(nc.tensor.transpose, ps[:, t, g * P:(g + 1) * P], oT[:, g, t * P:(t + 1) * P], env.ident[:],
                                  after=[m_oT] + R(f"b{t}"), count=(t, g) == (1, 3))
                slot("oT").read(m)
                for t in range(TT):
                    src = ps[:, t, :].rearrange("p (h d) -> p h d", h=XH)
                    dve.op(V.reciprocal, rs[:, t, :], src[:, :, XD], after=[m])
                    m_o = dve.op(V.tensor_tensor, o[:, t, :].rearrange("p (h d) -> p h d", h=XH), src[:, :, 0:XD],
                                 rs[:, t, :].unsqueeze(2).broadcast_to([P, XH, XD]), ALU.mult, after=R("o"))
                    slot(f"b{t}").read(m_o)
                for c in range(KT):
                    for t in range(TT):
                        m = pe.op(nc.tensor.transpose, ps[:, 2, (c * TT + t) * P:(c * TT + t + 1) * P], o[:, t, c * P:(c + 1) * P],
                                  env.ident[:], after=[m_o] + R("b2"), count=(c, t) == (1, 1))
                slot("o").read(m)
                m_onT = act.op(S.copy, flat(onT[:]), ps[:, 2, :], after=[m] + R("onT"))
                slot("b2").read(m_onT)
                for t in range(TT):
                    for k in range(KT):
                        m = pe.op(nc.tensor.matmul, ps[:, 3, t * D:(t + 1) * D], onT[:, k, t * P:(t + 1) * P], Wx["o_w"][:, k, :],
                                  start=(k == 0), stop=(k == 1), after=[m_onT] + R("b3"), count=(t, k) == (1, 1))
                slot("onT").read(m)
                m_y = dve.op(V.tensor_tensor, flat(y[i][:]), ps[:, 3, :], flat(xin[i][:]), ALU.add, after=[m] + R(f"y{i}"))
                slot("b3").read(m_y)
                slot(f"xin{i}").read(m_y)
                dve.op(V.tensor_tensor, y[i][:], y[i][:], bo[:].unsqueeze(1).broadcast_to([P, TT, D]), ALU.add)
                m_y = norm_rows(pg, env, y[i], bn, mv, [])
                m_y2 = pool.op(G.tensor_copy, env.x2[:, bass.ds(b * TT, TT), :], y[i][:], after=[m_y])
                for c in range(KT):
                    for t in range(TT):
                        m = pe.op(nc.tensor.transpose, ps[:, 4, (c * TT + t) * P:(c * TT + t + 1) * P], y[i][:, t, c * P:(c + 1) * P],
                                  env.ident[:], after=[m_y] + R("b4"), count=(c, t) == (1, 1))
                slot(f"y{i}").read(m, m_y2)
                m_2T = act.op(S.copy, flat(onT[:]), ps[:, 4, :], after=[m] + R("onT"))
                m = act.op(S.copy, env.x2T[:, :, bass.ds(b * T, T)], ps[:, 4, :].rearrange("p (c t) -> p c t", c=KT))
                slot("b4").read(m)
                for k in range(KT):
                    m = pe.op(nc.tensor.matmul, ps[0:NE, 5, 0:T], gate_w[:, k, :], onT[:, k, :], start=(k == 0), stop=(k == 1),
                              after=[m_2T] + R("b5"), count=k == 1)
                slot("onT").read(m)
                m = act.op(S.copy, lgT[:], ps[0:NE, 5, 0:T], after=[m] + R("lgT"))
                for t in range(TT):
                    m2_ = pe.op(nc.tensor.transpose, ps[:, 5, T + t * NE:T + (t + 1) * NE], lgT[:, t * P:(t + 1) * P],
                                env.ident[0:NE, 0:NE], split=True, after=[m], count=t == 1)
                slot("lgT").read(m2_)
                m = dve.op(V.tensor_copy, lg[:], ps[:, 5, T:T + TT * NE].rearrange("p (t n) -> p t n", t=TT), after=[m2_] + R("lg"))
                slot("b5").read(m)
                for t in range(TT):
                    dve.op(V.max, top[:, t, :], lg[:, t, :], after=R("top"), split=True)
                    dve.op(V.max_index, ti[:, t, :], top[:, t, :], lg[:, t, :], split=True)
                dve.op(V.tensor_copy, tif[:], ti[:])
                m = dve.op(V.tensor_tensor, wsel[:, :, 1:2], top[:, :, 1:2], top[:, :, 0:1], ALU.subtract)
                m = act.op(S.activation, wsel[:, :, 1:2], wsel[:, :, 1:2], ACT.Exp, after=[m])
                m = dve.op(V.tensor_scalar, wsel[:, :, 0:1], wsel[:, :, 1:2], 1.0, None, ALU.add, after=[m])
                dve.op(V.reciprocal, wsel[:, :, 0:1], wsel[:, :, 0:1])
                dve.op(V.tensor_tensor, wsel[:, :, 1:2], wsel[:, :, 1:2], wsel[:, :, 0:1], ALU.mult)
                for t in range(TT):
                    for k in range(2):
                        m = dve.op(V.tensor_scalar, tmp[:, k, :] if k else env.wte[:, bass.ds(b * TT + t, 1), :].rearrange("p a b -> p (a b)"),
                                   env.expert_no[:], tif[:, t, k:k + 1], wsel[:, t, k:k + 1], ALU.is_equal, ALU.mult)
                    w_ = env.wte[:, bass.ds(b * TT + t, 1), :].rearrange("p a b -> p (a b)")
                    m = dve.op(V.tensor_tensor, w_, w_, tmp[:, 1, :], ALU.add)
        pg.meet()


def phase_experts(pg, a, env):
    nc, pe, act, dve, pool = pg.nc, pg.pe, pg.act, pg.dve, pg.pool
    V, S, G = nc.vector, nc.scalar, nc.gpsimd
    with ExitStack() as mem:
        def sb(n, shape, dt=F32):
            return mem.enter_context(nc.sbuf_tensor(n, shape, dt))
        ps = env.ps
        wg = [sb(f"wg{i}", [P, KT, FF]) for i in range(2)]
        wu = [sb(f"wu{i}", [P, KT, FF]) for i in range(2)]
        wd = [sb(f"wd{i}", [P, len(FT), D]) for i in range(2)]
        sg = [sb(f"sg{i}", [P, TG]) for i in range(2)]
        hT = [sb(f"hT{i}", [P, len(FT), TG]) for i in range(2)]
        acc = env.x2
        sl = {}

        def slot(n):
            if n not in sl:
                sl[n] = pg.slot("e_" + n)
            return sl[n]

        for n in range(8):
            slot(f"b{n}")
        for n in ("wg", "wd", "sg", "hT"):
            for i in range(2):
                slot(f"{n}{i}")

        def R(*names):
            return [m for n in names for m in slot(n).readers]

        def load(i, g, u, d):
            pg.dma(f"wg{i}", wg[i][:], g, after=R(f"wg{i}"))
            m = pg.dma(f"wg{i}", wu[i][:], u)
            nfull = 2 * P
            pg.dma(f"wd{i}", wd[i][:, 0:2], d[0:nfull].rearrange("(k p) n -> p k n", p=P), after=R(f"wd{i}"))
            m2 = pg.dma(f"wd{i}", wd[i][0:FF - nfull, 2], d[nfull:FF])
            return m, m2

        def expert(i, m_w, m_d, weight):
            def up(tg, n):
                f0, fn = FT[n]
                par = n % 2
                for bank, w in ((0, wg[i]), (1, wu[i])):
                    for k in range(KT):
                        m = pe.op(nc.tensor.matmul, ps[0:fn, 2 * par + bank, :], w[:, k, f0:f0 + fn],
                                  env.x2T[:, k, tg * TG:(tg + 1) * TG], start=(k == 0), stop=(k == 1),
                                  after=[m_w] + R(f"b{2 * par + bank}"), count=k == 1)
                    if bank == 0:
                        m_s = act.op(S.activation, sg[par][0:fn, :], ps[0:fn, 2 * par, :], ACT.Silu, after=[m] + R(f"sg{par}"))
                        slot(f"b{2 * par}").read(m_s)
                m_h = dve.op(V.tensor_tensor, hT[tg % 2][0:fn, n, :], sg[par][0:fn, :], ps[0:fn, 2 * par + 1, :], ALU.mult,
                             after=[m, m_s] + R(f"hT{tg % 2}"))
                slot(f"b{2 * par + 1}").read(m_h)
                slot(f"sg{par}").read(m_h)
                return m, m_h

            def down(tg, half, m_h):
                bank = 4 + 2 * (tg % 2) + half
                for t in range(2):
                    tile = half * 2 + t
                    for n, (f0, fn) in enumerate(FT):
                        m = pe.op(nc.tensor.matmul, ps[:, bank, t * D:(t + 1) * D], hT[tg % 2][0:fn, n, tile * P:(tile + 1) * P],
                                  wd[i][0:fn, n, :], start=(n == 0), stop=(n == 2), after=[m_h, m_d] + R(f"b{bank}"),
                                  count=(t, n) == (1, 2))
                for t in range(2):
                    tile = tg * (TG // P) + half * 2 + t
                    src, dst = ps[:, bank, t * D:(t + 1) * D], acc[:, tile, :]
                    if weight is None:
                        m2 = dve.op(V.tensor_tensor, dst, src, dst, ALU.add, after=[m])
                    else:
                        m2 = dve.op(V.scalar_tensor_tensor, out=dst, in0=src, scalar=weight(tile), in1=dst, op0=ALU.mult,
                                    op1=ALU.add, after=[m])
                slot(f"b{bank}").read(m2)
                return m

            NG = NTOK // TG
            marks = {}
            for tg in range(NG + 1):
                for n in range(len(FT)):
                    if tg < NG:
                        m_up, marks[tg] = up(tg, n)
                    if tg > 0 and n < 2:
                        m_dn = down(tg - 1, n, marks[tg - 1])
                if tg > 0:
                    slot(f"hT{(tg - 1) % 2}").read(m_dn)
                if tg == NG - 1:
                    slot(f"wg{i}").read(m_up)
            slot(f"wd{i}").read(m_dn)

        def split(t):
            return t.rearrange("e (k p) n -> p e k n", p=P)

        wcol = [sb(f"wcol{i}", [P, NTOK // P]) for i in range(2)]
        for i in range(2):
            slot(f"wcol{i}")
        with pg.repeat("experts", NE // 2) as it:
            for i in range(2):
                e = it * 2 + i
                s1 = bass.ds(e, 1)
                ms = load(i, split(a["exp_gate"])[:, s1].rearrange("p e k n -> p (e k) n"),
                          split(a["exp_up"])[:, s1].rearrange("p e k n -> p (e k) n"),
                          a["exp_down"][s1].rearrange("e f n -> (e f) n"))
                dve.op(V.tensor_copy, wcol[i][:], env.wte[:, :, s1].rearrange("p t e -> p (t e)"))
                expert(i, *ms, lambda tile: wcol[i][:, tile:tile + 1])
        for i in range(NSH):
            ms = load(i, split(a["sh_gate"])[:, i], split(a["sh_up"])[:, i], a["sh_down"][i])
            expert(i, *ms, None)
        bn, mv = sb("ebn", [P, TT, 6]), sb("emv", [P, TT, 2])
        out = a["out"].rearrange("b (t p) d -> p b t d", p=P)
        with pg.repeat("finish", B // 2) as it:
            for i in range(2):
                b = it * 2 + i
                yb = sg[i][:].rearrange("p (t d) -> p t d", t=TT)
                m = dve.op(V.tensor_copy, yb, env.x2[:, bass.ds(b * TT, TT), :], after=R(f"sg{i}"))
                m = norm_rows(pg, env, yb, bn, mv, [])
                m = pg.dma(f"out{i}", out[:, bass.ds(b, 1)].rearrange("p b t d -> p (b t) d"), yb, after=[m])
                slot(f"sg{i}").read(m)
        pg.meet()


def decoder_program(nc, a, plan):
    with ExitStack() as ctx:
        pg = Program(nc, ctx, plan)

        class Env:
            pass

        env = Env()
        env.sb = lambda n, shape, dt=F32: ctx.enter_context(nc.sbuf_tensor(n, shape, dt))
        env.ps = ctx.enter_context(nc.psum_tensor("ps", [P, 8, 512], F32))
        env.tok_dram = nc.dram_tensor("tok_dram", [B, P, TT * 3 * D], F32).ap()
        env.a_dram = nc.dram_tensor("a_dram", [P, B, NP * CH], F32).ap()
        env.t_dram = nc.dram_tensor("t_dram", [2, P, B * NP, CH], F32).ap()
        env.fir_dram = nc.dram_tensor("fir_dram", [NF, NTOK, D], F32).ap()
        env.x1_dram = nc.dram_tensor("x1_dram", [B, T, D], F32).ap()
        env.beta = env.sb("beta", [P, B, NP])
        env.w1s = env.sb("w1s", [80, HF])
        make_constants(pg, a, env)
        phase_project(pg, a, env)
        phase_invert_and_fir(pg, a, env)
        phase_delta_and_gate(pg, a, env)
        env.x2 = env.sb("x2", [P, NTOK // P, D])
        env.x2T = env.sb("x2T", [P, KT, NTOK])
        env.wte = env.sb("wte", [P, NTOK // P, NE])
        phase_cross(pg, a, env)
        phase_experts(pg, a, env)
        return pg.new_plan


_NAMES = {"x": "x", "ctx": "ctx_1024"}
_NAMES |= {n: "L0_attn_" + n for n in ("Wq", "Wk", "Wv", "conv_q", "conv_k", "conv_v", "Wb", "gW1", "gb1", "gW2", "gb2",
                                       "log_tau", "eps_logit", "norm_w", "Wo")}
_NAMES |= {f"fir{i}": "L0_attn_fir_" + n for i, n in enumerate("sml")}
_NAMES |= {n: "L0_xattn_" + n for n in ("q_w", "q_b", "k_w", "k_b", "v_w", "v_b", "o_w", "o_b")}
_NAMES |= {n: "L0_ffn_" + n for n in ("gate_w", "exp_gate", "exp_up", "exp_down", "sh_gate", "sh_up", "sh_down")}


def kernel(**inputs):
    import numpy as np
    import concourse.bacc as bacc
    from concourse.bass_utils import run_bass_kernel_spmd

    arrays = {"in_" + n: np.ascontiguousarray(inputs[full]) for n, full in _NAMES.items()}

    def build(plan):
        nc = bacc.Bacc("TRN2", target_bir_lowering=False, num_devices=1)
        a = {n: nc.dram_tensor("in_" + n, arrays["in_" + n].shape, mybir.dt.from_np(arrays["in_" + n].dtype),
                               kind="ExternalInput").ap() for n in _NAMES}
        a["out"] = nc.dram_tensor("out", (B, T, D), F32, kind="ExternalOutput").ap()
        return nc, decoder_program(nc, a, plan)

    _, plan = build({})
    nc, again = build(plan)
    assert plan == again
    r = run_bass_kernel_spmd(nc, [arrays], core_ids=[0])
    return r.results[0]["out"]
```

```python
from contextlib import ExitStack, contextmanager

import concourse.bass as bass
from concourse import mybir

F32 = mybir.dt.float32
U32 = mybir.dt.uint32
F32R = mybir.dt.float32r
ALU = mybir.AluOpType
ACT = mybir.ActivationFunctionType
AX = mybir.AxisListType
ET = mybir.EngineType

P = 128
B, T, D = 8, 256, 256
KT = D // P
TT = T // P
H, DH = 4, 64
HL = P // DH
NP = TT * H
CH = 32
NCH = P // CH
TAPS = 4
FIRS = (3, 15, 64)
NF = len(FIRS)
NPATH = NF + 2
NS = 4
HF = 2 * D
BLK = 64
NBLK = T // BLK
XH, XD = 16, 16
NE, NSH, FF = 8, 2, 352
FT = [(0, 128), (128, 128), (256, 96)]
TG = 512
NTOK = B * T


class Mark:

    def __init__(self, src, index, loop, prev=False):
        self.src, self.index, self.loop, self.prev = src, index, loop, prev


class Counter:

    def __init__(self, prog, name, unit):
        self.prog, self.name, self.unit = prog, name, unit
        self.sem = prog.ctx.enter_context(prog.nc.semaphore(name))
        self.count = 0
        prog.counters.append(self)

    def tick(self, ins):
        ins.then_inc(self.sem, self.unit)
        self.count += 1
        return Mark(self, self.count, self.prog.loop)


class Slot:

    def __init__(self, prog, name):
        self.name, self.readers = name, []
        prog.slots.append(self)

    def read(self, *marks):
        self.readers = list(marks)
        return marks[-1]

    def also(self, *marks):
        self.readers += list(marks)


class Loop:
    def __init__(self, name, engines):
        self.name, self.engines, self.reg, self.base = name, engines, None, {}


class Engine:
    def __init__(self, prog, eng, name, serial):
        self.prog, self.eng, self.serial = prog, eng, serial
        self.done = Counter(prog, name, 1)
        self.seen = {}
        self.last = None

    def wait(self, marks):
        prog = self.prog
        best = {}
        for m in marks:
            if m is None:
                continue
            if isinstance(m, (list, tuple)):
                raise TypeError("flat list of marks")
            loop = m.loop
            if prog.loop is not None and loop is not prog.loop:
                if self in prog.loop.engines and not prog.loop.outside:
                    continue
            if loop is not None and prog.loop is loop:
                value = m.index - (prog.per(loop, m.src) if m.prev else 0)
                key = (m.src, loop)
            elif loop is not None:
                value, key = loop.final[m.src], (m.src, None)
            else:
                value, key = m.index, (m.src, None)
            if best.get(key, -10**9) < value:
                best[key] = value
        for (src, loop), value in best.items():
            if self.seen.get((src, loop), -10**9) >= value:
                continue
            self.seen[(src, loop)] = value
            if loop is None:
                self.eng.wait_ge(src.sem, value * src.unit)
            else:
                step = prog.per(loop, src) * src.unit
                self.eng.wait_ge(src.sem, loop.reg * step + value * src.unit)
                if self is prog.sp:
                    self.part()

    def part(self):
        if self.prog.loop is not None:
            self.eng.sem_inc(self.prog.parted, 1)

    def op(self, ins_of, *args, after=(), count=True, split=False, **kw):
        own = [self.last] if self.serial else []
        self.wait(own + list(after))
        if split or self is self.prog.pool:
            self.part()
        ins = ins_of(*args, **kw)
        if not count:
            return None
        self.last = self.done.tick(ins)
        return self.last


class Program:
    def __init__(self, nc, ctx, plan):
        self.nc, self.ctx, self.plan, self.new_plan = nc, ctx, plan, {}
        self.counters, self.slots, self.loop = [], [], None
        self.pe = Engine(self, nc.tensor, "pe_done", False)
        self.act = Engine(self, nc.scalar, "act_done", True)
        self.dve = Engine(self, nc.vector, "dve_done", True)
        self.pool = Engine(self, nc.gpsimd, "pool_done", True)
        self.sp = Engine(self, nc.sync, "sp_done", False)
        self.engines = [self.pe, self.act, self.dve, self.pool, self.sp]
        self.dma_sems = {}
        self.parted = ctx.enter_context(nc.semaphore("parted"))

    def per(self, loop, src):
        return self.plan.get(loop.name, {}).get("per", {}).get(src.name, 1)

    def slot(self, name):
        return Slot(self, name)

    def dma(self, stream, out, in_, after=(), queue=None, **kw):
        if stream not in self.dma_sems:
            self.dma_sems[stream] = Counter(self, "dma_" + stream, 16)
        q = queue or self.sp
        q.wait(list(after))
        return self.dma_sems[stream].tick(q.eng.dma_start(out, in_, **kw))

    def meet(self, engines=None):
        engines = engines or self.engines
        absent = [e.done for e in self.engines if e not in engines]
        for e in engines:
            e.wait([Mark(c, c.count, None) for c in self.counters if c.count and c not in absent])

    @contextmanager
    def repeat(self, name, n, engines=None, start=0):
        engines = engines or self.engines
        loop = Loop(name, engines)
        loop.outside = False
        plan = self.plan.get(name, {})
        per = plan.get("per", {})
        for c in per:
            if c.startswith("dma_") and c[4:] not in self.dma_sems:
                self.dma_sems[c[4:]] = Counter(self, c, 16)
        self.meet(engines)
        owner = {e.done: e for e in self.engines}
        for c in self.counters:
            if per.get(c.name):
                (owner.get(c) or engines[-1]).eng.sem_inc(c.sem, per[c.name] * c.unit)
                c.count += per[c.name]
        names = {c.name: c for c in self.counters}
        outer = {s: s.readers for s in self.slots}
        for s in self.slots:
            s.readers = [Mark(names[c], i, loop, True) for c, i in plan.get("slots", {}).get(s.name, [])
                         if c in names]
        for s in self.slots:
            for m in s.readers:
                m.index += m.src.count
        before = {c: c.count for c in self.counters}
        for e in engines:
            e.seen, e.last = {}, None
        with self.nc.Fori(0, n, engines=tuple(e.eng.engine for e in engines)) as reg:
            loop.reg, self.loop = reg, loop
            last_marks = plan.get("last", {})
            for e in engines:
                if e.serial and e.done.name in last_marks:
                    e.last = Mark(e.done, before[e.done] + last_marks[e.done.name], loop, True)
            yield reg
        self.loop = None
        new = {"per": {}, "slots": {}, "last": {}}
        loop.final = {}
        for c in self.counters:
            start_count = before.get(c, 0)
            made = c.count - start_count
            if made:
                new["per"][c.name] = made
            if c in owner and made:
                new["last"][c.name] = made
            c.count = start_count + made * n
            loop.final[c] = c.count
        for s in self.slots:
            mine = [m for m in s.readers if m.loop is loop and not m.prev]
            if mine:
                new["slots"][s.name] = [(m.src.name, m.index - before.get(m.src, 0)) for m in mine]
            elif s in outer:
                s.readers = outer[s]
        self.new_plan[name] = new
        for e in engines:
            e.seen, e.last = {}, None


def interleave(parts):
    parts = list(parts)
    while parts:
        parts = [g for g in parts if next(g, STOP) is not STOP]


STOP = object()


def pipeline(pg, name, stages, n):
    K = len(stages)

    def step(s, reg=0):
        interleave(stages[k](s - k + reg, (s - k) % 2) for k in range(K) if not isinstance(reg, int) or 0 <= s - k < n)

    pg.meet()
    for s in range(K - 1):
        step(s)
    pairs = (n - K + 1) // 2
    with pg.repeat(name, pairs) as it:
        for j in range(2):
            step(K - 1 + j, it * 2)
    for s in range(K - 1 + 2 * pairs, n + K - 1):
        step(s)


def make_constants(pg, a, env):
    nc, pool, dve, act, ctx = pg.nc, pg.pool, pg.dve, pg.act, pg.ctx
    sb = env.sb
    env.ident = sb("ident", [P, P])
    env.causal = sb("causal", [P, P])
    env.exponent = sb("exponent", [P, 3, 40])
    env.headmask = sb("headmask", [P, P // XD])
    env.expert_no = sb("expert_no", [P, NE])
    pool.op(nc.gpsimd.memset, env.ident[:], 0.0)
    pool.op(nc.gpsimd.affine_select, out=env.ident[:], in_=env.ident[:], compare_op=ALU.not_equal,
            fill=1.0, base=0, pattern=[[-1, P]], channel_multiplier=1)
    pool.op(nc.gpsimd.memset, env.causal[:], 1.0)
    pool.op(nc.gpsimd.affine_select, out=env.causal[:], in_=env.causal[:], compare_op=ALU.is_ge,
            fill=0.0, base=0, pattern=[[1, P]], channel_multiplier=-1)
    for k, x in enumerate((-0.5, 0.5, 2.718281828459045)):
        pool.op(nc.gpsimd.memset, env.exponent[:, k, :], x)
    pool.op(nc.gpsimd.memset, env.headmask[:], 1.0)
    pool.op(nc.gpsimd.affine_select, out=env.headmask[:], in_=env.headmask[:], compare_op=ALU.is_ge,
            fill=0.0, base=0, pattern=[[-XD, P // XD]], channel_multiplier=1)
    pool.op(nc.gpsimd.affine_select, out=env.headmask[:], in_=env.headmask[:], compare_op=ALU.is_ge,
            fill=0.0, base=XD - 1, pattern=[[XD, P // XD]], channel_multiplier=-1)
    for e in range(NE):
        pool.op(nc.gpsimd.memset, env.expert_no[:, e:e + 1], float(e))


def load_weight(pg, env, sb, name, dram, cols, stream):
    w = sb(name, [P, D // P, cols])
    m = pg.dma(stream, w[:], dram.rearrange("(k p) n -> p k n", p=P))
    return w, m


def phase_project(pg, a, env):
    nc, pe, act, dve, pool = pg.nc, pg.pe, pg.act, pg.dve, pg.pool
    V, S, G = nc.vector, nc.scalar, nc.gpsimd
    with ExitStack() as mem:
        def sb(n, shape, dt=F32):
            return mem.enter_context(nc.sbuf_tensor(n, shape, dt))
        ps = env.ps
        W = []
        for n, src in (("wq", a["Wq"]), ("wk", a["Wk"]), ("wv", a["Wv"])):
            w, m = load_weight(pg, env, sb, n, src, D, "w_project")
            W.append(w)
        wb, _ = load_weight(pg, env, sb, "wb", a["Wb"], H, "w_project")
        taps = sb("taps", [P, 3, KT, TAPS])
        for j, src in enumerate((a["conv_q"], a["conv_k"], a["conv_v"])):
            pg.dma("w_project", taps[:, j], src.rearrange("(k p) i -> p k i", p=P))

        sel = [sb(f"sel{i}", [P, NPATH, 2 * NPATH]) for i in range(2)]
        rows = [sb(f"gw1_rows{i}", [P, NPATH, HF]) for i in range(2)]
        sums = [sb(f"gw1_sums{i}", [2 * NPATH, HF]) for i in range(2)]
        for i, (lo, hi) in enumerate(((1.0 / DH, 1.0 / DH), (1.0 / DH, 1.0))):
            pool.op(G.memset, sel[i][:], 0.0)
            for n in range(NPATH):
                pool.op(G.memset, sel[i][0:DH, n, n:n + 1], lo)
                pool.op(G.memset, sel[i][DH:P, n, NPATH + n:NPATH + n + 1], hi)
        gw1_rows = a["gW1"][D:, :].rearrange("(n g p) c -> p g n c", n=NPATH, p=P)
        w1s_rows = env.w1s_dram.rearrange("(s n h) c -> s n h c", n=NPATH, h=H)

        xin = [sb(f"xin{i}", [P, TT, D]) for i in range(2)]
        xT = sb("xT", [P, KT, T])
        raw = [sb(f"raw{i}", [P, 3, KT, TAPS - 1 + T]) for i in range(2)]
        conv = [sb(f"conv{i}", [P, 3, KT, T]) for i in range(2)]
        tok = [sb(f"tok{i}", [P, TT, 3, D]) for i in range(2)]
        sq = sb("sq", [P, 2, TT, D])
        ss = sb("ss", [P, 2 * TT * H])
        rn = sb("rn", [P, 2 * TT * H])
        kT = sb("kT", [P, KT, TT, P])
        km = sb("km", [P, KT, TT, HL, P])
        diag = [sb(f"diag{i}", [P, NP, CH]) for i in range(2)]
        for i in range(2):
            dve.op(V.memset, raw[i][:], 0.0)
        dve.op(V.memset, km[:], 0.0)
        sl = {n: pg.slot("p_" + n) for n in ("xT", "sq", "ss", "rn", "kT", "km", *(f"b{k}" for k in range(8)))}
        for n in ("rows", "sums", "xin", "raw", "conv", "tok", "diag", "made_x", "made_rows", "made_conv"):
            for i in range(2):
                sl[f"{n}{i}"] = pg.slot(f"p_{n}{i}")

        def slot(n):
            return sl[n]

        def R(*names):
            return [m for n in names for m in slot(n).readers]

        def fetch(b, i):
            m = pg.dma(f"x{i}", xin[i][:], a["x"].rearrange("b (t p) d -> p b t d", p=P)[:, bass.ds(b, 1)]
                       .rearrange("p b t d -> p (b t) d"), after=R(f"xin{i}"))
            slot(f"made_x{i}").read(m)
            m = pg.dma(f"gw1_{i}", rows[i][:], gw1_rows[:, bass.ds(b, 1)].rearrange("p g n c -> p (g n) c"),
                       after=R(f"rows{i}"))
            slot(f"made_rows{i}").read(m)
            yield

        def project(b, i):
            for k in range(KT):
                for t in range(TT):
                    m = pe.op(nc.tensor.transpose, ps[:, 0, (k * TT + t) * P:(k * TT + t + 1) * P],
                              xin[i][:, t, k * P:(k + 1) * P], env.ident[:], count=(k, t) == (1, 1),
                              after=R(f"made_x{i}", "b0"))
            slot(f"xin{i}").read(m)
            m_xT = act.op(S.copy, xT[:].rearrange("p k t -> p (k t)"), ps[:, 0, :], after=[m] + R("xT"))
            slot("b0").read(m_xT)
            yield
            m_raw = []
            for j in range(3):
                for c in range(KT):
                    for k in range(KT):
                        m = pe.op(nc.tensor.matmul, ps[:, 1 + j, c * T:(c + 1) * T], W[j][:, k, c * P:(c + 1) * P],
                                  xT[:, k, :], start=(k == 0), stop=(k == KT - 1), count=(c, k) == (1, 1),
                                  after=[m_xT] + R(f"b{1 + j}"))
                m_raw.append(act.op(S.copy, raw[i][:, j, :, TAPS - 1:], ps[:, 1 + j, :].rearrange("p (c t) -> p c t", c=KT),
                                    after=[m] + R(f"raw{i}")))
                slot(f"b{1 + j}").read(m_raw[j])
                yield
            for t in range(TT):
                for k in range(KT):
                    m = pe.op(nc.tensor.matmul, ps[:, 0, t * H:(t + 1) * H], xT[:, k, t * P:(t + 1) * P],
                              wb[:, k, :], start=(k == 0), stop=(k == KT - 1), count=(t, k) == (1, 1), after=R("b0"))
            slot("xT").read(m)
            bt = env.beta[:, bass.ds(b, 1), :].rearrange("p b n -> p (b n)")
            m = act.op(S.activation, bt, ps[:, 0, 0:NP], ACT.Tanh, scale=0.5, after=[m])
            slot("b0").read(m)
            m_beta = dve.op(V.tensor_scalar, bt, bt, 0.5, 0.5, ALU.mult, ALU.add, after=[m])
            for j in range(3):
                m_first = []
                for c in range(KT):
                    m_first.append(act.op(S.activation, conv[i][:, j, c, :], raw[i][:, j, c, 0:T], ACT.Copy,
                                          scale=taps[:, j, c, 0:1], after=[m_raw[j]] + R(f"conv{i}")))
                for c in range(KT):
                    for s in range(1, TAPS):
                        m = dve.op(V.scalar_tensor_tensor, out=conv[i][:, j, c, :],
                                   in0=raw[i][:, j, c, s:s + T], scalar=taps[:, j, c, s:s + 1],
                                   in1=conv[i][:, j, c, :], op0=ALU.mult, op1=ALU.add, after=[m_raw[j], m_first[c]])
                yield
            slot(f"raw{i}").read(m)
            flat = conv[i][:].rearrange("p j c t -> p (j c t)")
            m_silu = act.op(S.activation, flat, flat, ACT.Silu, after=[m])
            slot(f"made_conv{i}").read(m_silu, m_beta)
            for n in range(NPATH):
                m = pe.op(nc.tensor.matmul, ps[0:2 * NPATH, 0, :], sel[i][:, n, :], rows[i][:, n, :], start=(n == 0),
                          stop=(n == NPATH - 1), count=n == NPATH - 1, after=R(f"made_rows{i}", "b0"))
            slot(f"rows{i}").read(m)
            m = dve.op(V.tensor_copy, sums[i][:], ps[0:2 * NPATH, 0, :], after=[m] + R(f"sums{i}"))
            slot("b0").read(m)
            yield
            head = b // 2 if isinstance(b, int) else b >> 1
            for lohi in range(2):
                m2 = pg.dma(f"sums{i}", w1s_rows[2 * i + lohi][:, bass.ds(head, 1), :].rearrange("n h c -> n (h c)"),
                            sums[i][lohi * NPATH:(lohi + 1) * NPATH, :], after=[m])
            slot(f"sums{i}").read(m2)
            yield

        def normalise(b, i):
            made = R(f"made_conv{i}")
            for j in range(3):
                for t in range(TT):
                    for c in range(KT):
                        m = pe.op(nc.tensor.transpose, ps[:, 4 + j, (t * KT + c) * P:(t * KT + c + 1) * P],
                                  conv[i][:, j, c, t * P:(t + 1) * P], env.ident[:], count=(t, c) == (1, 1),
                                  after=made + R(f"b{4 + j}"))
            m_t = m
            slot(f"conv{i}").read(m)
            m_sq = act.op(S.activation, sq[:].rearrange("p j t d -> p (j t d)"),
                          ps[:, 4:6, :].rearrange("p j n -> p (j n)"), ACT.Square, after=[m_t] + R("sq"))
            m_v = act.op(S.copy, tok[i][:, :, 2, :], ps[:, 6, :].rearrange("p (t d) -> p t d", t=TT),
                         after=[m_t] + R(f"tok{i}"))
            slot("b6").read(m_v)
            yield
            m_ss = dve.op(V.tensor_reduce, ss[:], sq[:].rearrange("p j t (h d) -> p (j t h) d", h=H), AX.X, ALU.add,
                          after=[m_sq] + R("ss"))
            slot("sq").read(m_ss)
            m = pool.op(G.tensor_scalar, rn[:], ss[:], 1.0, 1e-6, ALU.mult, ALU.add, after=[m_ss] + R("rn"))
            slot("ss").read(m)
            m_rn = pool.op(G.tensor_tensor, rn[:], rn[:], env.exponent[:, 0, 0:2 * NP], ALU.pow)
            yield
            for j in range(2):
                m_tok = dve.op(V.tensor_tensor, tok[i][:, :, j, :].rearrange("p t (h d) -> p t h d", h=H),
                               ps[:, 4 + j, :].rearrange("p (t h d) -> p t h d", t=TT, h=H),
                               rn[:, j * NP:(j + 1) * NP].rearrange("p (t h) -> p t h", t=TT).unsqueeze(3)
                               .broadcast_to([P, TT, H, DH]), ALU.mult, after=[m_rn, m_t] + R(f"tok{i}"))
            slot("rn").read(m_tok)
            slot("b4").read(m_sq, m_tok)
            slot("b5").read(m_sq, m_tok)
            m_st = pg.dma(f"tok{i}", env.tok_dram[bass.ds(b, 1)].rearrange("b p n -> p (b n)"),
                          tok[i][:].rearrange("p t j d -> p (t j d)"), after=[m_v, m_tok])
            for c in range(KT):
                for t in range(TT):
                    m = pe.op(nc.tensor.transpose, ps[:, 7, (c * TT + t) * P:(c * TT + t + 1) * P],
                              tok[i][:, t, 1, c * P:(c + 1) * P], env.ident[:], count=(c, t) == (1, 1),
                              after=[m_tok] + R("b7"))
            slot(f"tok{i}").read(m_st, m)
            yield
            m_kT = act.op(S.copy, kT[:].rearrange("p c t n -> p (c t n)"), ps[:, 7, :], after=[m] + R("kT"))
            for h in range(HL):
                q = slice(h * DH, (h + 1) * DH)
                m_km = act.op(S.copy, km[q, :, :, h, :].rearrange("p c t n -> p (c t) n"),
                              ps[q, 7, :].rearrange("p (c n) -> p c n", n=P), after=[m] + R("km"))
            slot("b7").read(m_km)
            yield
            for c in range(KT):
                for t in range(TT):
                    n = t * H + c * HL
                    m = pe.op(nc.tensor.matmul, ps[:, 4 + n // 4, (n % 4) * P:(n % 4 + HL) * P], kT[:, c, t, :],
                              km[:, c, t, :, :], start=True, stop=True, count=(c, t) == (1, 1),
                              after=[m_kT, m_km] + R("b4", "b5"))
            slot("kT").read(m)
            slot("km").read(m)
            yield
            last = m
            for c in range(NCH):
                q = slice(c * CH, (c + 1) * CH)
                src = ps[q, 4:6, :].rearrange("p u (n j) -> p (u n) j", j=P)[:, :, q]
                m = dve.op(V.tensor_tensor, diag[i][q, :, :], src,
                           env.beta[q, bass.ds(b, 1), :].rearrange("p b n -> p (b n)").unsqueeze(2)
                           .broadcast_to([CH, NP, CH]), ALU.mult, after=[last] + R(f"diag{i}"))
            slot("b4").read(m)
            slot("b5").read(m)
            m = pg.dma(f"diag{i}", env.a_dram[:, bass.ds(b, 1), :].rearrange("p b n -> p (b n)"),
                       diag[i][:].rearrange("p n j -> p (n j)"), after=[m])
            slot(f"diag{i}").read(m)
            yield

        pipeline(pg, "project", [fetch, project, normalise], B)
        pg.meet()


def phase_invert_and_fir(pg, a, env):
    nc, pe, act, dve, pool = pg.nc, pg.pe, pg.act, pg.dve, pg.pool
    G = B * NP * NCH // P
    with ExitStack() as mem:
        def sb(n, shape, dt=F32):
            return mem.enter_context(nc.sbuf_tensor(n, shape, dt))
        ps = env.ps
        am = sb("am", [P, G, CH, CH])
        inv = sb("inv", [P, G, CH, CH])
        tmp = sb("tmp", [P, G, CH, CH])
        for c in range(NCH):
            for g in range(G):
                m_am = pg.dma("am", am[c * CH:(c + 1) * CH, g],
                              env.a_dram[c * CH:(c + 1) * CH].rearrange("i b (n j) -> (b n) i j", j=CH)
                              [g * 32:(g + 1) * 32])
        win = sb("win", [P, B * NBLK, P])
        wpad = sb("wpad", [P, KT, NF, 2 * P])
        m_w = pool.op(nc.gpsimd.memset, wpad[:].rearrange("p k f n -> p (k f n)"), 0.0)
        m_win0 = pool.op(nc.gpsimd.memset, win[0:BLK].rearrange("p n c -> p (n c)"), 0.0)
        for f, taps in enumerate(FIRS):
            m_wp = pg.dma("wpad", wpad[:, :, f, P - taps:P], a[f"fir{f}"].rearrange("(k p) i -> p k i", p=P), after=[m_w])

        dve.op(nc.vector.memset, inv[:].rearrange("p g a b -> p (g a b)"), 0.0)
        dve.op(nc.vector.memset, inv[:].rearrange("p g a b -> p g (a b)")[:, :, 0:CH * CH:CH + 1], 1.0)
        for i in range(1, CH):
            dve.op(nc.vector.tensor_tensor, tmp[:, :, 0:i, 0:i], inv[:, :, 0:i, 0:i],
                   am[:, :, i, 0:i].unsqueeze(2).broadcast_to([P, G, i, i]), ALU.mult, after=[m_am])
            dve.op(nc.vector.tensor_reduce, inv[:, :, 0:i, i], tmp[:, :, 0:i, 0:i], AX.X, ALU.add, negate=True)
        m_inv = dve.last
        for g in range(G):
            m_tr = dve.op(nc.vector.tensor_copy, am[:, g], inv[:, g].rearrange("p j i -> p i j"))

        hank = sb("hank", [P, P, NF, BLK])
        stage = sb("stage", [P, NF, BLK, CH])
        shifted = sb("shifted", [P, NF, P + 8])
        s_h, s_sh, s_win, s_st = (pg.slot(n) for n in ("hank", "shifted", "win", "stage"))
        banks = [pg.slot(f"fir_bank{n}") for n in range(8)]
        tokv = env.tok_dram.rearrange("b p (t j d) -> j t p b d", t=TT, j=3)[2]
        for c in range(KT):
            for blk in range(NBLK):
                for half in range(2):
                    start = (blk - 1) * BLK + half * BLK
                    if start < 0:
                        continue
                    t, off = start // P, start % P
                    m_win = pg.dma("win", win[half * BLK:(half + 1) * BLK].rearrange("p (b n) c -> p n b c", n=NBLK)[:, blk],
                                   tokv[t, off:off + BLK, :, c * P:(c + 1) * P], after=[m_win0] + s_win.readers)
            with pg.repeat(f"hankel{c}", BLK // 8, engines=[pe, act, pool]) as it:
                m_s = pool.op(nc.gpsimd.tensor_copy, shifted[:], wpad[:, c, :, bass.ds(it * 8, P + 8)],
                              after=s_sh.readers)
                for f in range(NF):
                    for half in range(2):
                        n = f * 2 + half
                        for j in range(4):
                            m = pe.op(nc.tensor.transpose, ps[:, n, j * P:(j + 1) * P],
                                      shifted[:, f, half * 4 + j:half * 4 + j + P], env.ident[:],
                                      after=[m_s] + banks[n].readers)
                        dst = hank[:, :, f, bass.ds(it * (-8) + (BLK - 1 - half * 4 - 3), 4)]
                        m = act.op(nc.scalar.copy, dst.rearrange("p c j -> p j c"),
                                   ps[:, n, :].rearrange("p (j c) -> p j c", c=P)[:, ::-1, :], after=[m])
                        banks[n].read(m)
                s_sh.read(pe.last)
            pg.meet([pe])
            for pair in range(CH // 2):
                bank = pair % 8
                for u in range(2):
                    for q in range(NCH):
                        ch = q * CH + pair * 2 + u
                        m = pe.op(nc.tensor.matmul, ps[q * CH:(q + 1) * CH, bank, u * NF * BLK:(u + 1) * NF * BLK],
                                  win[:, :, ch], hank[:, ch, :, :].rearrange("p f t -> p (f t)"),
                                  start=True, stop=True, after=[m_win] + banks[bank].readers)
                m = act.op(nc.scalar.copy, stage[:].rearrange("p f t c -> p c (f t)")[:, pair * 2:pair * 2 + 2],
                           ps[:, bank, 0:2 * NF * BLK].rearrange("p (c n) -> p c n", c=2), after=[m] + s_st.readers)
                banks[bank].read(m)
            s_win.read(pe.last)
            ms = []
            for q in range(NCH):
                for f in range(NF):
                    ms.append(pg.dma("stage", env.fir_dram[f].rearrange("(n t) d -> n t d", t=BLK)
                                     [:, :, c * P + q * CH:c * P + (q + 1) * CH], stage[q * CH:(q + 1) * CH, f],
                                     after=[m]))
            s_st.read(*ms[-1:])
        for k, (src, m) in enumerate(((inv, m_inv), (am, m_tr))):
            for c in range(NCH):
                for g in range(G):
                    pg.dma("inv", env.t_dram[k, c * CH:(c + 1) * CH].rearrange("i n j -> n i j")[g * 32:(g + 1) * 32],
                           src[c * CH:(c + 1) * CH, g], after=[m])
        pg.meet()


def phase_delta_and_gate(pg, a, env):
    nc, pe, act, dve, pool = pg.nc, pg.pe, pg.act, pg.dve, pg.pool
    with ExitStack() as mem:
        def sb(n, shape, dt=F32):
            return mem.enter_context(nc.sbuf_tensor(n, shape, dt))
        ps = env.ps
        V, S, G = nc.vector, nc.scalar, nc.gpsimd
        w1x, _ = load_weight(pg, env, sb, "w1x", a["gW1"][0:D, :], HF, "w_gate")
        w1s = sb("w1s", [NS * NPATH * H, HF])
        pg.dma("w_gate", w1s[:], env.w1s_dram)
        gw2 = sb("gw2", [P, HF // P, H * NPATH])
        pg.dma("w_gate", gw2[:], a["gW2"].rearrange("(k p) n -> p k n", p=P))
        gb1 = sb("gb1", [P, HF // P])
        pg.dma("w_gate", gb1[:], a["gb1"].rearrange("(k p) -> p k", p=P), allow_slow_non_contiguous=True)
        wo, m_w = load_weight(pg, env, sb, "wo", a["Wo"], D, "w_gate")
        nw = sb("nw", [P, 1])
        for h in range(HL):
            pg.dma("w_gate", nw[h * DH:(h + 1) * DH, :], a["norm_w"].rearrange("(d o) -> d o", o=1))
        gb2 = sb("gb2", [P, H * NPATH])
        pg.dma("w_gate", gb2[:], a["gb2"].partition_broadcast(P))
        lt = sb("lt", [P, H])
        pg.dma("w_gate", lt[:], a["log_tau"].partition_broadcast(P))
        eps = sb("eps", [P, H, NPATH])
        m_w = pg.dma("w_gate", eps[:].rearrange("p h n -> p (h n)"), a["eps_logit"].rearrange("h n -> (h n)").partition_broadcast(P))
        dve.op(V.tensor_scalar, wo[:].rearrange("p k n -> p (k n)"), wo[:].rearrange("p k n -> p (k n)"),
               nw[:, 0:1], None, ALU.mult, after=[m_w])
        t1, t2 = sb("t1", [P, H]), sb("t2", [P, H])
        m = act.op(S.activation, t1[:], lt[:], ACT.Abs, after=[m_w])
        m = act.op(S.activation, t1[:], t1[:], ACT.Exp, scale=-1.0)
        m = act.op(S.activation, t1[:], t1[:], ACT.Ln, bias=1.0)
        dve.op(V.tensor_scalar, t2[:], lt[:], 0.0, 0.5, ALU.max, ALU.add)
        dve.op(V.tensor_tensor, t2[:], t2[:], t1[:], ALU.add, after=[m])
        itau = sb("itau", [P, H])
        dve.op(V.reciprocal, itau[:], t2[:])
        m = act.op(S.activation, eps[:].rearrange("p h n -> p (h n)"), eps[:].rearrange("p h n -> p (h n)"), ACT.Exp, scale=-1.0)
        dve.op(V.tensor_scalar, eps[:], eps[:], 1.0, None, ALU.add, after=[m])
        dve.op(V.reciprocal, eps[:], eps[:])
        dve.op(V.tensor_scalar, eps[:], eps[:], 0.2, None, ALU.mult)
        keep = sb("keep", [P, H])
        dve.op(V.tensor_reduce, keep[:], eps[:], AX.X, ALU.add)
        dve.op(V.tensor_scalar, keep[:], keep[:], -1.0, 1.0, ALU.mult, ALU.add)

        tok = [sb(f"dtok{i}", [P, TT, 3, D]) for i in range(2)]
        xin = [sb(f"dx{i}", [P, TT, D]) for i in range(2)]
        paths = [sb(f"paths{i}", [P, NPATH, TT, D]) for i in range(2)]
        g0 = [sb(f"g0_{i}", [P, NP, P]) for i in range(2)]
        x0 = [sb(f"x0_{i}", [P, NP, P]) for i in range(2)]
        xT = sb("dxT", [P, KT, T])
        kT = sb("dkT", [P, KT, TT, P])
        km, qm = sb("dkm", [P, KT, TT, HL, P]), sb("dqm", [P, KT, TT, HL, P])
        qT = [sb(f"dqT{i}", [P, KT, P]) for i in range(2)]
        kb = [sb(f"kb{i}", [P, TT, D]) for i in range(2)]
        vb = sb("vb", [P, TT, D])
        m1, m2 = sb("m1", [P, NP, P]), sb("m2", [P, NP, P])
        lT = [sb(f"lT{i}", [P, NP, P]) for i in range(2)]
        z = sb("z", [P, NP, P])
        x1 = sb("x1", [P, NP, P])
        gw = [sb(f"gw{i}", [P, NP, P]) for i in range(2)]
        sbd = sb("sbd", [P, KT, P])
        uT = sb("uT", [P, TT, KT, P])
        u = sb("u", [P, TT, KT, P])
        wTn = sb("wTn", [P, KT, P])
        oT = sb("oT", [P, TT, KT, P])
        st = sb("st", [P, TT, NS, NPATH, H])
        big = sb("big", [P, NPATH, TT, D])
        stT = sb("stT", [80, T])
        hid = sb("hid", [P, HF // P, T])
        lgT = sb("lgT", [H * NPATH, T])
        lg = sb("lg", [P, TT, H, NPATH])
        sm = sb("sm", [P, 2, TT * H])
        o = sb("o", [P, TT, D])
        onT = sb("onT", [P, KT, T])
        y = [sb(f"y{i}", [P, TT, D]) for i in range(2)]
        bn, mv = sb("bn", [P, TT, 6]), sb("mv", [P, TT, 2])
        for t in (m1, m2, sbd, *g0, *x0):
            pool.op(G.memset, t[:].rearrange("p a b -> p (a b)"), 0.0)
        for t in (km, qm):
            pool.op(G.memset, t[:], 0.0)
        sl = {}

        def slot(n):
            if n not in sl:
                sl[n] = pg.slot("d_" + n)
            return sl[n]

        for n in range(8):
            slot(f"b{n}")
        for n in ("xT", "kT", "km", "qm", "vb", "m1", "m2", "z", "x1", "sbd", "uT", "u", "wTn", "oT",
                  "st", "big", "stT", "hid", "lgT", "lg", "sm", "o", "onT", "bn"):
            slot(n)
        for n in ("tok", "xin", "paths", "g0", "x0", "y", "kb", "lT", "qT", "gw", "made_gw", "made_lT", "made_qT",
                  "made_x", "made_paths", "made_y"):
            for i in range(2):
                slot(f"{n}{i}")

        def R(*names):
            return [m for n in names for m in slot(n).readers]

        def flat(t):
            return t.rearrange("p a b -> p (a b)")

        def heads(t):
            return t.rearrange("p t (h d) -> p t h d", h=H)

        hs = [slice(0, DH), slice(DH, P)]

        def invert(b, i):
            s1 = bass.ds(b, 1)
            m_tok = pg.dma(f"dtok{i}", tok[i][:].rearrange("p t j d -> p (t j d)"),
                           env.tok_dram[s1].rearrange("b p n -> p (b n)"), after=R(f"tok{i}"))
            for c in range(NCH):
                q = slice(c * CH, (c + 1) * CH)
                m_g0 = pg.dma(f"g0{i}", g0[i][q, :, q], env.t_dram[0, q, bass.ds(b * NP, NP), :], after=R(f"g0{i}"))
                m_x0 = pg.dma(f"x0{i}", x0[i][q, :, q], env.t_dram[1, q, bass.ds(b * NP, NP), :], after=R(f"x0{i}"))
            bt = env.beta[:, s1, :].rearrange("p b (t h) -> p (b t) h", t=TT).unsqueeze(3).broadcast_to([P, TT, H, DH])
            m_kb = dve.op(V.tensor_tensor, heads(kb[i][:]), heads(tok[i][:, :, 1, :]), bt, ALU.mult, after=[m_tok] + R(f"kb{i}"))
            yield
            for bank in range(3):
                for c in range(KT):
                    for t in range(TT):
                        in_ = kb[i][:, t, c * P:(c + 1) * P] if bank == 1 else \
                            tok[i][:, t, 1 if bank == 0 else 0, c * P:(c + 1) * P]
                        m = pe.op(nc.tensor.transpose, ps[:, bank, (c * TT + t) * P:(c * TT + t + 1) * P], in_,
                                  env.ident[:], count=(c, t) == (1, 1), after=[m_kb if bank == 1 else m_tok] + R(f"b{bank}"))
                if bank == 1:
                    m_kT = act.op(S.copy, kT[:].rearrange("p c t n -> p (c t n)"), ps[:, 1, :], after=[m] + R("kT"))
                    slot("b1").read(m_kT)
                else:
                    dst, nm = (km, "km") if bank == 0 else (qm, "qm")
                    for h in range(HL):
                        m_m = dve.op(V.tensor_copy, dst[hs[h], :, :, h, :].rearrange("p c t n -> p (c t) n"),
                                     ps[hs[h], bank, :].rearrange("p (c n) -> p c n", n=P), after=[m] + R(nm))
                    if bank == 0:
                        m_km = m_m
                        slot("b0").read(m_m)
                    else:
                        m_qm = m_m
                        m_qT = act.op(S.copy, qT[i][:], ps[:, 2, :].rearrange("p (c t n) -> p c t n", c=KT, t=TT)[:, :, 1, :],
                                      after=[m, m_m] + R(f"qT{i}"))
                        slot("b2").read(m_qT)
                        slot(f"made_qT{i}").read(m_qT)
                yield
            for c in range(KT):
                for t in range(TT):
                    n = c * HL
                    m_A = pe.op(nc.tensor.matmul, ps[:, 3 * (1 - t), n * P:(n + HL) * P], kT[:, c, t, :], km[:, c, t, :, :],
                                start=True, stop=True, after=[m_km, m_kT] + R("b3", "b0"), count=(c, t) == (1, 1))
            slot("kT").read(m_A)
            for t in range(TT):
                pa = ps[:, 3 * (1 - t), :].rearrange("p (n j) -> p n j", j=P)
                tn = slice(t * H, (t + 1) * H)
                for lo in (0, 2 * CH):
                    m_m1 = act.op(S.activation, m1[lo + CH:lo + 2 * CH, tn, lo:lo + CH], pa[lo + CH:lo + 2 * CH, :, lo:lo + CH],
                                  ACT.Copy, scale=-1.0, after=[m_A] + R("m1"))
                m_m2 = act.op(S.activation, m2[2 * CH:P, tn, 0:2 * CH], pa[2 * CH:P, :, 0:2 * CH], ACT.Copy, scale=-1.0,
                              after=R("m2"))
                slot(f"b{3 * (1 - t)}").read(m_m2)
            yield
            for t in range(TT):
                for c in range(KT):
                    for h in range(HL):
                        n = c * HL + h
                        m_L = pe.op(nc.tensor.matmul, ps[:, 1 + t, n * P:(n + 1) * P], km[:, c, t, h, :], qm[:, c, t, h, :],
                                    start=True, stop=True, after=[m_qm, m_km] + R("b1", "b2"), count=(c, h) == (1, 1))
                m_lT = dve.op(V.tensor_tensor, lT[i][:, t * H:(t + 1) * H], ps[:, 1 + t, :].rearrange("p (n j) -> p n j", j=P),
                              env.causal[:].unsqueeze(1).broadcast_to([P, H, P]), ALU.mult, after=[m_L] + R(f"lT{i}"))
                slot(f"b{1 + t}").read(m_lT)
            slot("km").read(m_L)
            slot("qm").read(m_L)
            slot(f"made_lT{i}").read(m_lT)
            yield

            def each(lhs, rhs, banks, after, fn):
                made = []
                for u2 in range(2):
                    for n in range(4 * u2, 4 * u2 + 4):
                        out = ps[:, banks[u2], (n % 4) * P:(n % 4 + 1) * P]
                        if rhs is None:
                            m = pe.op(nc.tensor.transpose, out, lhs[:, n, :], env.ident[:], after=after[u2] + R(f"b{banks[u2]}"),
                                      count=n % 4 == 3)
                        else:
                            m = pe.op(nc.tensor.matmul, out, lhs[:, n, :], rhs[:, n, :], start=True, stop=True,
                                      after=after[u2] + R(f"b{banks[u2]}"), count=n % 4 == 3)
                    made.append(fn(ps[:, banks[u2], :], slice(4 * u2, 4 * u2 + 4), m))
                    slot(f"b{banks[u2]}").read(made[-1])
                return m, made

            def both(a_, b_=()):
                return [[x, *b_] for x in (a_ if isinstance(a_, list) else [a_, a_])]

            m, m_z = each(m1, g0[i], (3, 0), both(m_m1, [m_g0]), lambda p_, n_, m_:
                          act.op(S.copy, flat(z[:, n_]), p_, after=[m_] + R("z")))
            slot("m1").read(m)
            yield
            m, m_g = each(x0[i], z, (1, 2), both(m_z, [m_x0]), lambda p_, n_, m_:
                          dve.op(V.tensor_tensor, flat(gw[i][:, n_]), flat(g0[i][:, n_]), p_, ALU.add, after=[m_] + R(f"gw{i}")))
            slot(f"x0{i}").read(m)
            slot(f"g0{i}").read(*m_g)
            slot("z").read(m)
            yield
            m, m_x1 = each(gw[i], None, (3, 0), both(m_g), lambda p_, n_, m_:
                           act.op(S.copy, flat(x1[:, n_]), p_, after=[m_] + R("x1")))
            m, m_z = each(m2, gw[i], (1, 2), both(m_g, [m_m2]), lambda p_, n_, m_:
                          act.op(S.copy, flat(z[:, n_]), p_, after=[m_] + R("z")))
            slot("m2").read(m)
            yield
            m, m_g = each(x1, z, (3, 0), [[m_z[u_], m_x1[u_]] for u_ in range(2)], lambda p_, n_, m_:
                          dve.op(V.tensor_tensor, flat(gw[i][:, n_]), flat(gw[i][:, n_]), p_, ALU.add, after=[m_]))
            slot("z").read(m)
            slot("x1").read(m)
            slot(f"made_gw{i}").read(*m_g)
            yield

        def states(b, i):
            s1 = bass.ds(b, 1)
            m_x = pg.dma(f"dx{i}", xin[i][:], a["x"].rearrange("b (t p) d -> p b t d", p=P)[:, s1]
                         .rearrange("p b t d -> p (b t) d"), after=R(f"xin{i}"))
            slot(f"made_x{i}").read(m_x)
            for f in range(NF):
                m_fir = pg.dma(f"fir{i}", paths[i][:, f], env.fir_dram[f].rearrange("(b t p) d -> p b t d", p=P, t=TT)
                               [:, s1].rearrange("p b t d -> p (b t) d"), after=R(f"paths{i}"))
            bt = env.beta[:, s1, :].rearrange("p b (t h) -> p (b t) h", t=TT).unsqueeze(3).broadcast_to([P, TT, H, DH])
            m_vb = dve.op(V.tensor_tensor, heads(vb[:]), heads(tok[i][:, :, 2, :]), bt, ALU.mult,
                          after=R("vb", f"made_gw{i}", f"made_lT{i}", f"made_qT{i}"))
            m_v5 = pool.op(G.tensor_copy, paths[i][:, NPATH - 1], tok[i][:, :, 2, :], after=R(f"paths{i}", f"made_gw{i}"))
            made = R(f"made_gw{i}", f"made_lT{i}", f"made_qT{i}")

            def beta_v(t, c, h):
                n = t * H + c * HL + h
                return pe.op(nc.tensor.matmul, ps[hs[h], 4, c * P:(c + 1) * P],
                             vb[:, t, (c * HL + h) * DH:(c * HL + h + 1) * DH], gw[i][:, n, :], start=True,
                             stop=(t == 0), after=made + [m_vb] + R("b4"), skip_group_check=True, count=h == 1)

            for c in range(KT):
                for h in range(HL):
                    m_u0 = beta_v(0, c, h)
            for c in range(KT):
                for h in range(HL):
                    m = pe.op(nc.tensor.matmul, ps[hs[h], 5, c * P:(c + 1) * P],
                              kb[i][:, 1, (c * HL + h) * DH:(c * HL + h + 1) * DH], gw[i][:, H + c * HL + h, :], start=True,
                              stop=True, after=R("b5"), count=(c, h) == (1, 1))
            slot(f"kb{i}").read(m)
            m_wT = act.op(S.activation, flat(wTn[:]), ps[:, 5, 0:KT * P], ACT.Copy, scale=-1.0, after=[m] + R("wTn"))
            slot("b5").read(m_wT)
            m_uT = dve.op(V.tensor_copy, flat(uT[:, 0]), ps[:, 4, 0:KT * P], after=[m_u0] + R("uT"))
            slot("b4").read(m_uT)
            yield
            for c in range(KT):
                m = pe.op(nc.tensor.transpose, ps[:, 5, c * P:(c + 1) * P], uT[:, 0, c, :], env.ident[:], after=[m_uT] + R("b5"))
            m_u = dve.op(V.tensor_copy, flat(u[:, 0]), ps[:, 5, 0:KT * P], after=[m] + R("u"))
            slot("b5").read(m_u)
            yield
            for c in range(KT):
                m = pe.op(nc.tensor.matmul, ps[:, 5, c * P:(c + 1) * P], tok[i][:, 0, 1, c * P:(c + 1) * P], u[:, 0, c, :],
                          start=True, stop=True, after=[m_u] + R("b5"))
            slot(f"tok{i}").read(m, m_v5, m_vb)
            for h in range(HL):
                m_s = dve.op(V.tensor_copy, sbd[hs[h], :, hs[h]],
                             ps[hs[h], 5, 0:KT * P].rearrange("p (c n) -> p c n", c=KT)[:, :, hs[h]], after=[m] + R("sbd"))
            slot("b5").read(m_s)
            yield
            for c in range(KT):
                for h in range(HL):
                    beta_v(1, c, h)
                m = pe.op(nc.tensor.matmul, ps[:, 4, c * P:(c + 1) * P], sbd[:, c, :], wTn[:, c, :],
                          start=False, stop=True, after=[m_s, m_wT], skip_group_check=True)
            slot("wTn").read(m)
            slot("vb").read(m)
            slot(f"gw{i}").read(m)
            m_uT = dve.op(V.tensor_copy, flat(uT[:, 1]), ps[:, 4, 0:KT * P], after=[m])
            slot("b4").read(m_uT)
            yield
            for c in range(KT):
                m = pe.op(nc.tensor.transpose, ps[:, 5, c * P:(c + 1) * P], uT[:, 1, c, :], env.ident[:], after=[m_uT] + R("b5"))
            slot("uT").read(m)
            m_u = dve.op(V.tensor_copy, flat(u[:, 1]), ps[:, 5, 0:KT * P], after=[m])
            slot("b5").read(m_u)
            yield
            for t in range(TT):
                for c in range(KT):
                    if t:
                        pe.op(nc.tensor.matmul, ps[:, 4, (t * KT + c) * P:(t * KT + c + 1) * P], sbd[:, c, :], qT[i][:, c, :],
                              start=True, stop=False, after=[m_u] + R("b4"), count=False, skip_group_check=True)
                    for h in range(HL):
                        n = t * H + c * HL + h
                        m = pe.op(nc.tensor.matmul, ps[hs[h], 4, (t * KT + c) * P:(t * KT + c + 1) * P],
                                  u[:, t, c, hs[h]], lT[i][:, n, :], start=(t == 0), stop=True, after=[m_u] + R("b4"),
                                  skip_group_check=True, count=(t, c, h) == (1, 1, 1))
            for nm in ("u", f"lT{i}", f"qT{i}", "sbd"):
                slot(nm).read(m)
            m_oT = act.op(S.copy, oT[:].rearrange("p t c n -> p (t c n)"), ps[:, 4, :], after=[m] + R("oT"))
            slot("b4").read(m_oT)
            yield
            for t in range(TT):
                for c in range(KT):
                    m = pe.op(nc.tensor.transpose, ps[:, 5, (t * KT + c) * P:(t * KT + c + 1) * P], oT[:, t, c, :],
                              env.ident[:], after=[m_oT] + R("b5"), count=(t, c) == (1, 1))
            slot("oT").read(m)
            m_dl = act.op(S.copy, paths[i][:, NF].rearrange("p t d -> p (t d)"), ps[:, 5, :], after=[m] + R(f"paths{i}"))
            slot("b5").read(m_dl)
            slot(f"made_paths{i}").read(m_fir, m_v5, m_dl)
            yield

        def gate(b, i):
            s1 = bass.ds(b, 1)
            m_x = R(f"made_x{i}")
            for c in range(KT):
                for t in range(TT):
                    m = pe.op(nc.tensor.transpose, ps[:, 6, (c * TT + t) * P:(c * TT + t + 1) * P], xin[i][:, t, c * P:(c + 1) * P],
                              env.ident[:], count=(c, t) == (1, 1), after=m_x + R("b6"))
            m_xT = act.op(S.copy, flat(xT[:]), ps[:, 6, :], after=[m] + R("xT"))
            slot("b6").read(m_xT)
            made = R(f"made_paths{i}")
            pf = paths[i][:].rearrange("p n t (h d) -> p (n t h) d", h=H)

            def stat(s):
                return st[:, :, s].rearrange("p t n h -> p n t h")

            m_sq = act.op(S.activation, big[:].rearrange("p n t d -> p (n t d)"), paths[i][:].rearrange("p n t d -> p (n t d)"),
                          ACT.Square, after=made + R("big"))
            yield
            dve.op(V.tensor_reduce, stat(0), pf, AX.X, ALU.add, after=made + R("st"))
            yield
            dve.op(V.tensor_reduce, stat(2), pf, AX.X, ALU.add, apply_absolute_value=True)
            yield
            m_st = dve.op(V.tensor_reduce, stat(1), big[:].rearrange("p n t (h d) -> p (n t h) d", h=H), AX.X, ALU.add,
                          after=[m_sq])
            slot("big").read(m_st)
            m_st = pool.op(G.tensor_tensor, st[:, :, 3].rearrange("p t n h -> p t (n h)"), st[:, :, 1].rearrange("p t n h -> p t (n h)"),
                           env.exponent[:, 1, :].rearrange("p (t n) -> p t n", t=TT), ALU.pow, after=[m_st])
            yield
            for t in range(TT):
                m = pe.op(nc.tensor.transpose, ps[0:80, 7, t * P:(t + 1) * P], st[:, t].rearrange("p s n h -> p (s n h)"), env.ident[:],
                          after=[m_st] + R("b7"), count=t == 1)
            slot("st").read(m)
            m_stT = act.op(S.copy, stT[:], ps[0:80, 7, 0:T], after=[m] + R("stT"))
            slot("b7").read(m_stT)
            yield
            for c in range(HF // P):
                bank = 6 + c // 2
                for k in range(KT + 1):
                    l_ = w1x[:, k, c * P:(c + 1) * P] if k < KT else w1s[:, c * P:(c + 1) * P]
                    r_ = xT[:, k, :] if k < KT else stT[:]
                    m = pe.op(nc.tensor.matmul, ps[:, bank, (c % 2) * T:(c % 2 + 1) * T], l_, r_, start=(k == 0),
                              stop=(k == KT), after=[m_xT] + ([m_stT] if k == KT else []) + R(f"b{bank}"), count=k == KT)
                if c % 2:
                    for e in (c - 1, c):
                        m_h = act.op(S.activation, hid[:, e, :], ps[:, bank, (e % 2) * T:(e % 2 + 1) * T], ACT.Gelu,
                                     bias=gb1[:, e:e + 1], after=[m] + R("hid"))
                    slot(f"b{bank}").read(m_h)
                    yield
            slot("xT").read(m)
            slot("stT").read(m)
            for c in range(HF // P):
                m = pe.op(nc.tensor.matmul, ps[0:H * NPATH, 6, 0:T], gw2[:, c, :], hid[:, c, :], start=(c == 0),
                          stop=(c == HF // P - 1), after=[m_h] + R("b6"), count=c == 3)
            slot("hid").read(m)
            m = act.op(S.copy, lgT[:], ps[0:H * NPATH, 6, 0:T], after=[m] + R("lgT"))
            slot("b6").read(m)
            yield
            for t in range(TT):
                m2_ = pe.op(nc.tensor.transpose, ps[:, 7, t * H * NPATH:(t + 1) * H * NPATH], lgT[:, t * P:(t + 1) * P],
                            env.ident[0:H * NPATH, 0:H * NPATH], split=True, after=[m] + R("b7"), count=t == 1)
            slot("lgT").read(m2_)
            lf = lg[:].rearrange("p t h n -> p t (h n)")
            m = dve.op(V.tensor_tensor, lf, ps[:, 7, 0:TT * H * NPATH].rearrange("p (t n) -> p t n", t=TT),
                       gb2[:].unsqueeze(1).broadcast_to([P, TT, H * NPATH]), ALU.add, after=[m2_] + R("lg"))
            slot("b7").read(m)
            lh = lg[:].rearrange("p t h n -> p (t h) n")

            def per_head(t):
                return t.unsqueeze(1).unsqueeze(3).broadcast_to([P, TT, H, NPATH])

            yield
            dve.op(V.tensor_tensor, lg[:], lg[:], per_head(itau[:]), ALU.mult)
            dve.op(V.tensor_reduce, sm[:, 0, :], lh, AX.X, ALU.max, after=R("sm"))
            m = dve.op(V.tensor_tensor, lh, lh, sm[:, 0, :].unsqueeze(2).broadcast_to([P, NP, NPATH]), ALU.subtract)
            lw = lg[:].rearrange("p t h n -> p (t h n)")
            m = pool.op(G.tensor_tensor, lw, env.exponent[:, 2, :], lw, ALU.pow, after=[m])
            yield
            dve.op(V.tensor_reduce, sm[:, 1, :], lh, AX.X, ALU.add, after=[m])
            dve.op(V.reciprocal, sm[:, 1, :], sm[:, 1, :])
            dve.op(V.tensor_tensor, lh, lh, sm[:, 1, :].unsqueeze(2).broadcast_to([P, NP, NPATH]), ALU.mult)
            dve.op(V.tensor_tensor, lg[:], lg[:], per_head(keep[:]), ALU.mult)
            m_pr = dve.op(V.tensor_tensor, lg[:], lg[:], eps[:].unsqueeze(1).broadcast_to([P, TT, H, NPATH]), ALU.add)
            yield

            def weighed(E, eng, n):
                return E.op(eng.tensor_tensor, big[:, n].rearrange("p t (h d) -> p (t h) d", h=H),
                            paths[i][:, n].rearrange("p t (h d) -> p (t h) d", h=H),
                            lh[:, :, n:n + 1].broadcast_to([P, NP, DH]), ALU.mult, after=[m_pr])

            def path(n):
                return big[:, n].rearrange("p t d -> p (t d)")

            weighed(pool, G, 3)
            weighed(pool, G, 4)
            m_p = pool.op(G.tensor_tensor, path(3), path(3), path(4), ALU.add)
            for n in range(NF):
                m = weighed(dve, V, n)
            slot("lg").read(m, m_p)
            slot(f"paths{i}").read(m, m_p)
            yield
            dve.op(V.tensor_tensor, path(0), path(0), path(1), ALU.add)
            dve.op(V.tensor_tensor, path(0), path(0), path(2), ALU.add)
            m_o = dve.op(V.tensor_tensor, o[:].rearrange("p t d -> p (t d)"), path(0), path(3), ALU.add,
                         after=[m_p] + R("o"))
            m = act.op(S.activation, path(0), flat(o[:]), ACT.Square, after=[m_o])
            yield
            m = dve.op(V.tensor_reduce, sm[:, 0, :], big[:, 0].rearrange("p t (h d) -> p (t h) d", h=H), AX.X, ALU.add, after=[m])
            slot("big").read(m)
            m = pool.op(G.tensor_scalar, sm[:, 0, :], sm[:, 0, :], 1.0 / DH, 1e-5, ALU.mult, ALU.add, after=[m])
            m = pool.op(G.tensor_tensor, sm[:, 0, :], sm[:, 0, :], env.exponent[:, 0, 0:NP], ALU.pow)
            yield
            of = o[:].rearrange("p t (h d) -> p (t h) d", h=H)
            m_on = dve.op(V.tensor_tensor, of, of, sm[:, 0, :].unsqueeze(2).broadcast_to([P, NP, DH]), ALU.mult, after=[m])
            slot("sm").read(m_on)
            for c in range(KT):
                for t in range(TT):
                    m = pe.op(nc.tensor.transpose, ps[:, 6, (c * TT + t) * P:(c * TT + t + 1) * P], o[:, t, c * P:(c + 1) * P],
                              env.ident[:], after=[m_on] + R("b6"), count=(c, t) == (1, 1))
            slot("o").read(m)
            m_onT = act.op(S.copy, flat(onT[:]), ps[:, 6, :], after=[m] + R("onT"))
            slot("b6").read(m_onT)
            yield
            for t in range(TT):
                for k in range(KT):
                    m = pe.op(nc.tensor.matmul, ps[:, 7, t * D:(t + 1) * D], onT[:, k, t * P:(t + 1) * P], wo[:, k, :],
                              start=(k == 0), stop=(k == 1), after=[m_onT] + R("b7"), count=(t, k) == (1, 1))
            slot("onT").read(m)
            m = dve.op(V.tensor_tensor, flat(y[i][:]), ps[:, 7, :], flat(xin[i][:]), ALU.add, after=[m] + R(f"y{i}"))
            slot("b7").read(m)
            slot(f"xin{i}").read(m)
            yield
            m = norm_rows(pg, env, y[i], bn, mv, [m] + R("bn"))
            slot("bn").read(m)
            slot(f"made_y{i}").read(m)
            yield

        def store(b, i):
            m = pg.dma(f"x1_{i}", env.x1_dram.rearrange("b (t p) d -> p b t d", p=P)[:, bass.ds(b, 1)]
                       .rearrange("p b t d -> p (b t) d"), y[i][:], after=R(f"made_y{i}"))
            slot(f"y{i}").read(m)
            yield

        pipeline(pg, "delta", [invert, states, gate, store], B)
        pg.meet()


def norm_rows(pg, env, y, bn, mv, after):
    nc, dve, pool = pg.nc, pg.dve, pg.pool
    for t in range(TT):
        dve.op(nc.vector.bn_stats, bn[:, t, :], y[:, t, :], after=after)
        dve.op(nc.vector.bn_aggr, mv[:, t, :], bn[:, t, :], split=True)
    m = pool.op(nc.gpsimd.tensor_scalar, mv[:, :, 1], mv[:, :, 1], 1.0, 1e-5, ALU.mult, ALU.add, after=[dve.last])
    m = pool.op(nc.gpsimd.tensor_tensor, mv[:, :, 1], mv[:, :, 1], env.exponent[:, 0, 0:TT], ALU.pow)
    for t in range(TT):
        m = dve.op(nc.vector.tensor_scalar, y[:, t, :], y[:, t, :], mv[:, t, 0:1], mv[:, t, 1:2], ALU.subtract, ALU.mult, after=[m])
    return m


def phase_cross(pg, a, env):
    nc, pe, act, dve, pool = pg.nc, pg.pe, pg.act, pg.dve, pg.pool
    V, S, G = nc.vector, nc.scalar, nc.gpsimd
    HT = P // XD
    with ExitStack() as mem:
        def sb(n, shape, dt=F32):
            return mem.enter_context(nc.sbuf_tensor(n, shape, dt))
        ps = env.ps
        Wx = {n: load_weight(pg, env, sb, "x" + n, a[n], D, "w_cross")[0] for n in ("q_w", "k_w", "v_w", "o_w")}
        gate_w, _ = load_weight(pg, env, sb, "gate_w", a["gate_w"], NE, "w_cross")
        bq, bk = sb("bq", [P, KT]), sb("bk", [P, KT])
        pg.dma("w_cross", bq[:], a["q_b"].rearrange("(k p) -> p k", p=P), allow_slow_non_contiguous=True)
        pg.dma("w_cross", bk[:], a["k_b"].rearrange("(k p) -> p k", p=P), allow_slow_non_contiguous=True)
        bv, bo = sb("bv", [P, D]), sb("bo", [P, D])
        pg.dma("w_cross", bv[:], a["v_b"].partition_broadcast(P))
        pg.dma("w_cross", bo[:], a["o_b"].partition_broadcast(P))
        xin = [sb(f"cx{i}", [P, TT, D]) for i in range(2)]
        cin = [sb(f"cc{i}", [P, TT, D]) for i in range(2)]
        xT, cT = sb("cxT", [P, KT, T]), sb("ccT", [P, KT, T])
        qT, kT = sb("cqT", [P, KT, T]), sb("ckT", [P, KT, T])
        km = [sb(f"ckm{i}", [P, XH, T]) for i in range(2)]
        vv = [sb(f"vv{i}", [P, TT, XH, CH]) for i in range(2)]
        pr = [sb(f"pr{i}", [P, TT, 2, T]) for i in range(3)]
        pT = [sb(f"pT{i}", [P, 2, TT, T]) for i in range(2)]
        mx = sb("mx", [P, XH, TT])
        oT = sb("coT", [P, XH // 4, T])
        rs = sb("rs", [P, TT, XH])
        o = sb("co", [P, TT, D])
        onT = sb("conT", [P, KT, T])
        y = [sb(f"cy{i}", [P, TT, D]) for i in range(2)]
        bn, mv = sb("cbn", [P, TT, 6]), sb("cmv", [P, TT, 2])
        lgT = sb("clgT", [NE, T])
        lg = sb("clg", [P, TT, NE])
        top = sb("top", [P, TT, 8])
        ti = sb("ti", [P, TT, 8], U32)
        tif = sb("tif", [P, TT, 8])
        wsel = sb("wsel", [P, TT, 2])
        tmp = sb("ctmp", [P, TT, NE])
        for i in range(2):
            pool.op(G.memset, vv[i][:], 1.0)
        sl = {}

        def slot(n):
            if n not in sl:
                sl[n] = pg.slot("c_" + n)
            return sl[n]

        for n in range(8):
            slot(f"b{n}")
        for n in ("xT", "cT", "qT", "kT", "mx", "oT", "rs", "o", "onT", "bn", "lgT", "lg", "top", "tmp"):
            slot(n)
        for n in ("xin", "cin", "km", "vv", "pr", "pT", "y"):
            for i in range(3):
                slot(f"{n}{i}")

        def R(*names):
            return [m for n in names for m in slot(n).readers]

        def flat(t):
            return t.rearrange("p a b -> p (a b)")

        with pg.repeat("cross", B // 2) as it:
            for i in range(2):
                b = it * 2 + i
                s1 = bass.ds(b, 1)
                m_x = pg.dma(f"cx{i}", xin[i][:], env.x1_dram.rearrange("b (t p) d -> p b t d", p=P)[:, s1]
                             .rearrange("p b t d -> p (b t) d"), after=R(f"xin{i}"))
                m_c = pg.dma(f"cc{i}", cin[i][:], a["ctx"].rearrange("b (t p) d -> p b t d", p=P)[:, s1]
                             .rearrange("p b t d -> p (b t) d"), after=R(f"cin{i}"))
                for bank, src, dst, nm, m_in in ((0, cin[i], cT, "cT", m_c), (1, xin[i], xT, "xT", m_x)):
                    for c in range(KT):
                        for t in range(TT):
                            m = pe.op(nc.tensor.transpose, ps[:, bank, (c * TT + t) * P:(c * TT + t + 1) * P],
                                      src[:, t, c * P:(c + 1) * P], env.ident[:], after=[m_in] + R(f"b{bank}"),
                                      count=(c, t) == (1, 1))
                    if bank == 0:
                        slot(f"cin{i}").read(m)
                    m_e = act.op(S.copy, flat(dst[:]), ps[:, bank, :], after=[m] + R(nm))
                    slot(f"b{bank}").read(m_e)
                    if bank == 0:
                        m_cT = m_e
                    else:
                        m_xT = m_e
                for bank, w, src, dst, nm, bias, m_in in ((2, "k_w", cT, kT, "kT", bk, m_cT), (3, "q_w", xT, qT, "qT", bq, m_xT)):
                    for c in range(KT):
                        for k in range(KT):
                            m = pe.op(nc.tensor.matmul, ps[:, bank, c * T:(c + 1) * T], Wx[w][:, k, c * P:(c + 1) * P],
                                      src[:, k, :], start=(k == 0), stop=(k == 1), after=[m_in] + R(f"b{bank}"), count=k == 1)
                    for c in range(KT):
                        m_e = dve.op(V.tensor_scalar, dst[:, c, :], ps[:, bank, c * T:(c + 1) * T], bias[:, c:c + 1], None,
                                     ALU.add, after=[m] + R(nm))
                    slot(f"b{bank}").read(m_e)
                    if bank == 2:
                        m_kT = m_e
                    else:
                        m_qT = m_e
                slot("xT").read(m)
                for t in range(TT):
                    for k in range(KT):
                        m = pe.op(nc.tensor.matmul, ps[:, 0, t * D:(t + 1) * D], cT[:, k, t * P:(t + 1) * P],
                                  Wx["v_w"][:, k, :], start=(k == 0), stop=(k == 1), after=[m_cT] + R("b0"), count=(t, k) == (1, 1))
                slot("cT").read(m)
                for t in range(TT):
                    m_v = dve.op(V.tensor_tensor, vv[i][:, t, :, 0:XD], ps[:, 0, t * D:(t + 1) * D].rearrange("p (h d) -> p h d", h=XH),
                                 bv[:].rearrange("p (h d) -> p h d", h=XH), ALU.add, after=[m] + R(f"vv{i}"))
                slot("b0").read(m_v)
                m_km = []
                for h in range(XH):
                    m = pool.op(G.tensor_scalar, km[i][:, h, :], kT[:, h // HT, :], env.headmask[:, h % HT:h % HT + 1], 1.0,
                                ALU.mult, ALU.mult, after=[m_kT] + R(f"km{i}"))
                    m_km.append(m)
                slot("kT").read(m)
                NPAIR = XH // 2
                scored, expd, turned = {}, {}, {}

                def scores(g):
                    for t in range(TT):
                        bank = 2 + 2 * (g % 2) + t
                        m = pe.op(nc.tensor.matmul, ps[:, bank, :], qT[:, (2 * g) // HT, t * P:(t + 1) * P],
                                  flat(km[i][:, 2 * g:2 * g + 2, :]), start=True, stop=True,
                                  after=[m_qT, m_km[2 * g + 1]] + R(f"b{bank}"))
                    scored[g] = m

                def softmax(g):
                    bank = 2 + 2 * (g % 2)
                    m_mx = dve.op(V.tensor_reduce, mx[:, 2 * g:2 * g + 2, :].rearrange("p h t -> p t h"),
                                  ps[:, bank:bank + 2, :].rearrange("p t (h k) -> p t h k", h=2), AX.X, ALU.max,
                                  after=[scored[g]] + R("mx"))
                    m_mx = dve.op(V.tensor_scalar, mx[:, 2 * g:2 * g + 2, :], mx[:, 2 * g:2 * g + 2, :], -float(XD) ** -0.5,
                                  None, ALU.mult)
                    for t in range(TT):
                        for h in range(2):
                            m = act.op(S.activation, pr[g % 3][:, t, h, :], ps[:, bank + t, h * T:(h + 1) * T], ACT.Exp,
                                       bias=mx[:, 2 * g + h, t:t + 1], scale=float(XD) ** -0.5,
                                       after=[m_mx] + R(f"pr{g % 3}"))
                        slot(f"b{bank + t}").read(m)
                    expd[g] = m

                def turn(g):
                    for h in range(2):
                        for kt_ in range(TT):
                            for t in range(TT):
                                m = pe.op(nc.tensor.transpose, ps[:, h, (kt_ * TT + t) * P:(kt_ * TT + t + 1) * P],
                                          pr[g % 3][:, t, h, kt_ * P:(kt_ + 1) * P], env.ident[:],
                                          after=[expd[g]] + R(f"b{h}"), count=(kt_, t) == (1, 1))
                        E, fn = (act, S.copy) if h == 0 and g % 2 else (dve, V.tensor_copy)
                        m_e = E.op(fn, pT[g % 2][:, h].rearrange("p k t -> p (k t)"), ps[:, h, :], after=[m] + R(f"pT{g % 2}"))
                        slot(f"b{h}").read(m_e)
                        turned[g, h] = m_e
                    slot(f"pr{g % 3}").read(m)

                def values(g):
                    for h in range(2):
                        head = 2 * g + h
                        q = (head % 4) * CH
                        for k in range(TT):
                            m = pe.op(nc.tensor.matmul, ps[q:q + CH, 6 + head // 8, (head // 4 % 2) * T:(head // 4 % 2 + 1) * T],
                                      vv[i][:, k, head, :], pT[g % 2][:, h, k, :], start=(k == 0), stop=(k == 1),
                                      after=[turned[g, 0], turned[g, 1], m_v] + R("b6", "b7"), skip_group_check=True)
                    slot(f"pT{g % 2}").read(m)
                    return m

                for g in range(NPAIR + 2):
                    if g < NPAIR:
                        scores(g)
                        softmax(g)
                    if 1 <= g <= NPAIR:
                        turn(g - 1)
                    if g >= 2:
                        m = values(g - 2)
                slot("mx").read(expd[NPAIR - 1])
                slot(f"km{i}").read(scored[NPAIR - 1])
                slot("qT").read(scored[NPAIR - 1])
                slot(f"vv{i}").read(m)
                m_oT = act.op(S.copy, oT[:].rearrange("p g t -> p (g t)"), ps[:, 6:8, :].rearrange("p u n -> p (u n)"),
                              after=[m] + R("oT"))
                slot("b6").read(m_oT)
                slot("b7").read(m_oT)
                for t in range(TT):
                    for g in range(XH // 4):
                        m = pe.op(nc.tensor.transpose, ps[:, t, g * P:(g + 1) * P], oT[:, g, t * P:(t + 1) * P], env.ident[:],
                                  after=[m_oT] + R(f"b{t}"), count=(t, g) == (1, 3))
                slot("oT").read(m)
                for t in range(TT):
                    src = ps[:, t, :].rearrange("p (h d) -> p h d", h=XH)
                    dve.op(V.reciprocal, rs[:, t, :], src[:, :, XD], after=[m])
                    m_o = dve.op(V.tensor_tensor, o[:, t, :].rearrange("p (h d) -> p h d", h=XH), src[:, :, 0:XD],
                                 rs[:, t, :].unsqueeze(2).broadcast_to([P, XH, XD]), ALU.mult, after=R("o"))
                    slot(f"b{t}").read(m_o)
                for c in range(KT):
                    for t in range(TT):
                        m = pe.op(nc.tensor.transpose, ps[:, 2, (c * TT + t) * P:(c * TT + t + 1) * P], o[:, t, c * P:(c + 1) * P],
                                  env.ident[:], after=[m_o] + R("b2"), count=(c, t) == (1, 1))
                slot("o").read(m)
                m_onT = act.op(S.copy, flat(onT[:]), ps[:, 2, :], after=[m] + R("onT"))
                slot("b2").read(m_onT)
                for t in range(TT):
                    for k in range(KT):
                        m = pe.op(nc.tensor.matmul, ps[:, 3, t * D:(t + 1) * D], onT[:, k, t * P:(t + 1) * P], Wx["o_w"][:, k, :],
                                  start=(k == 0), stop=(k == 1), after=[m_onT] + R("b3"), count=(t, k) == (1, 1))
                slot("onT").read(m)
                m_y = dve.op(V.tensor_tensor, flat(y[i][:]), ps[:, 3, :], flat(xin[i][:]), ALU.add, after=[m] + R(f"y{i}"))
                slot("b3").read(m_y)
                slot(f"xin{i}").read(m_y)
                dve.op(V.tensor_tensor, y[i][:], y[i][:], bo[:].unsqueeze(1).broadcast_to([P, TT, D]), ALU.add)
                m_y = norm_rows(pg, env, y[i], bn, mv, [])
                m_y2 = pool.op(G.tensor_copy, env.x2[:, bass.ds(b * TT, TT), :], y[i][:], after=[m_y])
                for c in range(KT):
                    for t in range(TT):
                        m = pe.op(nc.tensor.transpose, ps[:, 4, (c * TT + t) * P:(c * TT + t + 1) * P], y[i][:, t, c * P:(c + 1) * P],
                                  env.ident[:], after=[m_y] + R("b4"), count=(c, t) == (1, 1))
                slot(f"y{i}").read(m, m_y2)
                m_2T = act.op(S.copy, flat(onT[:]), ps[:, 4, :], after=[m] + R("onT"))
                x2T = ps[:, 4, :].rearrange("p (c t) -> p c t", c=KT)
                hi, lo = (x_[:, :, bass.ds(b * T, T)] for x_ in env.x2T)
                m = act.op(S.copy, hi, x2T)
                m = dve.op(V.tensor_tensor, lo, x2T, hi, ALU.subtract, after=[m])
                slot("b4").read(m)
                for k in range(KT):
                    m = pe.op(nc.tensor.matmul, ps[0:NE, 5, 0:T], gate_w[:, k, :], onT[:, k, :], start=(k == 0), stop=(k == 1),
                              after=[m_2T] + R("b5"), count=k == 1)
                slot("onT").read(m)
                m = act.op(S.copy, lgT[:], ps[0:NE, 5, 0:T], after=[m] + R("lgT"))
                for t in range(TT):
                    m2_ = pe.op(nc.tensor.transpose, ps[:, 5, T + t * NE:T + (t + 1) * NE], lgT[:, t * P:(t + 1) * P],
                                env.ident[0:NE, 0:NE], split=True, after=[m], count=t == 1)
                slot("lgT").read(m2_)
                m = dve.op(V.tensor_copy, lg[:], ps[:, 5, T:T + TT * NE].rearrange("p (t n) -> p t n", t=TT), after=[m2_] + R("lg"))
                slot("b5").read(m)
                for t in range(TT):
                    dve.op(V.max, top[:, t, :], lg[:, t, :], after=R("top"), split=True)
                    dve.op(V.max_index, ti[:, t, :], top[:, t, :], lg[:, t, :], split=True)
                dve.op(V.tensor_copy, tif[:], ti[:])
                m = dve.op(V.tensor_tensor, wsel[:, :, 1:2], top[:, :, 1:2], top[:, :, 0:1], ALU.subtract)
                m = act.op(S.activation, wsel[:, :, 1:2], wsel[:, :, 1:2], ACT.Exp, after=[m])
                m = dve.op(V.tensor_scalar, wsel[:, :, 0:1], wsel[:, :, 1:2], 1.0, None, ALU.add, after=[m])
                dve.op(V.reciprocal, wsel[:, :, 0:1], wsel[:, :, 0:1])
                dve.op(V.tensor_tensor, wsel[:, :, 1:2], wsel[:, :, 1:2], wsel[:, :, 0:1], ALU.mult)
                for t in range(TT):
                    for k in range(2):
                        m = dve.op(V.tensor_scalar, tmp[:, k, :] if k else env.wte[:, bass.ds(b * TT + t, 1), :].rearrange("p a b -> p (a b)"),
                                   env.expert_no[:], tif[:, t, k:k + 1], wsel[:, t, k:k + 1], ALU.is_equal, ALU.mult)
                    w_ = env.wte[:, bass.ds(b * TT + t, 1), :].rearrange("p a b -> p (a b)")
                    m = dve.op(V.tensor_tensor, w_, w_, tmp[:, 1, :], ALU.add)
        pg.meet()


def phase_experts(pg, a, env):
    nc, pe, act, dve, pool = pg.nc, pg.pe, pg.act, pg.dve, pg.pool
    V, S, G = nc.vector, nc.scalar, nc.gpsimd
    with ExitStack() as mem:
        def sb(n, shape, dt=F32):
            return mem.enter_context(nc.sbuf_tensor(n, shape, dt))
        ps = env.ps
        raw = [sb(f"w_raw{i}", [P, 2, KT, FF]) for i in range(2)]
        rawd = [sb(f"wd_raw{i}", [P, len(FT), D]) for i in range(2)]
        w = [[sb(f"w{part}{i}", [P, 2, KT, FF], F32R) for part in ("hi", "lo")] for i in range(2)]
        wd = [[sb(f"wd{part}{i}", [P, len(FT), D], F32R) for part in ("hi", "lo")] for i in range(2)]
        sg = [sb(f"sg{i}", [P, TG]) for i in range(2)]
        h = [sb(f"h{i}", [P, TG]) for i in range(2)]
        hT = [[sb(f"hT{part}{i}", [P, len(FT), TG], F32R) for part in ("hi", "lo")] for i in range(2)]
        acc = env.x2
        sl = {}

        def slot(n):
            if n not in sl:
                sl[n] = pg.slot("e_" + n)
            return sl[n]

        for n in range(8):
            slot(f"b{n}")
        for n in ("raw", "rawd", "w", "wd", "made_w", "made_wd", "sg", "h", "hT"):
            for i in range(2):
                slot(f"{n}{i}")

        def R(*names):
            return [m for n in names for m in slot(n).readers]

        PARTS = ((0, 0), (0, 1), (1, 0))

        def split(hi, lo, whole, after, free):
            m = act.op(S.copy, hi, whole, after=after + free)
            return pool.op(G.tensor_tensor, lo, whole, hi, ALU.subtract, after=[m] + free)

        def load(i, g, u, d):
            pg.dma(f"w{i}", raw[i][:, 0], g, after=R(f"raw{i}"))
            m = pg.dma(f"w{i}", raw[i][:, 1], u)
            nfull = 2 * P
            pg.dma(f"wd{i}", rawd[i][:, 0:2], d[0:nfull].rearrange("(k p) n -> p k n", p=P), after=R(f"rawd{i}"))
            m2 = pg.dma(f"wd{i}", rawd[i][0:FF - nfull, 2], d[nfull:FF])
            m_w = split(w[i][0][:].rearrange("p j k n -> p (j k n)"), w[i][1][:].rearrange("p j k n -> p (j k n)"),
                        raw[i][:].rearrange("p j k n -> p (j k n)"), [m], R(f"w{i}"))
            slot(f"raw{i}").read(m_w)
            split(wd[i][0][:, 0:2], wd[i][1][:, 0:2], rawd[i][:, 0:2], [m2], R(f"wd{i}"))
            m_d = split(wd[i][0][0:FF - nfull, 2], wd[i][1][0:FF - nfull, 2], rawd[i][0:FF - nfull, 2], [m2], R(f"wd{i}"))
            slot(f"rawd{i}").read(m_d)
            slot(f"made_w{i}").read(m_w)
            slot(f"made_wd{i}").read(m_d)

        bn, mv = sb("ebn", [P, TT, 6]), sb("emv", [P, TT, 2])
        out = a["out"].rearrange("b (t p) d -> p (b t) d", p=P)

        def finish(tile):
            y = acc[:, tile:tile + TT, :]
            m = norm_rows(pg, env, y, bn, mv, [])
            pg.dma("out", out[:, tile:tile + TT, :], y, after=[m])

        def expert(i, weight, load_next=None, last=False):
            m_w, m_d = R(f"made_w{i}"), R(f"made_wd{i}")

            def up(tg, n):
                f0, fn = FT[n]
                par = n % 2
                for bank in (0, 1):
                    for k in range(KT):
                        for a_, b_ in PARTS:
                            m = pe.op(nc.tensor.matmul, ps[0:fn, 2 * par + bank, :], w[i][a_][:, bank, k, f0:f0 + fn],
                                      env.x2T[b_][:, k, tg * TG:(tg + 1) * TG], start=(k, a_, b_) == (0, 0, 0),
                                      stop=(k, a_) == (1, 1), after=m_w + R(f"b{2 * par + bank}"), count=(k, a_) == (1, 1))
                    if bank == 0:
                        m_s = act.op(S.activation, sg[par][0:fn, :], ps[0:fn, 2 * par, :], ACT.Silu, after=[m] + R(f"sg{par}"))
                        slot(f"b{2 * par}").read(m_s)
                m_h = dve.op(V.tensor_tensor, h[par][0:fn, :], sg[par][0:fn, :], ps[0:fn, 2 * par + 1, :], ALU.mult,
                             after=[m, m_s] + R(f"h{par}"))
                slot(f"b{2 * par + 1}").read(m_h)
                slot(f"sg{par}").read(m_h)
                m_h = split(*(x_[0:fn, n, :] for x_ in hT[tg % 2]), h[par][0:fn, :], [m_h], R(f"hT{tg % 2}"))
                slot(f"h{par}").read(m_h)
                return m, m_h

            def down(tg, half, m_h):
                bank = 4 + 2 * (tg % 2) + half
                for t in range(2):
                    tile = half * 2 + t
                    for n, (f0, fn) in enumerate(FT):
                        for a_, b_ in PARTS:
                            m = pe.op(nc.tensor.matmul, ps[:, bank, t * D:(t + 1) * D],
                                      hT[tg % 2][a_][0:fn, n, tile * P:(tile + 1) * P], wd[i][b_][0:fn, n, :],
                                      start=(n, a_, b_) == (0, 0, 0), stop=(n, a_) == (2, 1),
                                      after=[m_h] + m_d + R(f"b{bank}"), count=(t, n, a_) == (1, 2, 1))
                for t in range(2):
                    tile = tg * (TG // P) + half * 2 + t
                    src, dst = ps[:, bank, t * D:(t + 1) * D], acc[:, tile, :]
                    if weight is None:
                        m2 = dve.op(V.tensor_tensor, dst, src, dst, ALU.add, after=[m])
                    else:
                        m2 = dve.op(V.scalar_tensor_tensor, out=dst, in0=src, scalar=weight(tile), in1=dst, op0=ALU.mult,
                                    op1=ALU.add, after=[m])
                slot(f"b{bank}").read(m2)
                if last:
                    finish(tg * (TG // P) + half * 2)
                return m

            NG = NTOK // TG
            marks = {}
            for tg in range(NG + 1):
                for n in range(len(FT)):
                    if tg < NG:
                        m_up, marks[tg] = up(tg, n)
                    if tg > 0 and n > 0:
                        m_dn = down(tg - 1, n - 1, marks[tg - 1])
                if tg == 0 and load_next:
                    load_next()
                if tg > 0:
                    slot(f"hT{(tg - 1) % 2}").read(m_dn)
                if tg == NG - 1:
                    slot(f"w{i}").read(m_up)
            slot(f"wd{i}").read(m_dn)

        def rows(t):
            return t.rearrange("e (k p) n -> p e k n", p=P)

        wcol = [sb(f"wcol{i}", [P, NTOK // P]) for i in range(2)]
        for i in range(2):
            slot(f"wcol{i}")

        def load_expert(i, e):
            s1 = bass.ds(e, 1)
            load(i, rows(a["exp_gate"])[:, s1].rearrange("p e k n -> p (e k) n"),
                 rows(a["exp_up"])[:, s1].rearrange("p e k n -> p (e k) n"), a["exp_down"][s1].rearrange("e f n -> (e f) n"))

        def load_shared(i):
            load(i, rows(a["sh_gate"])[:, i], rows(a["sh_up"])[:, i], a["sh_down"][i])

        def routed_expert(i, e, load_next):
            dve.op(V.tensor_copy, wcol[i][:], env.wte[:, :, bass.ds(e, 1)].rearrange("p t e -> p (t e)"))
            expert(i, lambda tile: wcol[i][:, tile:tile + 1], load_next)

        load_expert(0, 0)
        with pg.repeat("experts", NE // 2 - 1) as it:
            routed_expert(0, it * 2, lambda: load_expert(1, it * 2 + 1))
            routed_expert(1, it * 2 + 1, lambda: load_expert(0, it * 2 + 2))
        routed_expert(0, NE - 2, lambda: load_expert(1, NE - 1))
        routed_expert(1, NE - 1, lambda: load_shared(0))
        expert(0, None, lambda: load_shared(1))
        expert(1, None, last=True)
        pg.meet()


def decoder_program(nc, a, plan):
    with ExitStack() as ctx:
        pg = Program(nc, ctx, plan)

        class Env:
            pass

        env = Env()
        env.sb = lambda n, shape, dt=F32: ctx.enter_context(nc.sbuf_tensor(n, shape, dt))
        env.ps = ctx.enter_context(nc.psum_tensor("ps", [P, 8, 512], F32))
        env.tok_dram = nc.dram_tensor("tok_dram", [B, P, TT * 3 * D], F32).ap()
        env.a_dram = nc.dram_tensor("a_dram", [P, B, NP * CH], F32).ap()
        env.t_dram = nc.dram_tensor("t_dram", [2, P, B * NP, CH], F32).ap()
        env.fir_dram = nc.dram_tensor("fir_dram", [NF, NTOK, D], F32).ap()
        env.w1s_dram = nc.dram_tensor("w1s_dram", [NS * NPATH * H, HF], F32).ap()
        env.x1_dram = nc.dram_tensor("x1_dram", [B, T, D], F32).ap()
        env.beta = env.sb("beta", [P, B, NP])
        make_constants(pg, a, env)
        phase_project(pg, a, env)
        phase_invert_and_fir(pg, a, env)
        phase_delta_and_gate(pg, a, env)
        env.x2 = env.sb("x2", [P, NTOK // P, D])
        env.x2T = [env.sb(f"x2T{part}", [P, KT, NTOK], F32R) for part in ("hi", "lo")]
        env.wte = env.sb("wte", [P, NTOK // P, NE])
        phase_cross(pg, a, env)
        phase_experts(pg, a, env)
        return pg.new_plan


_NAMES = {"x": "x", "ctx": "ctx_1024"}
_NAMES |= {n: "L0_attn_" + n for n in ("Wq", "Wk", "Wv", "conv_q", "conv_k", "conv_v", "Wb", "gW1", "gb1", "gW2", "gb2",
                                       "log_tau", "eps_logit", "norm_w", "Wo")}
_NAMES |= {f"fir{i}": "L0_attn_fir_" + n for i, n in enumerate("sml")}
_NAMES |= {n: "L0_xattn_" + n for n in ("q_w", "q_b", "k_w", "k_b", "v_w", "v_b", "o_w", "o_b")}
_NAMES |= {n: "L0_ffn_" + n for n in ("gate_w", "exp_gate", "exp_up", "exp_down", "sh_gate", "sh_up", "sh_down")}


def kernel(**inputs):
    import numpy as np
    import concourse.bacc as bacc
    from concourse.bass_utils import run_bass_kernel_spmd

    arrays = {"in_" + n: np.ascontiguousarray(inputs[full]) for n, full in _NAMES.items()}

    def build(plan):
        nc = bacc.Bacc("TRN2", target_bir_lowering=False, num_devices=1)
        a = {n: nc.dram_tensor("in_" + n, arrays["in_" + n].shape, mybir.dt.from_np(arrays["in_" + n].dtype),
                               kind="ExternalInput").ap() for n in _NAMES}
        a["out"] = nc.dram_tensor("out", (B, T, D), F32, kind="ExternalOutput").ap()
        return nc, decoder_program(nc, a, plan)

    _, plan = build({})
    nc, again = build(plan)
    assert plan == again
    r = run_bass_kernel_spmd(nc, [arrays], core_ids=[0])
    return r.results[0]["out"]
```

```python
from contextlib import ExitStack, contextmanager

import concourse.bass as bass
from concourse import mybir

F32 = mybir.dt.float32
U32 = mybir.dt.uint32
F32R = mybir.dt.float32r
ALU = mybir.AluOpType
ACT = mybir.ActivationFunctionType
AX = mybir.AxisListType
ET = mybir.EngineType

P = 128
B, T, D = 8, 256, 256
KT = D // P
TT = T // P
H, DH = 4, 64
HL = P // DH
NP = TT * H
CH = 32
NCH = P // CH
TAPS = 4
FIRS = (3, 15, 64)
NF = len(FIRS)
NPATH = NF + 2
NS = 4
HF = 2 * D
BLK = 64
NBLK = T // BLK
XH, XD = 16, 16
NE, NSH, FF = 8, 2, 352
FT = [(0, 128), (128, 128), (256, 96)]
TG = 512
NTOK = B * T


class Mark:

    def __init__(self, src, index, loop, prev=False):
        self.src, self.index, self.loop, self.prev = src, index, loop, prev


class Counter:

    def __init__(self, prog, name, unit):
        self.prog, self.name, self.unit = prog, name, unit
        self.sem = prog.ctx.enter_context(prog.nc.semaphore(name))
        self.count = 0
        prog.counters.append(self)

    def tick(self, ins):
        ins.then_inc(self.sem, self.unit)
        self.count += 1
        return Mark(self, self.count, self.prog.loop)


class Slot:

    def __init__(self, prog, name):
        self.name, self.readers = name, []
        prog.slots.append(self)

    def read(self, *marks):
        self.readers = list(marks)
        return marks[-1]

    def also(self, *marks):
        self.readers += list(marks)


class Loop:
    def __init__(self, name, engines):
        self.name, self.engines, self.reg, self.base = name, engines, None, {}


class Engine:
    def __init__(self, prog, eng, name, serial):
        self.prog, self.eng, self.serial = prog, eng, serial
        self.done = Counter(prog, name, 1)
        self.seen = {}
        self.last = None

    def wait(self, marks):
        prog = self.prog
        best = {}
        for m in marks:
            if m is None:
                continue
            if isinstance(m, (list, tuple)):
                raise TypeError("flat list of marks")
            loop = m.loop
            if prog.loop is not None and loop is not prog.loop:
                if self in prog.loop.engines and not prog.loop.outside:
                    continue
            if loop is not None and prog.loop is loop:
                value = m.index - (prog.per(loop, m.src) if m.prev else 0)
                key = (m.src, loop)
            elif loop is not None:
                value, key = loop.final[m.src], (m.src, None)
            else:
                value, key = m.index, (m.src, None)
            if best.get(key, -10**9) < value:
                best[key] = value
        for (src, loop), value in best.items():
            if self.seen.get((src, loop), -10**9) >= value:
                continue
            self.seen[(src, loop)] = value
            if loop is None:
                self.eng.wait_ge(src.sem, value * src.unit)
            else:
                step = prog.per(loop, src) * src.unit
                self.eng.wait_ge(src.sem, loop.reg * step + value * src.unit)
                if self is prog.sp:
                    self.part()

    def part(self):
        if self.prog.loop is not None:
            self.eng.sem_inc(self.prog.parted, 1)

    def op(self, ins_of, *args, after=(), count=True, split=False, alone=False, **kw):
        own = [self.last] if self.serial and not alone else []
        self.wait(own + list(after))
        if split or self is self.prog.pool:
            self.part()
        ins = ins_of(*args, **kw)
        if not count:
            return None
        self.last = self.done.tick(ins)
        return self.last


class Program:
    def __init__(self, nc, ctx, plan):
        self.nc, self.ctx, self.plan, self.new_plan = nc, ctx, plan, {}
        self.counters, self.slots, self.loop = [], [], None
        self.pe = Engine(self, nc.tensor, "pe_done", False)
        self.act = Engine(self, nc.scalar, "act_done", True)
        self.dve = Engine(self, nc.vector, "dve_done", True)
        self.pool = Engine(self, nc.gpsimd, "pool_done", True)
        self.sp = Engine(self, nc.sync, "sp_done", False)
        self.engines = [self.pe, self.act, self.dve, self.pool, self.sp]
        self.dma_sems = {}
        self.parted = ctx.enter_context(nc.semaphore("parted"))

    def per(self, loop, src):
        return self.plan.get(loop.name, {}).get("per", {}).get(src.name, 1)

    def slot(self, name):
        return Slot(self, name)

    def dma(self, stream, out, in_, after=(), queue=None, **kw):
        if stream not in self.dma_sems:
            self.dma_sems[stream] = Counter(self, "dma_" + stream, 16)
        q = queue or self.sp
        q.wait(list(after))
        return self.dma_sems[stream].tick(q.eng.dma_start(out, in_, **kw))

    def meet(self, engines=None, leave=()):
        engines = engines or self.engines
        absent = [e.done for e in self.engines if e not in engines]
        for e in engines:
            e.wait([Mark(c, c.count, None) for c in self.counters
                    if c.count and c not in absent and c.name not in ["dma_" + n for n in leave]])

    @contextmanager
    def repeat(self, name, n, engines=None, leave=()):
        engines = engines or self.engines
        loop = Loop(name, engines)
        loop.outside = False
        plan = self.plan.get(name, {})
        per = plan.get("per", {})
        for c in per:
            if c.startswith("dma_") and c[4:] not in self.dma_sems:
                self.dma_sems[c[4:]] = Counter(self, c, 16)
        self.meet(engines, leave)
        owner = {e.done: e for e in self.engines}
        for c in self.counters:
            if per.get(c.name):
                (owner.get(c) or engines[-1]).eng.sem_inc(c.sem, per[c.name] * c.unit)
                c.count += per[c.name]
        names = {c.name: c for c in self.counters}
        outer = {s: s.readers for s in self.slots}
        for s in self.slots:
            s.readers = [Mark(names[c], i, loop, True) for c, i in plan.get("slots", {}).get(s.name, [])
                         if c in names]
        for s in self.slots:
            for m in s.readers:
                m.index += m.src.count
        before = {c: c.count for c in self.counters}
        for e in engines:
            e.seen, e.last = {}, None
        with self.nc.Fori(0, n, engines=tuple(e.eng.engine for e in engines)) as reg:
            loop.reg, self.loop = reg, loop
            last_marks = plan.get("last", {})
            for e in engines:
                if e.serial and e.done.name in last_marks:
                    e.last = Mark(e.done, before[e.done] + last_marks[e.done.name], loop, True)
            yield reg
        self.loop = None
        new = {"per": {}, "slots": {}, "last": {}}
        loop.final = {}
        for c in self.counters:
            start_count = before.get(c, 0)
            made = c.count - start_count
            if made:
                new["per"][c.name] = made
            if c in owner and made:
                new["last"][c.name] = made
            c.count = start_count + made * n
            loop.final[c] = c.count
        for s in self.slots:
            mine = [m for m in s.readers if m.loop is loop and not m.prev]
            if mine:
                new["slots"][s.name] = [(m.src.name, m.index - before.get(m.src, 0)) for m in mine]
            elif s in outer:
                s.readers = outer[s]
        self.new_plan[name] = new
        for e in engines:
            e.seen, e.last = {}, None


def interleave(parts):
    parts = list(parts)
    while parts:
        parts = [g for g in parts if next(g, STOP) is not STOP]


STOP = object()


def pipeline(pg, name, stages, n, leave=(), before={}):
    K = len(stages)

    def step(s, reg=0):
        interleave(stages[k](s - k + reg, (s - k) % 2) for k in range(K) if not isinstance(reg, int) or 0 <= s - k < n)

    pg.meet(leave=leave)
    for s in range(K - 1):
        if s in before:
            before[s]()
        step(s)
    pairs = (n - K + 1) // 2
    with pg.repeat(name, pairs) as it:
        for j in range(2):
            step(K - 1 + j, it * 2)
    for s in range(K - 1 + 2 * pairs, n + K - 1):
        step(s)


def make_constants(pg, a, env):
    nc, pool, dve, act, ctx = pg.nc, pg.pool, pg.dve, pg.act, pg.ctx
    sb = env.sb
    env.ident = sb("ident", [P, P])
    env.causal = sb("causal", [P, P])
    env.exponent = sb("exponent", [P, 3, 40])
    env.headmask = sb("headmask", [P, P // XD])
    env.expert_no = sb("expert_no", [P, NE])
    pool.op(nc.gpsimd.memset, env.ident[:], 0.0)
    pool.op(nc.gpsimd.affine_select, out=env.ident[:], in_=env.ident[:], compare_op=ALU.not_equal,
            fill=1.0, base=0, pattern=[[-1, P]], channel_multiplier=1)
    pool.op(nc.gpsimd.memset, env.causal[:], 1.0)
    pool.op(nc.gpsimd.affine_select, out=env.causal[:], in_=env.causal[:], compare_op=ALU.is_ge,
            fill=0.0, base=0, pattern=[[1, P]], channel_multiplier=-1)
    for k, x in enumerate((-0.5, 0.5, 2.718281828459045)):
        pool.op(nc.gpsimd.memset, env.exponent[:, k, :], x)
    pool.op(nc.gpsimd.memset, env.headmask[:], 1.0)
    pool.op(nc.gpsimd.affine_select, out=env.headmask[:], in_=env.headmask[:], compare_op=ALU.is_ge,
            fill=0.0, base=0, pattern=[[-XD, P // XD]], channel_multiplier=1)
    pool.op(nc.gpsimd.affine_select, out=env.headmask[:], in_=env.headmask[:], compare_op=ALU.is_ge,
            fill=0.0, base=XD - 1, pattern=[[XD, P // XD]], channel_multiplier=-1)
    for e in range(NE):
        pool.op(nc.gpsimd.memset, env.expert_no[:, e:e + 1], float(e))


def load_weight(pg, env, sb, name, dram, cols, stream):
    w = sb(name, [P, D // P, cols])
    m = pg.dma(stream, w[:], dram.rearrange("(k p) n -> p k n", p=P))
    return w, m


def phase_project(pg, a, env):
    nc, pe, act, dve, pool = pg.nc, pg.pe, pg.act, pg.dve, pg.pool
    V, S, G = nc.vector, nc.scalar, nc.gpsimd
    with ExitStack() as mem:
        def sb(n, shape, dt=F32):
            return mem.enter_context(nc.sbuf_tensor(n, shape, dt))
        ps = env.ps
        W = []
        for n, src in (("wq", a["Wq"]), ("wk", a["Wk"]), ("wv", a["Wv"])):
            w, m = load_weight(pg, env, sb, n, src, D, "w_project")
            W.append(w)
        wb, _ = load_weight(pg, env, sb, "wb", a["Wb"], H, "w_project")
        taps = sb("taps", [P, 3, KT, TAPS])
        for j, src in enumerate((a["conv_q"], a["conv_k"], a["conv_v"])):
            pg.dma("w_project", taps[:, j], src.rearrange("(k p) i -> p k i", p=P))

        sel = [sb(f"sel{i}", [P, NPATH, 2 * NPATH]) for i in range(2)]
        rows = [sb(f"gw1_rows{i}", [P, NPATH, HF]) for i in range(2)]
        sums = [sb(f"gw1_sums{i}", [2 * NPATH, HF]) for i in range(2)]
        for i, (lo, hi) in enumerate(((1.0 / DH, 1.0 / DH), (1.0 / DH, 1.0))):
            pool.op(G.memset, sel[i][:], 0.0)
            for n in range(NPATH):
                pool.op(G.memset, sel[i][0:DH, n, n:n + 1], lo)
                pool.op(G.memset, sel[i][DH:P, n, NPATH + n:NPATH + n + 1], hi)
        gw1_rows = a["gW1"][D:, :].rearrange("(n g p) c -> p g n c", n=NPATH, p=P)
        w1s_rows = env.w1s_dram.rearrange("(s n h) c -> s n h c", n=NPATH, h=H)

        m_zero = pool.op(nc.gpsimd.memset, env.wpad[:].rearrange("p k f n -> p (k f n)"), 0.0)
        for f, n_taps in enumerate(FIRS):
            pg.dma("wpad", env.wpad[:, :, f, P - n_taps:P], a[f"fir{f}"].rearrange("(k p) i -> p k i", p=P), after=[m_zero])
        xin = [sb(f"xin{i}", [P, TT, D]) for i in range(2)]
        xT = sb("xT", [P, KT, T])
        raw = [sb(f"raw{i}", [P, 3, KT, TAPS - 1 + T]) for i in range(2)]
        conv = [sb(f"conv{i}", [P, 3, KT, T]) for i in range(2)]
        tok = [sb(f"tok{i}", [P, TT, 3, D]) for i in range(2)]
        sq = sb("sq", [P, 2, TT, D])
        ss = sb("ss", [P, 2 * TT * H])
        rn = sb("rn", [P, 2 * TT * H])
        kT = sb("kT", [P, KT, TT, P])
        km = sb("km", [P, KT, TT, HL, P])
        diag = [sb(f"diag{i}", [P, NP, CH]) for i in range(2)]
        for i in range(2):
            dve.op(V.memset, raw[i][:], 0.0)
        dve.op(V.memset, km[:], 0.0)
        sl = {n: pg.slot("p_" + n) for n in ("xT", "sq", "ss", "rn", "kT", "km", *(f"b{k}" for k in range(8)))}
        for n in ("rows", "sums", "xin", "raw", "conv", "tok", "diag", "made_x", "made_rows", "made_conv"):
            for i in range(2):
                sl[f"{n}{i}"] = pg.slot(f"p_{n}{i}")

        def slot(n):
            return sl[n]

        def R(*names):
            return [m for n in names for m in slot(n).readers]

        def fetch(b, i):
            m = pg.dma(f"x{i}", xin[i][:], a["x"].rearrange("b (t p) d -> p b t d", p=P)[:, bass.ds(b, 1)]
                       .rearrange("p b t d -> p (b t) d"), after=R(f"xin{i}"))
            slot(f"made_x{i}").read(m)
            m = pg.dma(f"gw1_{i}", rows[i][:], gw1_rows[:, bass.ds(b, 1)].rearrange("p g n c -> p (g n) c"),
                       after=R(f"rows{i}"))
            slot(f"made_rows{i}").read(m)
            yield

        def project(b, i):
            for k in range(KT):
                for t in range(TT):
                    m = pe.op(nc.tensor.transpose, ps[:, 0, (k * TT + t) * P:(k * TT + t + 1) * P],
                              xin[i][:, t, k * P:(k + 1) * P], env.ident[:], count=(k, t) == (1, 1),
                              after=R(f"made_x{i}", "b0"))
            slot(f"xin{i}").read(m)
            m_xT = act.op(S.copy, xT[:].rearrange("p k t -> p (k t)"), ps[:, 0, :], after=[m] + R("xT"))
            slot("b0").read(m_xT)
            yield
            m_raw = []
            for j in range(3):
                for c in range(KT):
                    for k in range(KT):
                        m = pe.op(nc.tensor.matmul, ps[:, 1 + j, c * T:(c + 1) * T], W[j][:, k, c * P:(c + 1) * P],
                                  xT[:, k, :], start=(k == 0), stop=(k == KT - 1), count=(c, k) == (1, 1),
                                  after=[m_xT] + R(f"b{1 + j}"))
                m_raw.append(act.op(S.copy, raw[i][:, j, :, TAPS - 1:], ps[:, 1 + j, :].rearrange("p (c t) -> p c t", c=KT),
                                    after=[m] + R(f"raw{i}"), alone=True))
                slot(f"b{1 + j}").read(m_raw[j])
                yield
            for t in range(TT):
                for k in range(KT):
                    m = pe.op(nc.tensor.matmul, ps[:, 0, t * H:(t + 1) * H], xT[:, k, t * P:(t + 1) * P],
                              wb[:, k, :], start=(k == 0), stop=(k == KT - 1), count=(t, k) == (1, 1), after=R("b0"))
            slot("xT").read(m)
            bt = env.beta[:, bass.ds(b, 1), :].rearrange("p b n -> p (b n)")
            m = act.op(S.activation, bt, ps[:, 0, 0:NP], ACT.Tanh, scale=0.5, after=[m])
            slot("b0").read(m)
            m_beta = dve.op(V.tensor_scalar, bt, bt, 0.5, 0.5, ALU.mult, ALU.add, after=[m])
            for j in range(3):
                m_first = []
                for c in range(KT):
                    m_first.append(act.op(S.activation, conv[i][:, j, c, :], raw[i][:, j, c, 0:T], ACT.Copy,
                                          scale=taps[:, j, c, 0:1], after=[m_raw[j]] + R(f"conv{i}"), alone=True))
                for s in range(1, TAPS):
                    for c in range(KT):
                        m = dve.op(V.scalar_tensor_tensor, out=conv[i][:, j, c, :],
                                   in0=raw[i][:, j, c, s:s + T], scalar=taps[:, j, c, s:s + 1],
                                   in1=conv[i][:, j, c, :], op0=ALU.mult, op1=ALU.add,
                                   after=[m_raw[j], m_first[c]], alone=True)
                        m_first[c] = m
                yield
            slot(f"raw{i}").read(m)
            flat = conv[i][:].rearrange("p j c t -> p (j c t)")
            m_silu = act.op(S.activation, flat, flat, ACT.Silu, after=[m])
            slot(f"made_conv{i}").read(m_silu, m_beta)
            yield
            for n in range(NPATH):
                m = pe.op(nc.tensor.matmul, ps[0:2 * NPATH, 0, :], sel[i][:, n, :], rows[i][:, n, :], start=(n == 0),
                          stop=(n == NPATH - 1), count=n == NPATH - 1, after=R(f"made_rows{i}", "b0"))
            slot(f"rows{i}").read(m)
            m = dve.op(V.tensor_copy, sums[i][:], ps[0:2 * NPATH, 0, :], after=[m] + R(f"sums{i}"))
            slot("b0").read(m)
            yield
            head = b // 2 if isinstance(b, int) else b >> 1
            for lohi in range(2):
                m2 = pg.dma(f"sums{i}", w1s_rows[2 * i + lohi][:, bass.ds(head, 1), :].rearrange("n h c -> n (h c)"),
                            sums[i][lohi * NPATH:(lohi + 1) * NPATH, :], after=[m])
            slot(f"sums{i}").read(m2)
            yield

        def normalise(b, i):
            made = R(f"made_conv{i}")
            for j in range(3):
                for t in range(TT):
                    for c in range(KT):
                        m = pe.op(nc.tensor.transpose, ps[:, 4 + j, (t * KT + c) * P:(t * KT + c + 1) * P],
                                  conv[i][:, j, c, t * P:(t + 1) * P], env.ident[:], count=(t, c) == (1, 1),
                                  after=made + R(f"b{4 + j}"))
            m_t = m
            slot(f"conv{i}").read(m)
            m_sq = act.op(S.activation, sq[:].rearrange("p j t d -> p (j t d)"),
                          ps[:, 4:6, :].rearrange("p j n -> p (j n)"), ACT.Square, after=[m_t] + R("sq"))
            m_v = act.op(S.copy, tok[i][:, :, 2, :], ps[:, 6, :].rearrange("p (t d) -> p t d", t=TT),
                         after=[m_t] + R(f"tok{i}"), alone=True)
            slot("b6").read(m_v)
            yield
            m_ss = dve.op(V.tensor_reduce, ss[:], sq[:].rearrange("p j t (h d) -> p (j t h) d", h=H), AX.X, ALU.add,
                          after=[m_sq] + R("ss"))
            slot("sq").read(m_ss)
            m = pool.op(G.tensor_scalar, rn[:], ss[:], 1.0, 1e-6, ALU.mult, ALU.add, after=[m_ss] + R("rn"))
            slot("ss").read(m)
            m_rn = pool.op(G.tensor_tensor, rn[:], rn[:], env.exponent[:, 0, 0:2 * NP], ALU.pow)
            yield
            yield
            for j in range(2):
                m_tok = dve.op(V.tensor_tensor, tok[i][:, :, j, :].rearrange("p t (h d) -> p t h d", h=H),
                               ps[:, 4 + j, :].rearrange("p (t h d) -> p t h d", t=TT, h=H),
                               rn[:, j * NP:(j + 1) * NP].rearrange("p (t h) -> p t h", t=TT).unsqueeze(3)
                               .broadcast_to([P, TT, H, DH]), ALU.mult, after=[m_rn, m_t] + R(f"tok{i}"), alone=True)
            slot("rn").read(m_tok)
            slot("b4").read(m_sq, m_tok)
            slot("b5").read(m_sq, m_tok)
            m_st = pg.dma(f"tok{i}", env.tok_dram[bass.ds(b, 1)].rearrange("b p n -> p (b n)"),
                          tok[i][:].rearrange("p t j d -> p (t j d)"), after=[m_v, m_tok])
            yield
            for c in range(KT):
                for t in range(TT):
                    m = pe.op(nc.tensor.transpose, ps[:, 7, (c * TT + t) * P:(c * TT + t + 1) * P],
                              tok[i][:, t, 1, c * P:(c + 1) * P], env.ident[:], count=(c, t) == (1, 1),
                              after=[m_tok] + R("b7"))
            slot(f"tok{i}").read(m_st, m)
            yield
            m_kT = act.op(S.copy, kT[:].rearrange("p c t n -> p (c t n)"), ps[:, 7, :], after=[m] + R("kT"))
            for h in range(HL):
                q = slice(h * DH, (h + 1) * DH)
                m_km = act.op(S.copy, km[q, :, :, h, :].rearrange("p c t n -> p (c t) n"),
                              ps[q, 7, :].rearrange("p (c n) -> p c n", n=P), after=[m] + R("km"), alone=True)
            slot("b7").read(m_km)
            yield
            for c in range(KT):
                for t in range(TT):
                    n = t * H + c * HL
                    m = pe.op(nc.tensor.matmul, ps[:, 4 + n // 4, (n % 4) * P:(n % 4 + HL) * P], kT[:, c, t, :],
                              km[:, c, t, :, :], start=True, stop=True, count=(c, t) == (1, 1),
                              after=[m_kT, m_km] + R("b4", "b5"))
            slot("kT").read(m)
            slot("km").read(m)
            yield
            last = m
            for c in range(NCH):
                q = slice(c * CH, (c + 1) * CH)
                src = ps[q, 4:6, :].rearrange("p u (n j) -> p (u n) j", j=P)[:, :, q]
                m = dve.op(V.tensor_tensor, diag[i][q, :, :], src,
                           env.beta[q, bass.ds(b, 1), :].rearrange("p b n -> p (b n)").unsqueeze(2)
                           .broadcast_to([CH, NP, CH]), ALU.mult, after=[last] + made + R(f"diag{i}"), alone=True)
            slot("b4").read(m)
            slot("b5").read(m)
            m = pg.dma(f"diag{i}", env.a_dram[:, bass.ds(b, 1), :].rearrange("p b n -> p (b n)"),
                       diag[i][:].rearrange("p n j -> p (n j)"), after=[m])
            slot(f"diag{i}").read(m)
            yield

        pipeline(pg, "project", [fetch, project, normalise], B)
        pg.meet()


def phase_invert_and_fir(pg, a, env):
    nc, pe, act, dve, pool = pg.nc, pg.pe, pg.act, pg.dve, pg.pool
    G = B * NP * NCH // P
    with ExitStack() as mem:
        def sb(n, shape, dt=F32):
            return mem.enter_context(nc.sbuf_tensor(n, shape, dt))
        ps = env.ps
        stage = sb("stage", [P, NF, BLK, CH])
        am = sb("am", [P, G, CH, CH])
        inv = sb("inv", [P, G, CH, CH])
        tmp = sb("tmp", [P, G, CH, CH])
        win = sb("win", [P, B * NBLK, P])
        m_win0 = pool.op(nc.gpsimd.memset, win[0:BLK].rearrange("p n c -> p (n c)"), 0.0)


        for c in range(NCH):
            for g in range(G):
                m_am = pg.dma("am", am[c * CH:(c + 1) * CH, g],
                              env.a_dram[c * CH:(c + 1) * CH].rearrange("i b (n j) -> (b n) i j", j=CH)
                              [g * 32:(g + 1) * 32])

        dve.op(nc.vector.memset, inv[:].rearrange("p g a b -> p (g a b)"), 0.0)
        dve.op(nc.vector.memset, inv[:].rearrange("p g a b -> p g (a b)")[:, :, 0:CH * CH:CH + 1], 1.0)
        for i in range(1, CH):
            dve.op(nc.vector.tensor_tensor, tmp[:, :, 0:i, 0:i], inv[:, :, 0:i, 0:i],
                   am[:, :, i, 0:i].unsqueeze(2).broadcast_to([P, G, i, i]), ALU.mult, after=[m_am])
            dve.op(nc.vector.tensor_reduce, inv[:, :, 0:i, i], tmp[:, :, 0:i, 0:i], AX.X, ALU.add, negate=True)
        m_inv = dve.last
        for g in range(G):
            m_tr = dve.op(nc.vector.tensor_copy, am[:, g], inv[:, g].rearrange("p j i -> p i j"))

        hank = sb("hank", [P, P, NF, BLK])
        shifted = [sb(f"shifted{i}", [P, NF, P + 8]) for i in range(2)]
        s_win, s_st = pg.slot("win"), pg.slot("stage")
        s_sh = [pg.slot(f"shifted{i}") for i in range(2)]
        banks = [pg.slot(f"fir_bank{n}") for n in range(8)]
        tokv = env.tok_dram.rearrange("b p (t j d) -> j t p b d", t=TT, j=3)[2]
        for c in range(KT):
            for blk in range(NBLK):
                for half in range(2):
                    start = (blk - 1) * BLK + half * BLK
                    if start < 0:
                        continue
                    t, off = start // P, start % P
                    m_win = pg.dma("win", win[half * BLK:(half + 1) * BLK].rearrange("p (b n) c -> p n b c", n=NBLK)[:, blk],
                                   tokv[t, off:off + BLK, :, c * P:(c + 1) * P], after=[m_win0] + s_win.readers)
            with pg.repeat(f"hankel{c}", BLK // 16, engines=[pe, act, pool], leave=["am", "stage", "win"]) as it:
                for i in range(2):
                    m_s = pool.op(nc.gpsimd.tensor_copy, shifted[i][:], env.wpad[:, c, :, bass.ds(it * 16 + i * 8, P + 8)],
                                  after=s_sh[i].readers)
                    for f in range(NF):
                        for half in range(2):
                            n = f * 2 + half
                            for j in range(4):
                                m = pe.op(nc.tensor.transpose, ps[:, n, j * P:(j + 1) * P],
                                          shifted[i][:, f, half * 4 + j:half * 4 + j + P], env.ident[:], count=j == 3,
                                          after=[m_s] + banks[n].readers)
                            dst = hank[:, :, f, bass.ds(it * (-16) + (BLK - 1 - i * 8 - half * 4 - 3), 4)]
                            m = act.op(nc.scalar.copy, dst.rearrange("p c j -> p j c"),
                                       ps[:, n, :].rearrange("p (j c) -> p j c", c=P)[:, ::-1, :], after=[m], alone=True)
                            banks[n].read(m)
                    s_sh[i].read(pe.last)
            pg.meet([pe], leave=["am", "stage"])
            for pair in range(CH // 2):
                bank = pair % 8
                for u in range(2):
                    for q in range(NCH):
                        ch = q * CH + pair * 2 + u
                        m = pe.op(nc.tensor.matmul, ps[q * CH:(q + 1) * CH, bank, u * NF * BLK:(u + 1) * NF * BLK],
                                  win[:, :, ch], hank[:, ch, :, :].rearrange("p f t -> p (f t)"),
                                  start=True, stop=True, after=[m_win] + banks[bank].readers)
                m = act.op(nc.scalar.copy, stage[:].rearrange("p f t c -> p c (f t)")[:, pair * 2:pair * 2 + 2],
                           ps[:, bank, 0:2 * NF * BLK].rearrange("p (c n) -> p c n", c=2), after=[m] + s_st.readers)
                banks[bank].read(m)
            s_win.read(pe.last)
            if c == KT - 1:
                for k, (src, m_src) in enumerate(((inv, m_inv), (am, m_tr))):
                    for q in range(NCH):
                        for g in range(G):
                            pg.dma("inv", env.t_dram[k, q * CH:(q + 1) * CH].rearrange("i n j -> n i j")[g * 32:(g + 1) * 32],
                                   src[q * CH:(q + 1) * CH, g], after=[m_src])
            ms = []
            for q in range(NCH):
                for f in range(NF):
                    ms.append(pg.dma("stage", env.fir_dram[f, c * NCH + q].rearrange("(n t) d -> n (t d)", t=BLK),
                                     stage[q * CH:(q + 1) * CH, f].rearrange("p t d -> p (t d)"), after=[m]))
            s_st.read(*ms[-1:])
            env.fir_stored = ms[-1]
        pg.meet(leave=["stage"])


def phase_delta_and_gate(pg, a, env):
    nc, pe, act, dve, pool = pg.nc, pg.pe, pg.act, pg.dve, pg.pool
    with ExitStack() as mem:
        def sb(n, shape, dt=F32):
            return mem.enter_context(nc.sbuf_tensor(n, shape, dt))
        ps = env.ps
        V, S, G = nc.vector, nc.scalar, nc.gpsimd
        paths = [sb(f"paths{i}", [P, NPATH, TT, D]) for i in range(2)]
        sqs = sb("sqs", [P, NPATH, TT, D])
        tok = [sb(f"dtok{i}", [P, TT, 3, D]) for i in range(2)]
        g0 = [sb(f"g0_{i}", [P, NP, P]) for i in range(2)]
        x0 = [sb(f"x0_{i}", [P, NP, P]) for i in range(2)]
        x_gate = [sb(f"dx_gate{i}", [P, TT, D]) for i in range(2)]
        x_res = [sb(f"dx_res{i}", [P, TT, D]) for i in range(2)]
        xT = sb("dxT", [P, KT, T])
        kT = sb("dkT", [P, KT, TT, P])
        km, qm = sb("dkm", [P, KT, TT, HL, P]), sb("dqm", [P, KT, TT, HL, P])
        qT = [sb(f"dqT{i}", [P, KT, P]) for i in range(2)]
        kb = [sb(f"kb{i}", [P, TT, D]) for i in range(2)]
        vb = sb("vb", [P, TT, D])
        m1, m2 = sb("m1", [P, NP, P]), sb("m2", [P, NP, P])
        lT = [sb(f"lT{i}", [P, NP, P]) for i in range(2)]
        z = sb("z", [P, NP, P])
        x1 = sb("x1", [P, NP, P])
        gw = [sb(f"gw{i}", [P, NP, P]) for i in range(2)]
        sbd = sb("sbd", [P, KT, P])
        uT = sb("uT", [P, TT, KT, P])
        u = sb("u", [P, TT, KT, P])
        wTn = sb("wTn", [P, KT, P])
        oT = sb("oT", [P, TT, KT, P])
        st = sb("st", [P, TT, NS, NPATH, H])
        big = sb("big", [P, NPATH, TT, D])
        stT = sb("stT", [80, T])
        hid = sb("hid", [P, HF // P, T])
        lgT = sb("lgT", [H * NPATH, T])
        lg = sb("lg", [P, TT, H, NPATH])
        sos = [sb(f"so{i}", [P, NP]) for i in range(2)]
        sm, sp = sb("sm", [P, TT * H]), sb("sp", [P, TT * H])
        os_ = [sb(f"o{i}", [P, TT, D]) for i in range(2)]
        onT = sb("onT", [P, KT, T])
        y = [sb(f"y{i}", [P, TT, D]) for i in range(2)]
        bn, mv = sb("bn", [P, TT, 6]), sb("mv", [P, TT, 2])
        for t in (*g0, *x0):
            dve.op(V.memset, t[:].rearrange("p a b -> p (a b)"), 0.0)
        for t in (km, qm, m1, m2, sbd):
            pool.op(G.memset, t[:], 0.0)
        w1x = sb("w1x", [P, KT, HF])
        w1s = sb("w1s", [NS * NPATH * H, HF])
        gw2 = sb("gw2", [P, HF // P, H * NPATH])
        gb1 = sb("gb1", [P, HF // P])
        wo = sb("wo", [P, KT, D])
        nw = sb("nw", [P, 1])
        gb2 = sb("gb2", [P, H * NPATH])
        lt = sb("lt", [P, H])
        eps = sb("eps", [P, H, NPATH])
        t1, t2, itau, keep = (sb(n, [P, H]) for n in ("t1", "t2", "itau", "keep"))

        ready = []

        def parameters():
            pg.dma("w_gate", w1x[:], a["gW1"][0:D, :].rearrange("(k p) n -> p k n", p=P))
            pg.dma("w_gate", w1s[:], env.w1s_dram)
            pg.dma("w_gate", gw2[:], a["gW2"].rearrange("(k p) n -> p k n", p=P))
            pg.dma("w_gate", gb1[:], a["gb1"].rearrange("(k p) -> p k", p=P), allow_slow_non_contiguous=True)
            pg.dma("w_gate", wo[:], a["Wo"].rearrange("(k p) n -> p k n", p=P))
            for h in range(HL):
                pg.dma("w_gate", nw[h * DH:(h + 1) * DH, :], a["norm_w"].rearrange("(d o) -> d o", o=1))
            pg.dma("w_gate", gb2[:], a["gb2"].partition_broadcast(P))
            pg.dma("w_gate", lt[:], a["log_tau"].partition_broadcast(P))
            m_w = pg.dma("w_gate", eps[:].rearrange("p h n -> p (h n)"), a["eps_logit"].rearrange("h n -> (h n)").partition_broadcast(P))
            dve.op(V.tensor_scalar, wo[:].rearrange("p k n -> p (k n)"), wo[:].rearrange("p k n -> p (k n)"),
                   nw[:, 0:1], None, ALU.mult, after=[m_w])
            m = act.op(S.activation, t1[:], lt[:], ACT.Abs, after=[m_w])
            m = act.op(S.activation, t1[:], t1[:], ACT.Exp, scale=-1.0)
            m = act.op(S.activation, t1[:], t1[:], ACT.Ln, bias=1.0)
            dve.op(V.tensor_scalar, t2[:], lt[:], 0.0, 0.5, ALU.max, ALU.add)
            dve.op(V.tensor_tensor, t2[:], t2[:], t1[:], ALU.add, after=[m])
            dve.op(V.reciprocal, itau[:], t2[:])
            m = act.op(S.activation, eps[:].rearrange("p h n -> p (h n)"), eps[:].rearrange("p h n -> p (h n)"), ACT.Exp, scale=-1.0)
            dve.op(V.tensor_scalar, eps[:], eps[:], 1.0, None, ALU.add, after=[m])
            dve.op(V.reciprocal, eps[:], eps[:])
            dve.op(V.tensor_scalar, eps[:], eps[:], 0.2, None, ALU.mult)
            dve.op(V.tensor_reduce, keep[:], eps[:], AX.X, ALU.add)
            dve.op(V.tensor_scalar, keep[:], keep[:], -1.0, 1.0, ALU.mult, ALU.add)
            ready.extend([m_w, act.last, dve.last])
            load_cross_parameters(pg, a, env)

        def await_parameters():
            for e in pg.engines:
                e.wait(ready)

        sl = {}

        def slot(n):
            if n not in sl:
                sl[n] = pg.slot("d_" + n)
            return sl[n]

        for n in range(8):
            slot(f"b{n}")
        for n in ("xT", "kT", "km", "qm", "vb", "m1", "m2", "z", "x1", "sbd", "uT", "u", "wTn", "oT",
                  "st", "big", "sqs", "stT", "hid", "lgT", "lg", "sm", "sp", "onT", "bn"):
            slot(n)
        for n in ("tok", "x_gate", "x_res", "o", "so", "made_o", "made_st", "paths", "g0", "x0", "y", "kb", "lT", "qT",
                  "gw", "made_gw", "made_lT", "made_qT",
                  "made_paths"):
            for i in range(2):
                slot(f"{n}{i}")

        def R(*names):
            return [m for n in names for m in slot(n).readers]

        def flat(t):
            return t.rearrange("p a b -> p (a b)")

        def heads(t):
            return t.rearrange("p t (h d) -> p t h d", h=H)

        hs = [slice(0, DH), slice(DH, P)]

        def invert(b, i):
            s1 = bass.ds(b, 1)
            m_tok = pg.dma(f"dtok{i}", tok[i][:].rearrange("p t j d -> p (t j d)"),
                           env.tok_dram[s1].rearrange("b p n -> p (b n)"), after=R(f"tok{i}"))
            for c in range(NCH):
                q = slice(c * CH, (c + 1) * CH)
                m_g0 = pg.dma(f"g0{i}", g0[i][q, :, q], env.t_dram[0, q, bass.ds(b * NP, NP), :], after=R(f"g0{i}"))
                m_x0 = pg.dma(f"x0{i}", x0[i][q, :, q], env.t_dram[1, q, bass.ds(b * NP, NP), :], after=R(f"x0{i}"))
            bt = env.beta[:, s1, :].rearrange("p b (t h) -> p (b t) h", t=TT).unsqueeze(3).broadcast_to([P, TT, H, DH])
            m_kb = dve.op(V.tensor_tensor, heads(kb[i][:]), heads(tok[i][:, :, 1, :]), bt, ALU.mult, after=[m_tok] + R(f"kb{i}"),
                          alone=True)
            yield
            for bank in range(3):
                for c in range(KT):
                    for t in range(TT):
                        in_ = kb[i][:, t, c * P:(c + 1) * P] if bank == 1 else \
                            tok[i][:, t, 1 if bank == 0 else 0, c * P:(c + 1) * P]
                        m = pe.op(nc.tensor.transpose, ps[:, bank, (c * TT + t) * P:(c * TT + t + 1) * P], in_,
                                  env.ident[:], count=(c, t) == (1, 1), after=[m_kb if bank == 1 else m_tok] + R(f"b{bank}"))
                if bank == 1:
                    m_kT = act.op(S.copy, kT[:].rearrange("p c t n -> p (c t n)"), ps[:, 1, :], after=[m] + R("kT"), alone=True)
                    slot("b1").read(m_kT)
                else:
                    dst, nm = (km, "km") if bank == 0 else (qm, "qm")
                    for h in range(HL):
                        m_m = dve.op(V.tensor_copy, dst[hs[h], :, :, h, :].rearrange("p c t n -> p (c t) n"),
                                     ps[hs[h], bank, :].rearrange("p (c n) -> p c n", n=P), after=[m] + R(nm), alone=True)
                    if bank == 0:
                        m_km = m_m
                        slot("b0").read(m_m)
                    else:
                        m_qm = m_m
                        m_qT = act.op(S.copy, qT[i][:], ps[:, 2, :].rearrange("p (c t n) -> p c t n", c=KT, t=TT)[:, :, 1, :],
                                      after=[m, m_m] + R(f"qT{i}"), alone=True)
                        slot("b2").read(m_qT)
                        slot(f"made_qT{i}").read(m_qT)
                yield
            for c in range(KT):
                for t in range(TT):
                    n = c * HL
                    m_A = pe.op(nc.tensor.matmul, ps[:, 3 * (1 - t), n * P:(n + HL) * P], kT[:, c, t, :], km[:, c, t, :, :],
                                start=True, stop=True, after=[m_km, m_kT] + R("b3", "b0"), count=(c, t) == (1, 1))
            slot("kT").read(m_A)
            for t in range(TT):
                pa = ps[:, 3 * (1 - t), :].rearrange("p (n j) -> p n j", j=P)
                tn = slice(t * H, (t + 1) * H)
                for lo in (0, 2 * CH):
                    m_m1 = act.op(S.activation, m1[lo + CH:lo + 2 * CH, tn, lo:lo + CH], pa[lo + CH:lo + 2 * CH, :, lo:lo + CH],
                                  ACT.Copy, scale=-1.0, after=[m_A] + R("m1"), alone=True)
                m_m2 = act.op(S.activation, m2[2 * CH:P, tn, 0:2 * CH], pa[2 * CH:P, :, 0:2 * CH], ACT.Copy, scale=-1.0,
                              after=[m_A] + R("m2"), alone=True)
                slot(f"b{3 * (1 - t)}").read(m_m2)
            yield
            for t in range(TT):
                for c in range(KT):
                    for h in range(HL):
                        n = c * HL + h
                        m_L = pe.op(nc.tensor.matmul, ps[:, 1 + t, n * P:(n + 1) * P], km[:, c, t, h, :], qm[:, c, t, h, :],
                                    start=True, stop=True, after=[m_qm, m_km] + R("b1", "b2"), count=(c, h) == (1, 1))
                m_lT = dve.op(V.tensor_tensor, lT[i][:, t * H:(t + 1) * H], ps[:, 1 + t, :].rearrange("p (n j) -> p n j", j=P),
                              env.causal[:].unsqueeze(1).broadcast_to([P, H, P]), ALU.mult, after=[m_L] + R(f"lT{i}"), alone=True)
                slot(f"b{1 + t}").read(m_lT)
            slot("km").read(m_L)
            slot("qm").read(m_L)
            slot(f"made_lT{i}").read(m_lT)
            yield

            def each(lhs, rhs, banks, after, fn):
                made = []
                for u2 in range(2):
                    for n in range(4 * u2, 4 * u2 + 4):
                        out = ps[:, banks[u2], (n % 4) * P:(n % 4 + 1) * P]
                        if rhs is None:
                            m = pe.op(nc.tensor.transpose, out, lhs[:, n, :], env.ident[:], after=after[u2] + R(f"b{banks[u2]}"),
                                      count=n % 4 == 3)
                        else:
                            m = pe.op(nc.tensor.matmul, out, lhs[:, n, :], rhs[:, n, :], start=True, stop=True,
                                      after=after[u2] + R(f"b{banks[u2]}"), count=n % 4 == 3)
                    made.append(fn(ps[:, banks[u2], :], slice(4 * u2, 4 * u2 + 4), m))
                    slot(f"b{banks[u2]}").read(made[-1])
                return m, made

            def both(a_, b_=()):
                return [[x, *b_] for x in (a_ if isinstance(a_, list) else [a_, a_])]

            m, m_z = each(m1, g0[i], (3, 0), both(m_m1, [m_g0]), lambda p_, n_, m_:
                          act.op(S.copy, flat(z[:, n_]), p_, after=[m_] + R("z"), alone=True))
            slot("m1").read(m)
            yield
            m, m_g = each(x0[i], z, (1, 2), both(m_z, [m_x0]), lambda p_, n_, m_:
                          dve.op(V.tensor_tensor, flat(gw[i][:, n_]), flat(g0[i][:, n_]), p_, ALU.add, after=[m_, m_g0] + R(f"gw{i}"), alone=True))
            slot(f"x0{i}").read(m)
            slot(f"g0{i}").read(*m_g)
            slot("z").read(m)
            yield
            m, m_x1 = each(gw[i], None, (3, 0), both(m_g), lambda p_, n_, m_:
                           act.op(S.copy, flat(x1[:, n_]), p_, after=[m_] + R("x1"), alone=True))
            m, m_z = each(m2, gw[i], (1, 2), both(m_g, [m_m2]), lambda p_, n_, m_:
                          act.op(S.copy, flat(z[:, n_]), p_, after=[m_] + R("z"), alone=True))
            slot("m2").read(m)
            yield
            m, m_g = each(x1, z, (3, 0), [[m_z[u_], m_x1[u_]] for u_ in range(2)], lambda p_, n_, m_:
                          dve.op(V.tensor_tensor, flat(gw[i][:, n_]), flat(gw[i][:, n_]), p_, ALU.add, after=[m_]))
            slot("z").read(m)
            slot("x1").read(m)
            slot(f"made_gw{i}").read(*m_g)
            yield

        def states(b, i):
            s1 = bass.ds(b, 1)
            bt = env.beta[:, s1, :].rearrange("p b (t h) -> p (b t) h", t=TT).unsqueeze(3).broadcast_to([P, TT, H, DH])
            m_vb = dve.op(V.tensor_tensor, heads(vb[:]), heads(tok[i][:, :, 2, :]), bt, ALU.mult,
                          after=R("vb", f"made_gw{i}", f"made_lT{i}", f"made_qT{i}"))
            made = R(f"made_gw{i}", f"made_lT{i}", f"made_qT{i}")
            yield

            def beta_v(t, c, h):
                n = t * H + c * HL + h
                return pe.op(nc.tensor.matmul, ps[hs[h], 4, c * P:(c + 1) * P],
                             vb[:, t, (c * HL + h) * DH:(c * HL + h + 1) * DH], gw[i][:, n, :], start=True,
                             stop=(t == 0), after=made + [m_vb] + R("b4"), skip_group_check=True, count=h == 1)

            for c in range(KT):
                for h in range(HL):
                    m_u0 = beta_v(0, c, h)
            for c in range(KT):
                for h in range(HL):
                    m = pe.op(nc.tensor.matmul, ps[hs[h], 5, c * P:(c + 1) * P],
                              kb[i][:, 1, (c * HL + h) * DH:(c * HL + h + 1) * DH], gw[i][:, H + c * HL + h, :], start=True,
                              stop=True, after=R("b5"), count=(c, h) == (1, 1))
            slot(f"kb{i}").read(m)
            m_wT = act.op(S.activation, flat(wTn[:]), ps[:, 5, 0:KT * P], ACT.Copy, scale=-1.0, after=[m] + R("wTn"))
            slot("b5").read(m_wT)
            m_uT = dve.op(V.tensor_copy, flat(uT[:, 0]), ps[:, 4, 0:KT * P], after=[m_u0] + R("uT"), alone=True)
            slot("b4").read(m_uT)
            yield
            for c in range(KT):
                m = pe.op(nc.tensor.transpose, ps[:, 5, c * P:(c + 1) * P], uT[:, 0, c, :], env.ident[:], after=[m_uT] + R("b5"))
            m_u = act.op(S.copy, flat(u[:, 0]), ps[:, 5, 0:KT * P], after=[m] + R("u"), alone=True)
            slot("b5").read(m_u)
            yield
            for c in range(KT):
                m = pe.op(nc.tensor.matmul, ps[:, 5, c * P:(c + 1) * P], tok[i][:, 0, 1, c * P:(c + 1) * P], u[:, 0, c, :],
                          start=True, stop=True, after=[m_u] + R("b5"))
            m_k = m
            for h in range(HL):
                m_s = dve.op(V.tensor_copy, sbd[hs[h], :, hs[h]],
                             ps[hs[h], 5, 0:KT * P].rearrange("p (c n) -> p c n", c=KT)[:, :, hs[h]], after=[m] + R("sbd"), alone=True)
            slot("b5").read(m_s)
            yield
            for c in range(KT):
                for h in range(HL):
                    beta_v(1, c, h)
                m = pe.op(nc.tensor.matmul, ps[:, 4, c * P:(c + 1) * P], sbd[:, c, :], wTn[:, c, :],
                          start=False, stop=True, after=[m_s, m_wT], skip_group_check=True)
            slot("wTn").read(m)
            slot("vb").read(m)
            slot(f"gw{i}").read(m)
            m_uT = dve.op(V.tensor_copy, flat(uT[:, 1]), ps[:, 4, 0:KT * P], after=[m] + R("uT"), alone=True)
            slot("b4").read(m_uT)
            yield
            for c in range(KT):
                m = pe.op(nc.tensor.transpose, ps[:, 5, c * P:(c + 1) * P], uT[:, 1, c, :], env.ident[:], after=[m_uT] + R("b5"))
            slot("uT").read(m)
            m_u = act.op(S.copy, flat(u[:, 1]), ps[:, 5, 0:KT * P], after=[m] + R("u"), alone=True)
            slot("b5").read(m_u)
            yield
            for t in range(TT):
                for c in range(KT):
                    if t:
                        pe.op(nc.tensor.matmul, ps[:, 4, (t * KT + c) * P:(t * KT + c + 1) * P], sbd[:, c, :], qT[i][:, c, :],
                              start=True, stop=False, after=[m_u] + R("b4"), count=False, skip_group_check=True)
                    for h in range(HL):
                        n = t * H + c * HL + h
                        m = pe.op(nc.tensor.matmul, ps[hs[h], 4, (t * KT + c) * P:(t * KT + c + 1) * P],
                                  u[:, t, c, hs[h]], lT[i][:, n, :], start=(t == 0), stop=True, after=[m_u] + R("b4"),
                                  skip_group_check=True, count=(t, c, h) == (1, 1, 1))
            for nm in ("u", f"lT{i}", f"qT{i}", "sbd"):
                slot(nm).read(m)
            m_oT = act.op(S.copy, oT[:].rearrange("p t c n -> p (t c n)"), ps[:, 4, :], after=[m] + R("oT"), alone=True)
            slot("b4").read(m_oT)
            yield
            for f in range(NF):
                for t in range(TT):
                    m_fir = pg.dma(f"fir{i}", paths[i][:, f, t, :].rearrange("p (k c) -> p k c", c=CH),
                                   env.fir_dram[f].rearrange("k (n p) c -> p n k c", p=P)[:, bass.ds(b * TT + t, 1)]
                                   .rearrange("p n k c -> p (n k) c"), after=R(f"paths{i}"))
            m_v5 = act.op(S.copy, paths[i][:, NPATH - 1], tok[i][:, :, 2, :], after=R(f"paths{i}") + made, alone=True)
            slot(f"tok{i}").read(m_k, m_v5, m_vb)
            for t in range(TT):
                for c in range(KT):
                    m = pe.op(nc.tensor.transpose, ps[:, 5, (t * KT + c) * P:(t * KT + c + 1) * P], oT[:, t, c, :],
                              env.ident[:], after=[m_oT] + R("b5"), count=(t, c) == (1, 1))
            slot("oT").read(m)
            m_dl = act.op(S.copy, paths[i][:, NF].rearrange("p t d -> p (t d)"), ps[:, 5, :], after=[m] + R(f"paths{i}"), alone=True)
            slot("b5").read(m_dl)
            slot(f"made_paths{i}").read(m_fir, m_v5, m_dl)
            yield

        def per_head(t):
            return t.unsqueeze(1).unsqueeze(3).broadcast_to([P, TT, H, NPATH])

        def statistics(b, i):
            m_r = pg.dma(f"dx_gate{i}", x_gate[i][:], a["x"].rearrange("b (t p) d -> p b t d", p=P)[:, bass.ds(b, 1)]
                         .rearrange("p b t d -> p (b t) d"), after=R(f"x_gate{i}"))
            made = R(f"made_paths{i}")

            def stat(s, t, src, **kw):
                return dve.op(V.tensor_reduce, st[:, t, s], src[:, :, t, :].rearrange("p n (h d) -> p n h d", h=H), AX.X,
                              ALU.add, alone=True, **kw)

            def norm(t, m):
                return pool.op(G.tensor_tensor, st[:, t, 3].rearrange("p n h -> p (n h)"), st[:, t, 1].rearrange("p n h -> p (n h)"),
                               env.exponent[:, 1, 0:NPATH * H], ALU.pow, after=[m])

            yield
            m_sq = act.op(S.activation, sqs[:].rearrange("p n t d -> p (n t d)"), paths[i][:].rearrange("p n t d -> p (n t d)"),
                          ACT.Square, after=made + R("sqs"), alone=True)
            stat(0, 0, paths[i], after=made + R("st"))
            yield
            norm(0, stat(1, 0, sqs, after=[m_sq]))
            yield
            m = stat(1, 1, sqs)
            slot("sqs").read(m)
            m_st = norm(1, m)
            yield
            stat(0, 1, paths[i])
            yield
            stat(2, 0, paths[i], apply_absolute_value=True)
            yield
            yield
            m_abs = stat(2, 1, paths[i], apply_absolute_value=True)
            slot(f"made_st{i}").read(m_st, m_abs, m_r)
            yield

        def gate(b, i):
            m_r = pg.dma(f"dx_res{i}", x_res[i][:], a["x"].rearrange("b (t p) d -> p b t d", p=P)[:, bass.ds(b, 1)]
                         .rearrange("p b t d -> p (b t) d"), after=R(f"x_res{i}"))
            o = os_[i]
            made = R(f"made_st{i}")
            for c in range(KT):
                for t in range(TT):
                    m = pe.op(nc.tensor.transpose, ps[:, 6, (c * TT + t) * P:(c * TT + t + 1) * P], x_gate[i][:, t, c * P:(c + 1) * P],
                              env.ident[:], count=(c, t) == (1, 1), after=made + R("b6"))
            m_xT = act.op(S.copy, flat(xT[:]), ps[:, 6, :], after=[m] + R("xT"), alone=True)
            slot("b6").read(m_xT)
            slot(f"x_gate{i}").read(m)
            for t in range(TT):
                m = pe.op(nc.tensor.transpose, ps[0:80, 7, t * P:(t + 1) * P], st[:, t].rearrange("p s n h -> p (s n h)"), env.ident[:],
                          after=made + R("b7"), count=t == 1)
            slot("st").read(m)
            m_stT = act.op(S.copy, stT[:], ps[0:80, 7, 0:T], after=[m] + R("stT"), alone=True)
            slot("b7").read(m_stT)
            yield
            for c in range(HF // P):
                bank = 6 + c // 2
                for k in range(KT + 1):
                    l_ = w1x[:, k, c * P:(c + 1) * P] if k < KT else w1s[:, c * P:(c + 1) * P]
                    r_ = xT[:, k, :] if k < KT else stT[:]
                    m = pe.op(nc.tensor.matmul, ps[:, bank, (c % 2) * T:(c % 2 + 1) * T], l_, r_, start=(k == 0),
                              stop=(k == KT), after=[m_xT] + ([m_stT] if k == KT else []) + R(f"b{bank}"), count=k == KT)
                if c % 2:
                    for e in (c - 1, c):
                        m_h = act.op(S.activation, hid[:, e, :], ps[:, bank, (e % 2) * T:(e % 2 + 1) * T], ACT.Gelu,
                                     bias=gb1[:, e:e + 1], after=[m] + R("hid"), alone=True)
                    slot(f"b{bank}").read(m_h)
                    yield
            slot("xT").read(m)
            slot("stT").read(m)
            for c in range(HF // P):
                m = pe.op(nc.tensor.matmul, ps[0:H * NPATH, 6, 0:T], gw2[:, c, :], hid[:, c, :], start=(c == 0),
                          stop=(c == HF // P - 1), after=[m_h] + R("b6"), count=c == 3)
            slot("hid").read(m)
            m = act.op(S.copy, lgT[:], ps[0:H * NPATH, 6, 0:T], after=[m] + R("lgT"))
            slot("b6").read(m)
            yield
            for t in range(TT):
                m2_ = pe.op(nc.tensor.transpose, ps[:, 7, t * H * NPATH:(t + 1) * H * NPATH], lgT[:, t * P:(t + 1) * P],
                            env.ident[0:H * NPATH, 0:H * NPATH], split=True, after=[m] + R("b7"), count=t == 1)
            slot("lgT").read(m2_)
            lf = lg[:].rearrange("p t h n -> p t (h n)")
            m = dve.op(V.tensor_tensor, lf, ps[:, 7, 0:TT * H * NPATH].rearrange("p (t n) -> p t n", t=TT),
                       gb2[:].unsqueeze(1).broadcast_to([P, TT, H * NPATH]), ALU.add, after=[m2_] + R("lg"))
            slot("b7").read(m)
            lh = lg[:].rearrange("p t h n -> p (t h) n")

            dve.op(V.tensor_tensor, lg[:], lg[:], per_head(itau[:]), ALU.mult)
            dve.op(V.tensor_reduce, sm[:], lh, AX.X, ALU.max, after=R("sm"))
            m = dve.op(V.tensor_tensor, lh, lh, sm[:].unsqueeze(2).broadcast_to([P, NP, NPATH]), ALU.subtract)
            lw = lg[:].rearrange("p t h n -> p (t h n)")
            m = act.op(S.activation, lw, lw, ACT.Exp, after=[m])
            slot("sm").read(m)
            yield
            dve.op(V.tensor_reduce, sp[:], lh, AX.X, ALU.add, after=[m] + R("sp"))
            dve.op(V.reciprocal, sp[:], sp[:])
            dve.op(V.tensor_tensor, lh, lh, sp[:].unsqueeze(2).broadcast_to([P, NP, NPATH]), ALU.mult)
            dve.op(V.tensor_tensor, lg[:], lg[:], per_head(keep[:]), ALU.mult)
            m_pr = dve.op(V.tensor_tensor, lg[:], lg[:], eps[:].unsqueeze(1).broadcast_to([P, TT, H, NPATH]), ALU.add)
            slot("sp").read(m_pr)

            def weighed(E, eng, n):
                return E.op(eng.tensor_tensor, big[:, n].rearrange("p t (h d) -> p (t h) d", h=H),
                            paths[i][:, n].rearrange("p t (h d) -> p (t h) d", h=H),
                            lh[:, :, n:n + 1].broadcast_to([P, NP, DH]), ALU.mult, after=[m_pr] + R("big"), alone=True)

            def path(n):
                return big[:, n].rearrange("p t d -> p (t d)")

            weighed(pool, G, 3)
            weighed(pool, G, 4)
            m_p = pool.op(G.tensor_tensor, path(3), path(3), path(4), ALU.add)
            for n in range(NF):
                m = weighed(dve, V, n)
            slot("lg").read(m, m_p)
            slot(f"paths{i}").read(m, m_p)
            yield
            dve.op(V.tensor_tensor, path(0), path(0), path(1), ALU.add)
            dve.op(V.tensor_tensor, path(0), path(0), path(2), ALU.add)
            m_o = dve.op(V.tensor_tensor, flat(o[:]), path(0), path(3), ALU.add, after=[m_p] + R(f"o{i}"))
            m = act.op(S.activation, path(0), flat(o[:]), ACT.Square, after=[m_o])
            yield
            so = sos[i]
            m = dve.op(V.tensor_reduce, so[:], big[:, 0].rearrange("p t (h d) -> p (t h) d", h=H), AX.X, ALU.add, after=[m] + R(f"so{i}"))
            slot("big").read(m)
            m = pool.op(G.tensor_scalar, so[:], so[:], 1.0 / DH, 1e-5, ALU.mult, ALU.add, after=[m])
            m = pool.op(G.tensor_tensor, so[:], so[:], env.exponent[:, 0, 0:NP], ALU.pow)
            slot(f"made_o{i}").read(m, m_r)
            yield

        def project_out(b, i):
            made, o, so = R(f"made_o{i}"), os_[i], sos[i]
            of = o[:].rearrange("p t (h d) -> p (t h) d", h=H)
            m_on = dve.op(V.tensor_tensor, of, of, so[:].unsqueeze(2).broadcast_to([P, NP, DH]), ALU.mult, after=made)
            slot(f"so{i}").read(m_on)
            yield
            for c in range(KT):
                for t in range(TT):
                    m = pe.op(nc.tensor.transpose, ps[:, 6, (c * TT + t) * P:(c * TT + t + 1) * P], o[:, t, c * P:(c + 1) * P],
                              env.ident[:], after=[m_on] + R("b6"), count=(c, t) == (1, 1))
            slot(f"o{i}").read(m)
            m_onT = act.op(S.copy, flat(onT[:]), ps[:, 6, :], after=[m] + R("onT"))
            slot("b6").read(m_onT)
            yield
            for t in range(TT):
                for k in range(KT):
                    m = pe.op(nc.tensor.matmul, ps[:, 7, t * D:(t + 1) * D], onT[:, k, t * P:(t + 1) * P], wo[:, k, :],
                              start=(k == 0), stop=(k == 1), after=[m_onT] + R("b7"), count=(t, k) == (1, 1))
            slot("onT").read(m)
            m = dve.op(V.tensor_tensor, flat(y[i][:]), ps[:, 7, :], flat(x_res[i][:]), ALU.add, after=[m] + R(f"y{i}"))
            slot("b7").read(m)
            slot(f"x_res{i}").read(m)
            yield
            m = yield from norm_rows(pg, env, y[i], bn, mv, [m] + R("bn"))
            slot("bn").read(m)
            m = pg.dma(f"x1_{i}", env.x1_dram.rearrange("b (t p) d -> p b t d", p=P)[:, bass.ds(b, 1)]
                       .rearrange("p b t d -> p (b t) d"), y[i][:], after=[m])
            slot(f"y{i}").read(m)
            yield

        for n in ("paths0", "paths1", "sqs"):
            slot(n).read(env.fir_stored)
        pipeline(pg, "delta", [invert, states, statistics, gate, project_out], B, leave=["stage"],
                 before={1: parameters, 3: await_parameters})
        pg.meet()


def norm_rows(pg, env, y, bn, mv, after):
    nc, dve, pool = pg.nc, pg.dve, pg.pool
    for t in range(TT):
        dve.op(nc.vector.bn_stats, bn[:, t, :], y[:, t, :], after=after)
        dve.op(nc.vector.bn_aggr, mv[:, t, :], bn[:, t, :], split=True)
    m = pool.op(nc.gpsimd.tensor_scalar, mv[:, :, 1], mv[:, :, 1], 1.0, 1e-5, ALU.mult, ALU.add, after=[dve.last])
    m_rstd = pool.op(nc.gpsimd.tensor_tensor, mv[:, :, 1], mv[:, :, 1], env.exponent[:, 0, 0:TT], ALU.pow)
    yield
    for t in range(TT):
        m = dve.op(nc.vector.tensor_scalar, y[:, t, :], y[:, t, :], mv[:, t, 0:1], mv[:, t, 1:2], ALU.subtract, ALU.mult,
                   after=[m_rstd], alone=t > 0)
    return m


def place_cross_parameters(env):
    env.Wx = {n: env.sb("x" + n, [P, KT, D]) for n in ("q_w", "k_w", "v_w", "o_w")}
    env.gate_w = env.sb("gate_w", [P, KT, NE])
    env.bq, env.bk = env.sb("bq", [P, KT]), env.sb("bk", [P, KT])
    env.bv, env.bo = env.sb("bv", [P, D]), env.sb("bo", [P, D])


def load_cross_parameters(pg, a, env):
    after = [env.fir_stored]
    for w, n in [(env.Wx[n], n) for n in env.Wx] + [(env.gate_w, "gate_w")]:
        pg.dma("w_cross", w[:], a[n].rearrange("(k p) n -> p k n", p=P), after=after)
    for w, n in ((env.bq, "q_b"), (env.bk, "k_b")):
        pg.dma("w_cross", w[:], a[n].rearrange("(k p) -> p k", p=P), after=after, allow_slow_non_contiguous=True)
    for w, n in ((env.bv, "v_b"), (env.bo, "o_b")):
        pg.dma("w_cross", w[:], a[n].partition_broadcast(P), after=after)


def phase_cross(pg, a, env):
    nc, pe, act, dve, pool = pg.nc, pg.pe, pg.act, pg.dve, pg.pool
    V, S, G = nc.vector, nc.scalar, nc.gpsimd
    HT = P // XD
    with ExitStack() as mem:
        def sb(n, shape, dt=F32):
            return mem.enter_context(nc.sbuf_tensor(n, shape, dt))
        ps = env.ps
        Wx, gate_w, bq, bk, bv, bo = env.Wx, env.gate_w, env.bq, env.bk, env.bv, env.bo
        xin = [sb(f"cx{i}", [P, TT, D]) for i in range(2)]
        cin = [sb(f"cc{i}", [P, TT, D]) for i in range(2)]
        xT, cT = sb("cxT", [P, KT, T]), sb("ccT", [P, KT, T])
        x_res = [sb(f"cxr{i}", [P, TT, D]) for i in range(2)]
        qT, kT = [sb(f"cqT{i}", [P, KT, T]) for i in range(2)], sb("ckT", [P, KT, T])
        km = [sb(f"ckm{i}", [P, XH, T]) for i in range(2)]
        vv = [sb(f"vv{i}", [P, TT, XH, CH]) for i in range(2)]
        pr = [sb(f"pr{i}", [P, TT, 2, T]) for i in range(3)]
        pT = [sb(f"pT{i}", [P, 2, TT, T]) for i in range(2)]
        mx = sb("mx", [P, TT, XH])
        oTs = [sb(f"coT{i}", [P, XH // 4, T]) for i in range(2)]
        rs = sb("rs", [P, TT, XH])
        o = sb("co", [P, TT, D])
        onT = sb("conT", [P, KT, T])
        y = [sb(f"cy{i}", [P, TT, D]) for i in range(2)]
        bn, mv = sb("cbn", [P, TT, 6]), sb("cmv", [P, TT, 2])
        lgT = sb("clgT", [NE, T])
        lg = sb("clg", [P, TT, NE])
        top = sb("top", [P, TT, 8])
        ti = sb("ti", [P, TT, 8], U32)
        tif = sb("tif", [P, TT, 8])
        wsel = sb("wsel", [P, TT, 2])
        tmp = sb("ctmp", [P, TT, NE])
        for i in range(2):
            pool.op(G.memset, vv[i][:], 1.0)
        sl = {}

        def slot(n):
            if n not in sl:
                sl[n] = pg.slot("c_" + n)
            return sl[n]

        for n in range(8):
            slot(f"b{n}")
        for n in ("xT", "cT", "kT", "mx", "rs", "o", "onT", "bn", "lgT", "lg", "top", "tmp"):
            slot(n)
        for n in ("xin", "cin", "x_res", "qT", "oT", "km", "vv", "pr", "pT", "y", "made_qkv", "made_oT", "made_x"):
            for i in range(3):
                slot(f"{n}{i}")

        def R(*names):
            return [m for n in names for m in slot(n).readers]

        def flat(t):
            return t.rearrange("p a b -> p (a b)")

        SHARED = 7

        def keys(b, i):
            s1 = bass.ds(b, 1)
            m_c = pg.dma(f"cc{i}", cin[i][:], a["ctx"].rearrange("b (t p) d -> p b t d", p=P)[:, s1]
                         .rearrange("p b t d -> p (b t) d"), after=R(f"cin{i}"))
            m_x = pg.dma(f"cx{i}", xin[i][:], env.x1_dram.rearrange("b (t p) d -> p b t d", p=P)[:, s1]
                         .rearrange("p b t d -> p (b t) d"), after=R(f"xin{i}"))
            bank = ps[:, SHARED, :]

            def turned_in(src, dst, nm, nm_in, m_in):
                for c in range(KT):
                    for t in range(TT):
                        m = pe.op(nc.tensor.transpose, bank[:, (c * TT + t) * P:(c * TT + t + 1) * P],
                                  src[:, t, c * P:(c + 1) * P], env.ident[:], after=[m_in] + R("b7"), count=(c, t) == (1, 1))
                slot(nm_in).read(m)
                m = act.op(S.copy, flat(dst[:]), bank, after=[m] + R(nm))
                slot("b7").read(m)
                return m

            def projected(w, src, dst, nm, bias, scale, m_in):
                for c in range(KT):
                    for k in range(KT):
                        m = pe.op(nc.tensor.matmul, bank[:, c * T:(c + 1) * T], Wx[w][:, k, c * P:(c + 1) * P],
                                  src[:, k, :], start=(k == 0), stop=(k == 1), after=[m_in] + R("b7"), count=(c, k) == (1, 1))
                for c in range(KT):
                    m_e = dve.op(V.tensor_scalar, dst[:, c, :], bank[:, c * T:(c + 1) * T], bias[:, c:c + 1], scale,
                                 ALU.add, ALU.mult, after=[m] + R(nm), alone=True)
                slot("b7").read(m_e)
                return m, m_e

            m_cT = turned_in(cin[i], cT, "cT", f"cin{i}", m_c)
            yield
            m, m_kT = projected("k_w", cT, kT, "kT", bk, 1.0, m_cT)
            yield
            for h in range(XH):
                m_km = pool.op(G.tensor_scalar, km[i][:, h, :], kT[:, h // HT, :], env.headmask[:, h % HT:h % HT + 1], 1.0,
                               ALU.mult, ALU.mult, after=[m_kT] + R(f"km{i}"))
            slot("kT").read(m_km)
            yield
            for t in range(TT):
                for k in range(KT):
                    m = pe.op(nc.tensor.matmul, bank[:, t * D:(t + 1) * D], cT[:, k, t * P:(t + 1) * P],
                              Wx["v_w"][:, k, :], start=(k == 0), stop=(k == 1), after=R("b7"), count=(t, k) == (1, 1))
            slot("cT").read(m)
            for t in range(TT):
                m_v = dve.op(V.tensor_tensor, vv[i][:, t, :, 0:XD], bank[:, t * D:(t + 1) * D].rearrange("p (h d) -> p h d", h=XH),
                             bv[:].rearrange("p (h d) -> p h d", h=XH), ALU.add, after=[m] + R(f"vv{i}"))
            slot("b7").read(m_v)
            yield
            m_xT = turned_in(xin[i], xT, "xT", f"xin{i}", m_x)
            yield
            m, m_qT = projected("q_w", xT, qT[i], f"qT{i}", bq, float(XD) ** -0.5, m_xT)
            slot("xT").read(m)
            slot(f"made_qkv{i}").read(m_km, m_v, m_qT)
            yield

        def attend(b, i):
            m_r = pg.dma(f"cxr{i}", x_res[i][:], env.x1_dram.rearrange("b (t p) d -> p b t d", p=P)[:, bass.ds(b, 1)]
                         .rearrange("p b t d -> p (b t) d"), after=R(f"x_res{i}"))
            slot(f"made_x{i}").read(m_r)
            made = R(f"made_qkv{i}")
            NPAIR = XH // 2
            expd, turned = {}, {}

            def scores(g):
                for t in range(TT):
                    bank = (2 * g + t) % 3
                    m_s = pe.op(nc.tensor.matmul, ps[:, bank, :], qT[i][:, (2 * g) // HT, t * P:(t + 1) * P],
                                flat(km[i][:, 2 * g:2 * g + 2, :]), start=True, stop=True, after=made + R(f"b{bank}"))
                    m_mx = dve.op(V.tensor_reduce, mx[:, t, 2 * g:2 * g + 2], ps[:, bank, :].rearrange("p (h k) -> p h k", h=2),
                                  AX.X, ALU.max, negate=True, after=[m_s] + R("mx"), alone=True)
                    for h in range(2):
                        m = act.op(S.activation, pr[g % 3][:, t, h, :], ps[:, bank, h * T:(h + 1) * T], ACT.Exp,
                                   bias=mx[:, t, 2 * g + h:2 * g + h + 1], after=[m_mx] + R(f"pr{g % 3}"), alone=True)
                    slot(f"b{bank}").read(m)
                expd[g] = m
                return m_s

            def turn(g):
                for h in range(2):
                    for kt_ in range(TT):
                        for t in range(TT):
                            m = pe.op(nc.tensor.transpose, ps[:, 3 + h, (kt_ * TT + t) * P:(kt_ * TT + t + 1) * P],
                                      pr[g % 3][:, t, h, kt_ * P:(kt_ + 1) * P], env.ident[:],
                                      after=[expd[g]] + R(f"b{3 + h}"), count=(kt_, t) == (1, 1))
                    E, fn = (act, S.copy) if h == 0 else (dve, V.tensor_copy)
                    m_e = E.op(fn, pT[g % 2][:, h].rearrange("p k t -> p (k t)"), ps[:, 3 + h, :], after=[m] + R(f"pT{g % 2}"),
                               alone=True)
                    slot(f"b{3 + h}").read(m_e)
                    turned[g, h] = m_e
                slot(f"pr{g % 3}").read(m)

            def values(g):
                for h in range(2):
                    head = 2 * g + h
                    for k in range(TT):
                        q4 = head % 4
                        m = pe.op(nc.tensor.matmul, ps[q4 * CH:(q4 + 1) * CH, 5 + head // 8, (head // 4 % 2) * T:(head // 4 % 2 + 1) * T],
                                  vv[i][:, k, head, :], pT[g % 2][:, h, k, :], start=(k == 0), stop=(k == 1),
                                  after=[turned[g, 0], turned[g, 1]] + R("b5", "b6"), skip_group_check=True,
                                  count=(h, k) == (1, 1))
                slot(f"pT{g % 2}").read(m)
                return m

            for g in range(NPAIR + 2):
                if g < NPAIR:
                    m_s = scores(g)
                if 1 <= g <= NPAIR:
                    turn(g - 1)
                if g >= 2:
                    m = values(g - 2)
                yield
            slot("mx").read(expd[NPAIR - 1])
            slot(f"km{i}").read(m_s)
            slot(f"qT{i}").read(m_s)
            slot(f"vv{i}").read(m)
            m_oT = act.op(S.copy, oTs[i][:].rearrange("p g t -> p (g t)"), ps[:, 5:7, :].rearrange("p u n -> p (u n)"),
                          after=[m] + R(f"oT{i}"))
            slot("b5").read(m_oT)
            slot("b6").read(m_oT)
            slot(f"made_oT{i}").read(m_oT)
            yield

        def output(b, i):
            bank = ps[:, SHARED, :]
            made = R(f"made_oT{i}")
            for t in range(TT):
                for g in range(XH // 4):
                    m = pe.op(nc.tensor.transpose, bank[:, g * P:(g + 1) * P], oTs[i][:, g, t * P:(t + 1) * P], env.ident[:],
                              after=made + R("b7"), count=g == 3)
                src = bank.rearrange("p (h d) -> p h d", h=XH)
                dve.op(V.reciprocal, rs[:, t, :], src[:, :, XD], after=[m])
                m_o = dve.op(V.tensor_tensor, o[:, t, :].rearrange("p (h d) -> p h d", h=XH), src[:, :, 0:XD],
                             rs[:, t, :].unsqueeze(2).broadcast_to([P, XH, XD]), ALU.mult, after=R("o"))
                slot("b7").read(m_o)
                if t == 0:
                    yield
            slot(f"oT{i}").read(m)
            yield
            for c in range(KT):
                for t in range(TT):
                    m = pe.op(nc.tensor.transpose, bank[:, (c * TT + t) * P:(c * TT + t + 1) * P], o[:, t, c * P:(c + 1) * P],
                              env.ident[:], after=[m_o] + R("b7"), count=(c, t) == (1, 1))
            slot("o").read(m)
            m_onT = act.op(S.copy, flat(onT[:]), bank, after=[m] + R("onT"))
            slot("b7").read(m_onT)
            yield
            for t in range(TT):
                for k in range(KT):
                    m = pe.op(nc.tensor.matmul, bank[:, t * D:(t + 1) * D], onT[:, k, t * P:(t + 1) * P], Wx["o_w"][:, k, :],
                              start=(k == 0), stop=(k == 1), after=[m_onT] + R("b7"), count=(t, k) == (1, 1))
            slot("onT").read(m)
            m_y = dve.op(V.tensor_tensor, flat(y[i][:]), bank, flat(x_res[i][:]), ALU.add, after=[m] + R(f"y{i}", f"made_x{i}"))
            slot("b7").read(m_y)
            slot(f"x_res{i}").read(m_y)
            dve.op(V.tensor_tensor, y[i][:], y[i][:], bo[:].unsqueeze(1).broadcast_to([P, TT, D]), ALU.add)
            m_y = yield from norm_rows(pg, env, y[i], bn, mv, R("bn"))
            slot("bn").read(m_y)
            m_y2 = pool.op(G.tensor_copy, env.x2[:, bass.ds(b * TT, TT), :], y[i][:], after=[m_y])
            yield
            for c in range(KT):
                for t in range(TT):
                    m = pe.op(nc.tensor.transpose, bank[:, (c * TT + t) * P:(c * TT + t + 1) * P], y[i][:, t, c * P:(c + 1) * P],
                              env.ident[:], after=[m_y] + R("b7"), count=(c, t) == (1, 1))
            slot(f"y{i}").read(m, m_y2)
            m_2T = act.op(S.copy, flat(onT[:]), bank, after=[m] + R("onT"))
            slot("b7").read(m_2T)
            hi, lo = (x_[:, :, bass.ds(b * T, T)] for x_ in env.x2T)
            m = act.op(S.copy, hi, onT[:])
            m_lo = pool.op(G.tensor_tensor, lo, onT[:], hi, ALU.subtract, after=[m])
            yield
            for k in range(KT):
                m = pe.op(nc.tensor.matmul, ps[0:NE, SHARED, 0:T], gate_w[:, k, :], onT[:, k, :], start=(k == 0), stop=(k == 1),
                          after=[m_2T] + R("b7"), count=k == 1)
            slot("onT").read(m, m_lo)
            m = act.op(S.copy, lgT[:], ps[0:NE, SHARED, 0:T], after=[m] + R("lgT"))
            slot("b7").read(m)
            yield
            for t in range(TT):
                m2_ = pe.op(nc.tensor.transpose, bank[:, t * NE:(t + 1) * NE], lgT[:, t * P:(t + 1) * P],
                            env.ident[0:NE, 0:NE], split=True, after=[m] + R("b7"), count=t == 1)
            slot("lgT").read(m2_)
            m = dve.op(V.tensor_copy, lg[:], bank[:, 0:TT * NE].rearrange("p (t n) -> p t n", t=TT), after=[m2_] + R("lg"))
            slot("b7").read(m)
            for t in range(TT):
                dve.op(V.max, top[:, t, :], lg[:, t, :], after=R("top"), split=True)
                dve.op(V.max_index, ti[:, t, :], top[:, t, :], lg[:, t, :], split=True)
            dve.op(V.tensor_copy, tif[:], ti[:])
            m = dve.op(V.tensor_tensor, wsel[:, :, 1:2], top[:, :, 1:2], top[:, :, 0:1], ALU.subtract)
            m = act.op(S.activation, wsel[:, :, 1:2], wsel[:, :, 1:2], ACT.Exp, after=[m])
            yield
            m = dve.op(V.tensor_scalar, wsel[:, :, 0:1], wsel[:, :, 1:2], 1.0, None, ALU.add, after=[m])
            dve.op(V.reciprocal, wsel[:, :, 0:1], wsel[:, :, 0:1])
            dve.op(V.tensor_tensor, wsel[:, :, 1:2], wsel[:, :, 1:2], wsel[:, :, 0:1], ALU.mult)
            for t in range(TT):
                w_ = env.wte[:, bass.ds(b * TT + t, 1), :].rearrange("p a b -> p (a b)")
                for k in range(2):
                    m = dve.op(V.tensor_scalar, tmp[:, k, :] if k else w_, env.expert_no[:], tif[:, t, k:k + 1],
                               wsel[:, t, k:k + 1], ALU.is_equal, ALU.mult)
                m = dve.op(V.tensor_tensor, w_, w_, tmp[:, 1, :], ALU.add)
            yield

        pipeline(pg, "cross", [keys, attend, output], B, before={1: lambda: load_expert(pg, a, env, 0, 0)})
        pg.meet()


PARTS = ((0, 0), (0, 1), (1, 0))


def split(pg, hi, lo, whole, after, free):
    m = pg.act.op(pg.nc.scalar.copy, hi, whole, after=after + free, alone=True)
    return pg.pool.op(pg.nc.gpsimd.tensor_tensor, lo, whole, hi, ALU.subtract, after=[m] + free)


def place_expert_weights(env, sb, i):
    env.raw[i] = sb(f"w_raw{i}", [P, 2, KT, FF])
    env.rawd[i] = sb(f"wd_raw{i}", [P, len(FT), D])
    env.w[i] = [sb(f"w{part}{i}", [P, 2, KT, FF], F32R) for part in ("hi", "lo")]
    env.wd[i] = [sb(f"wd{part}{i}", [P, len(FT), D], F32R) for part in ("hi", "lo")]


def load_expert_weights(pg, env, i, g, u, d):
    raw, rawd, w, wd = env.raw[i], env.rawd[i], env.w[i], env.wd[i]
    pg.dma(f"w{i}", raw[:, 0], g, after=env.raw_split[i].readers)
    m_gu = pg.dma(f"w{i}", raw[:, 1], u)
    nfull = 2 * P
    pg.dma(f"wd{i}", rawd[:, 0:2], d[0:nfull].rearrange("(k p) n -> p k n", p=P), after=env.rawd_split[i].readers)
    m_d = pg.dma(f"wd{i}", rawd[0:FF - nfull, 2], d[nfull:FF])
    m_w = split(pg, w[0][:].rearrange("p j k n -> p (j k n)"), w[1][:].rearrange("p j k n -> p (j k n)"),
                raw[:].rearrange("p j k n -> p (j k n)"), [m_gu], env.w_used[i].readers)
    env.raw_split[i].read(m_w)
    env.w_ready[i].read(m_w)
    split(pg, wd[0][:, 0:2], wd[1][:, 0:2], rawd[:, 0:2], [m_d], env.wd_used[i].readers)
    m_wd = split(pg, wd[0][0:FF - nfull, 2], wd[1][0:FF - nfull, 2], rawd[0:FF - nfull, 2], [m_d], env.wd_used[i].readers)
    env.rawd_split[i].read(m_wd)
    env.wd_ready[i].read(m_wd)


def load_expert(pg, a, env, i, e):
    s1 = bass.ds(e, 1)
    g, u = (a[n].rearrange("e (k p) n -> p e k n", p=P)[:, s1].rearrange("p e k n -> p (e k) n")
            for n in ("exp_gate", "exp_up"))
    load_expert_weights(pg, env, i, g, u, a["exp_down"][s1].rearrange("e f n -> (e f) n"))


def load_shared(pg, a, env, i):
    g, u = (a[n][i].rearrange("(k p) n -> p k n", p=P) for n in ("sh_gate", "sh_up"))
    load_expert_weights(pg, env, i, g, u, a["sh_down"][i])


def phase_experts(pg, a, env):
    nc, pe, act, dve, pool = pg.nc, pg.pe, pg.act, pg.dve, pg.pool
    V, S, G = nc.vector, nc.scalar, nc.gpsimd
    with ExitStack() as mem:
        def sb(n, shape, dt=F32):
            return mem.enter_context(nc.sbuf_tensor(n, shape, dt))
        ps = env.ps
        sg = [sb(f"sg{i}", [P, TG]) for i in range(2)]
        h = [sb(f"h{i}", [P, TG]) for i in range(2)]
        hT = [[sb(f"hT{part}{i}", [P, len(FT), TG], F32R) for part in ("hi", "lo")] for i in range(2)]
        acc = env.x2
        sl = {}

        def slot(n):
            if n not in sl:
                sl[n] = pg.slot("e_" + n)
            return sl[n]

        for n in range(8):
            slot(f"b{n}")
        for n in ("sg", "h", "hT"):
            for i in range(2):
                slot(f"{n}{i}")
        place_expert_weights(env, sb, 1)
        w, wd = env.w, env.wd

        def R(*names):
            return [m for n in names for m in slot(n).readers]

        bns, mvs = [sb(f"ebn{i}", [P, TT, 6]) for i in range(2)], [sb(f"emv{i}", [P, TT, 2]) for i in range(2)]
        finishing = []
        out = a["out"].rearrange("b (t p) d -> p (b t) d", p=P)

        def finish(tile):
            y = acc[:, tile:tile + TT, :]
            m = yield from norm_rows(pg, env, y, bns[tile // TT % 2], mvs[tile // TT % 2], [])
            pg.dma("out", out[:, tile:tile + TT, :], y, after=[m])

        def expert(i, weight, load_next=None, last=False):
            m_w, m_d = env.w_ready[i].readers, env.wd_ready[i].readers

            def up(tg, n):
                f0, fn = FT[n]
                par = n % 2
                for bank in (0, 1):
                    for k in range(KT):
                        for a_, b_ in PARTS:
                            m = pe.op(nc.tensor.matmul, ps[0:fn, 2 * par + bank, :], w[i][a_][:, bank, k, f0:f0 + fn],
                                      env.x2T[b_][:, k, tg * TG:(tg + 1) * TG], start=(k, a_, b_) == (0, 0, 0),
                                      stop=(k, a_) == (1, 1), after=m_w + R(f"b{2 * par + bank}"), count=(k, a_) == (1, 1))
                    if bank == 0:
                        m_s = act.op(S.activation, sg[par][0:fn, :], ps[0:fn, 2 * par, :], ACT.Silu, after=[m] + R(f"sg{par}"))
                        slot(f"b{2 * par}").read(m_s)
                m_h = dve.op(V.tensor_tensor, h[par][0:fn, :], sg[par][0:fn, :], ps[0:fn, 2 * par + 1, :], ALU.mult,
                             after=[m, m_s] + R(f"h{par}"))
                slot(f"b{2 * par + 1}").read(m_h)
                slot(f"sg{par}").read(m_h)
                m_h = split(pg, *(x_[0:fn, n, :] for x_ in hT[tg % 2]), h[par][0:fn, :], [m_h], R(f"hT{tg % 2}"))
                slot(f"h{par}").read(m_h)
                return m, m_h

            def down(tg, half, m_h):
                bank = 4 + 2 * (tg % 2) + half
                for t in range(2):
                    tile = half * 2 + t
                    for n, (f0, fn) in enumerate(FT):
                        for a_, b_ in PARTS:
                            m = pe.op(nc.tensor.matmul, ps[:, bank, t * D:(t + 1) * D],
                                      hT[tg % 2][a_][0:fn, n, tile * P:(tile + 1) * P], wd[i][b_][0:fn, n, :],
                                      start=(n, a_, b_) == (0, 0, 0), stop=(n, a_) == (2, 1),
                                      after=[m_h] + m_d + R(f"b{bank}"), count=(t, n, a_) == (1, 2, 1))
                for t in range(2):
                    tile = tg * (TG // P) + half * 2 + t
                    src, dst = ps[:, bank, t * D:(t + 1) * D], acc[:, tile, :]
                    if weight is None:
                        m2 = dve.op(V.tensor_tensor, dst, src, dst, ALU.add, after=[m])
                    else:
                        m2 = dve.op(V.scalar_tensor_tensor, out=dst, in0=src, scalar=weight(tile), in1=dst, op0=ALU.mult,
                                    op1=ALU.add, after=[m])
                slot(f"b{bank}").read(m2)
                if last:
                    finishing.append(finish(tg * (TG // P) + half * 2))
                    next(finishing[-1])
                    for g_ in finishing[:-1]:
                        next(g_, STOP)
                    del finishing[:-1]
                return m

            NG = NTOK // TG
            marks = {}
            for tg in range(NG + 1):
                for n in range(len(FT)):
                    if tg < NG:
                        m_up, marks[tg] = up(tg, n)
                    if tg > 0 and n > 0:
                        m_dn = down(tg - 1, n - 1, marks[tg - 1])
                if tg == 0 and load_next:
                    load_next()
                if tg > 0:
                    slot(f"hT{(tg - 1) % 2}").read(m_dn)
                if tg == NG - 1:
                    env.w_used[i].read(m_up)
            env.wd_used[i].read(m_dn)

        wcol = [sb(f"wcol{i}", [P, NTOK // P]) for i in range(2)]
        for i in range(2):
            slot(f"wcol{i}")

        def routed_expert(i, e, load_next):
            dve.op(V.tensor_copy, wcol[i][:], env.wte[:, :, bass.ds(e, 1)].rearrange("p t e -> p (t e)"))
            expert(i, lambda tile: wcol[i][:, tile:tile + 1], load_next)

        with pg.repeat("experts", NE // 2 - 1) as it:
            routed_expert(0, it * 2, lambda: load_expert(pg, a, env, 1, it * 2 + 1))
            routed_expert(1, it * 2 + 1, lambda: load_expert(pg, a, env, 0, it * 2 + 2))
        routed_expert(0, NE - 2, lambda: load_expert(pg, a, env, 1, NE - 1))
        routed_expert(1, NE - 1, lambda: load_shared(pg, a, env, 0))
        expert(0, None, lambda: load_shared(pg, a, env, 1))
        expert(1, None, last=True)
        next(finishing[0], STOP)
        pg.meet()


def decoder_program(nc, a, plan):
    with ExitStack() as ctx:
        pg = Program(nc, ctx, plan)

        class Env:
            pass

        env = Env()
        env.sb = lambda n, shape, dt=F32: ctx.enter_context(nc.sbuf_tensor(n, shape, dt))
        env.ps = ctx.enter_context(nc.psum_tensor("ps", [P, 8, 512], F32))
        env.tok_dram = nc.dram_tensor("tok_dram", [B, P, TT * 3 * D], F32).ap()
        env.a_dram = nc.dram_tensor("a_dram", [P, B, NP * CH], F32).ap()
        env.t_dram = nc.dram_tensor("t_dram", [2, P, B * NP, CH], F32).ap()
        env.fir_dram = nc.dram_tensor("fir_dram", [NF, D // CH, NTOK, CH], F32).ap()
        env.w1s_dram = nc.dram_tensor("w1s_dram", [NS * NPATH * H, HF], F32).ap()
        env.x1_dram = nc.dram_tensor("x1_dram", [B, T, D], F32).ap()
        env.beta = env.sb("beta", [P, B, NP])
        env.wpad = env.sb("wpad", [P, KT, NF, 2 * P])
        make_constants(pg, a, env)
        phase_project(pg, a, env)
        phase_invert_and_fir(pg, a, env)
        place_cross_parameters(env)
        phase_delta_and_gate(pg, a, env)
        env.x2 = env.sb("x2", [P, NTOK // P, D])
        env.x2T = [env.sb(f"x2T{part}", [P, KT, NTOK], F32R) for part in ("hi", "lo")]
        env.wte = env.sb("wte", [P, NTOK // P, NE])
        env.raw, env.rawd, env.w, env.wd = [None] * 2, [None] * 2, [None] * 2, [None] * 2
        place_expert_weights(env, env.sb, 0)
        env.raw_split, env.rawd_split, env.w_ready, env.wd_ready, env.w_used, env.wd_used = (
            [pg.slot(f"e_{n}{i}") for i in range(2)] for n in ("raw_split", "rawd_split", "w_ready", "wd_ready", "w_used", "wd_used"))
        phase_cross(pg, a, env)
        phase_experts(pg, a, env)
        return pg.new_plan


_NAMES = {"x": "x", "ctx": "ctx_1024"}
_NAMES |= {n: "L0_attn_" + n for n in ("Wq", "Wk", "Wv", "conv_q", "conv_k", "conv_v", "Wb", "gW1", "gb1", "gW2", "gb2",
                                       "log_tau", "eps_logit", "norm_w", "Wo")}
_NAMES |= {f"fir{i}": "L0_attn_fir_" + n for i, n in enumerate("sml")}
_NAMES |= {n: "L0_xattn_" + n for n in ("q_w", "q_b", "k_w", "k_b", "v_w", "v_b", "o_w", "o_b")}
_NAMES |= {n: "L0_ffn_" + n for n in ("gate_w", "exp_gate", "exp_up", "exp_down", "sh_gate", "sh_up", "sh_down")}


def kernel(**inputs):
    import numpy as np
    import concourse.bacc as bacc
    from concourse.bass_utils import run_bass_kernel_spmd

    arrays = {"in_" + n: np.ascontiguousarray(inputs[full]) for n, full in _NAMES.items()}

    def build(plan):
        nc = bacc.Bacc("TRN2", target_bir_lowering=False, num_devices=1)
        a = {n: nc.dram_tensor("in_" + n, arrays["in_" + n].shape, mybir.dt.from_np(arrays["in_" + n].dtype),
                               kind="ExternalInput").ap() for n in _NAMES}
        a["out"] = nc.dram_tensor("out", (B, T, D), F32, kind="ExternalOutput").ap()
        return nc, decoder_program(nc, a, plan)

    _, plan = build({})
    nc, again = build(plan)
    assert plan == again
    r = run_bass_kernel_spmd(nc, [arrays], core_ids=[0])
    return r.results[0]["out"]
```
